# Optimizing a Trainium2 kernel written in Bass

```python
import numpy as np
import jax
import jax.numpy as jnp

def _softmax(x, axis=-1):
    return jax.nn.softmax(x, axis=axis)

def _gelu(x):
    return jax.nn.gelu(x, approximate=True)

def _silu(x):
    return jax.nn.silu(x)

def _sigmoid(x):
    return jax.nn.sigmoid(x)

def _layernorm(x, axis=-1, eps=1e-05):
    m = jnp.mean(x, axis=axis, keepdims=True)
    v = jnp.var(x, axis=axis, keepdims=True)
    return (x - m) / jnp.sqrt(v + eps)

def _scatter_add(tgt, idx, src, axis=0):
    return tgt.at[idx].add(src)

def _segment_sum(src, seg, n):
    return jax.ops.segment_sum(src, seg, n)
kernel_name = 'mk_adj_ffn_d1_adj_r2_ec32e1'

def setup_inputs(seed: int=0):
    np.random.seed(seed)
    _w = jnp.asarray

    def _rec_inputs():
        import jax
        import jax.numpy as jnp
        _gk = jax.random.key(seed)
        x = -0.0005207 + 1.001 * jax.random.normal(jax.random.fold_in(_gk, 1), (2048, 256), jnp.float32)
        _w = (1.0 + jnp.arange(2048, dtype=jnp.float32)) ** (-0.5)
        _w = _w / _w.mean()
        _pij = jnp.clip(0.00195312 * _w[:, None] * _w[None, :], 0.0, 1.0)
        _a = jax.random.uniform(jax.random.fold_in(_gk, 2), (2048, 2048)) < _pij
        _af = _a.astype(jnp.float32)
        adj = _af
        return (x, adj)
    x, adj = _rec_inputs()

    def _L0_gnn_setup():
        import jax, jax.numpy as jnp
        import numpy as np
        N = 2048
        INPUT_DIM = 256
        KEY_DIM = 64
        OUT_DIM = 256
        N_HEADS = 8

        def _xavier_normal(key, shape, gain):
            fan_in, fan_out = (shape[-2], shape[-1])
            std = gain * (2.0 / (fan_in + fan_out)) ** 0.5
            return jax.random.normal(key, shape, dtype=jnp.float32) * std
        key = jax.random.key(seed)
        kx, ka, kk, kq, kv, ko = jax.random.split(key, 6)
        gain = 2.0 ** 0.5
        node_matrix = jax.random.normal(kx, (N, INPUT_DIM), dtype=jnp.float32)
        adjacency_matrix = jax.random.randint(ka, (N, N), 0, 2).astype(jnp.float32)
        Wks = _xavier_normal(kk, (N_HEADS, INPUT_DIM, KEY_DIM), gain)
        Wqs = _xavier_normal(kq, (N_HEADS, INPUT_DIM, KEY_DIM), gain)
        Wvs = _xavier_normal(kv, (N_HEADS, INPUT_DIM, KEY_DIM), gain)
        Wo = _xavier_normal(ko, (N_HEADS, KEY_DIM, OUT_DIM), gain)
        return {'node_matrix': node_matrix, 'adjacency_matrix': adjacency_matrix, 'Wks': Wks, 'Wqs': Wqs, 'Wvs': Wvs, 'Wo': Wo}
    _L0_gnn_all = _L0_gnn_setup()
    _L0_gnn_in = {k: v for k, v in _L0_gnn_all.items() if k in ('Wks', 'Wqs', 'Wvs', 'Wo')}
    del _L0_gnn_all

    def _L0_ffn_setup():
        import jax, jax.numpy as jnp
        import numpy as np
        B, S, D, H, E = (4, 1024, 256, 8, 8)
        FF = 4 * D
        HD = D // H
        EPS = 1e-05

        def _layernorm(x, g, b):
            mu = jnp.mean(x, axis=-1, keepdims=True)
            var = jnp.mean((x - mu) ** 2, axis=-1, keepdims=True)
            return (x - mu) * jax.lax.rsqrt(var + EPS) * g + b
        key = jax.random.key(seed)
        ks = jax.random.split(key, 16)
        s = 0.02
        return {'x': jax.random.normal(ks[0], (B, S, D), dtype=jnp.float32), 'ln1_g': jnp.ones((D,), jnp.float32), 'ln1_b': jnp.zeros((D,), jnp.float32), 'Wq': jax.random.normal(ks[1], (D, D), jnp.float32) * s, 'bq': jnp.zeros((D,), jnp.float32), 'Wk': jax.random.normal(ks[2], (D, D), jnp.float32) * s, 'bk': jnp.zeros((D,), jnp.float32), 'Wv': jax.random.normal(ks[3], (D, D), jnp.float32) * s, 'bv': jnp.zeros((D,), jnp.float32), 'Wo': jax.random.normal(ks[4], (D, D), jnp.float32) * s, 'bo': jnp.zeros((D,), jnp.float32), 'gate_W': jax.random.normal(ks[5], (D, E), jnp.float32) * s, 'gate_b': jnp.zeros((E,), jnp.float32), 'W1': jax.random.normal(ks[6], (E, D, FF), jnp.float32) * s, 'b1': jnp.zeros((E, FF), jnp.float32), 'W2': jax.random.normal(ks[7], (E, FF, D), jnp.float32) * s, 'b2': jnp.zeros((E, D), jnp.float32)}
    _L0_ffn_all = _L0_ffn_setup()
    _L0_ffn_in = {k: v for k, v in _L0_ffn_all.items() if k in ('ln1_g', 'ln1_b', 'Wq', 'bq', 'Wk', 'bk', 'Wv', 'bv', 'Wo', 'bo', 'gate_W', 'gate_b', 'W1', 'b1', 'W2', 'b2')}
    del _L0_ffn_all
    return {'x': x, 'adj': adj, 'L0_gnn_Wks': _L0_gnn_in['Wks'], 'L0_gnn_Wqs': _L0_gnn_in['Wqs'], 'L0_gnn_Wvs': _L0_gnn_in['Wvs'], 'L0_gnn_Wo': _L0_gnn_in['Wo'], 'L0_ffn_ln1_g': _L0_ffn_in['ln1_g'], 'L0_ffn_ln1_b': _L0_ffn_in['ln1_b'], 'L0_ffn_Wq': _L0_ffn_in['Wq'], 'L0_ffn_bq': _L0_ffn_in['bq'], 'L0_ffn_Wk': _L0_ffn_in['Wk'], 'L0_ffn_bk': _L0_ffn_in['bk'], 'L0_ffn_Wv': _L0_ffn_in['Wv'], 'L0_ffn_bv': _L0_ffn_in['bv'], 'L0_ffn_Wo': _L0_ffn_in['Wo'], 'L0_ffn_bo': _L0_ffn_in['bo'], 'L0_ffn_gate_W': _L0_ffn_in['gate_W'], 'L0_ffn_gate_b': _L0_ffn_in['gate_b'], 'L0_ffn_W1': _L0_ffn_in['W1'], 'L0_ffn_b1': _L0_ffn_in['b1'], 'L0_ffn_W2': _L0_ffn_in['W2'], 'L0_ffn_b2': _L0_ffn_in['b2']}

def reference(x, adj, L0_gnn_Wks, L0_gnn_Wqs, L0_gnn_Wvs, L0_gnn_Wo, L0_ffn_ln1_g, L0_ffn_ln1_b, L0_ffn_Wq, L0_ffn_bq, L0_ffn_Wk, L0_ffn_bk, L0_ffn_Wv, L0_ffn_bv, L0_ffn_Wo, L0_ffn_bo, L0_ffn_gate_W, L0_ffn_gate_b, L0_ffn_W1, L0_ffn_b1, L0_ffn_W2, L0_ffn_b2):
    import jax
    import jax.numpy as jnp

    def _L0_gnn_ref(node_matrix, adjacency_matrix, Wks, Wqs, Wvs, Wo):
        import jax, jax.numpy as jnp
        import numpy as np
        N = 2048
        INPUT_DIM = 256
        KEY_DIM = 64
        OUT_DIM = 256
        N_HEADS = 8

        def _xavier_normal(key, shape, gain):
            fan_in, fan_out = (shape[-2], shape[-1])
            std = gain * (2.0 / (fan_in + fan_out)) ** 0.5
            return jax.random.normal(key, shape, dtype=jnp.float32) * std
        n = adjacency_matrix.shape[0]
        adj = jnp.maximum(adjacency_matrix, jnp.eye(n, dtype=adjacency_matrix.dtype))
        keys = jnp.einsum('nj,hjk->hnk', node_matrix, Wks)
        queries = jnp.einsum('nj,hjk->hnk', node_matrix, Wqs)
        values = jnp.einsum('nj,hjk->hnk', node_matrix, Wvs)
        key_dim = Wks.shape[-1]
        atts = jnp.einsum('hqk,hmk->hqm', queries, keys) / key_dim ** 0.5
        atts = atts - 1e+16 * (1.0 - adj)[None, :, :]
        atts = jax.nn.softmax(atts, axis=-1)
        return jnp.einsum('hqm,hmk,hko->qo', atts, values, Wo)

    def _L0_ffn_ref(x, ln1_g, ln1_b, Wq, bq, Wk, bk, Wv, bv, Wo, bo, gate_W, gate_b, W1, b1, W2, b2):
        import jax, jax.numpy as jnp
        import numpy as np
        B, S, D, H, E = (4, 1024, 256, 8, 8)
        FF = 4 * D
        HD = D // H
        EPS = 1e-05

        def _layernorm(x, g, b):
            mu = jnp.mean(x, axis=-1, keepdims=True)
            var = jnp.mean((x - mu) ** 2, axis=-1, keepdims=True)
            return (x - mu) * jax.lax.rsqrt(var + EPS) * g + b
        b, s, d = x.shape
        q = (x @ Wq + bq).reshape(b, s, H, HD)
        k = (x @ Wk + bk).reshape(b, s, H, HD)
        v = (x @ Wv + bv).reshape(b, s, H, HD)
        scores = jnp.einsum('bqhd,bkhd->bhqk', q, k) / jnp.sqrt(jnp.float32(HD))
        attn = jax.nn.softmax(scores, axis=-1)
        o = jnp.einsum('bhqk,bkhd->bqhd', attn, v).reshape(b, s, d) @ Wo + bo
        h = _layernorm(x + o, ln1_g, ln1_b)
        t = h.reshape(b * s, d)
        probs = jax.nn.softmax(t @ gate_W + gate_b, axis=-1)
        idx = jnp.argmax(probs, axis=-1)
        gw = jnp.max(probs, axis=-1)
        hid = jax.nn.gelu(jnp.einsum('nd,edf->enf', t, W1) + b1[:, None, :])
        out_all = jnp.einsum('enf,efd->end', hid, W2) + b2[:, None, :]
        onehot = jax.nn.one_hot(idx, E, dtype=t.dtype)
        out = jnp.einsum('ne,end->nd', onehot, out_all)
        out = out * gw[:, None]
        return out.reshape(b, s, d)
    x = x + _L0_gnn_ref(_layernorm(x, axis=-1), adj, L0_gnn_Wks, L0_gnn_Wqs, L0_gnn_Wvs, L0_gnn_Wo)
    x = x + _L0_ffn_ref(_layernorm(x, axis=-1)[None], L0_ffn_ln1_g, L0_ffn_ln1_b, L0_ffn_Wq, L0_ffn_bq, L0_ffn_Wk, L0_ffn_bk, L0_ffn_Wv, L0_ffn_bv, L0_ffn_Wo, L0_ffn_bo, L0_ffn_gate_W, L0_ffn_gate_b, L0_ffn_W1, L0_ffn_b1, L0_ffn_W2, L0_ffn_b2)[0]
    return x

_drawn_inputs = setup_inputs


def setup_inputs(seed=0):
    import zlib

    import numpy as np

    out = dict(_drawn_inputs(seed))
    spreads = {'L0_ffn_ln1_g': (1.0, 0.6),
     'L0_ffn_ln1_b': (0.0, 0.8),
     'L0_ffn_bq': (0.0, 0.8),
     'L0_ffn_bk': (0.0, 0.8),
     'L0_ffn_bv': (0.0, 0.8),
     'L0_ffn_bo': (0.0, 0.8),
     'L0_ffn_gate_b': (0.0, 0.8),
     'L0_ffn_b1': (0.0, 0.8),
     'L0_ffn_b2': (0.0, 0.8)}
    factors = {'L0_ffn_Wq': 8.0,
     'L0_ffn_Wk': 8.0,
     'L0_ffn_Wv': 8.0,
     'L0_ffn_Wo': 8.0,
     'L0_ffn_gate_W': 7.463,
     'L0_ffn_W1': 8.0,
     'L0_ffn_W2': 8.0}
    for name, (base, spread) in spreads.items():
        noise = np.random.default_rng([zlib.crc32(name.encode()), seed]).standard_normal(out[name].shape)
        drawn = base * np.exp(spread * noise) if base else spread * noise
        out[name] = jnp.asarray(drawn.astype(out[name].dtype))
    for name, factor in factors.items():
        out[name] = (out[name] * factor).astype(out[name].dtype)
    return out
```

```python
from contextlib import ExitStack

import concourse.bass as bass
from concourse import mybir

F32 = mybir.dt.float32
F16 = mybir.dt.float16
BF16 = mybir.dt.bfloat16
F8 = mybir.dt.float8e5
I32 = mybir.dt.int32
U32 = mybir.dt.uint32
ALU = mybir.AluOpType
ACT = mybir.ActivationFunctionType
AX = mybir.AxisListType


class Names:
    pass


P = 128
N = 2048
D = 256
T = N // P
KC = D // P
HEADS = 8
EXPERTS = 8
FF = 4 * D
FC = FF // P
EPS = 1e-5
BLOCK = 512
NB = N // BLOCK
SLOTS = (N - EXPERTS) // P + EXPERTS
MASKED = 8e16

QP = 2
GQ = N // QP
UNITS = QP * T
RING = 4
SCORE_SLOTS = 2
PAIRS = HEADS // 2
TOP_STEP = 28


def max_units(step):
    if step <= 14:
        return range(3 * step, 3 * step + 3)
    if 17 <= step <= 26:
        return range(45 + 2 * (step - 17), min(45 + 2 * (step - 17) + 2, T * NB))
    return range(0)


TILE_PAIRS = (SLOTS - 1) // 2
SUM_TILES = T - 2
SUMS = SUM_TILES - 1

KB = 1024

ROUTE_EXP, ROUTE_ONE_HOT, ROUTE_ROWS, ROUTE_DONE = 2, 6, 35, 39


def fused_graph_ffn(nc, x, adj, gW, fW, out):
    ctx = ExitStack()
    with ctx:
        def sb(name, shape, dt):
            return ctx.enter_context(nc.sbuf_tensor(name, shape, dt))

        def sem(name):
            return ctx.enter_context(nc.semaphore(name))

        def dram(name, shape, dt):
            return nc.dram_tensor(name, shape, dt, kind="Internal").ap()

        arena = sb("arena", [P, 202 * KB // 4], F32)
        size = {F32: 4, I32: 4, U32: 4, F16: 2, BF16: 2, F8: 1}

        def at(kb, shape, dt):
            n = 1
            for s in shape[1:]:
                n *= s
            words = n * size[dt] // 4
            a = arena[0:shape[0], int(kb * KB) // 4:int(kb * KB) // 4 + words]
            if dt != F32:
                a = a.bitcast(dt)
            if len(shape) == 3:
                a = a.rearrange("p (a b) -> p a b", a=shape[1])
            if len(shape) == 4:
                a = a.rearrange("p (a b c) -> p a b c", a=shape[1], b=shape[2])
            return a

        xs = at(0, [P, T, D], F32)
        gwo = at(16, [P, 4, D], F32)
        bias_v, bias_o, ln_g, ln_b = (at(16 + i, [P, D], F32) for i in range(4))
        fwq, fwk, fwv, fwo = (at(20 + 2 * i, [P, KC, D], F32) for i in range(4))
        mask_rows = at(28, [P, T, N], BF16)
        mask_cols = at(92, [P, T, N], F8)
        w1h = at(28, [P, EXPERTS * KC * FF], F16)
        w1l = at(60, [P, EXPERTS * KC * FF], F16)
        w2h = at(92, [P, EXPERTS * FC * D], F16)
        w2l = at(162, [P, EXPERTS * FC * D], F16)
        nT = at(124, [P, KC, N], F32)
        gwqkv = [at(140 + 4 * i, [P, KC, HEADS * 64], F32) for i in range(3)]
        adj_in = at(152, [P, 2, N], F32)
        hi_st = at(168, [P, 2, N], F16)
        lo_st = at(176, [P, 2, N], F16)
        v_st = at(184, [P, 2, BLOCK], F32)
        nx = at(188, [P, 4, D], F32)
        w_in = at(194, [P, 2, 1024], F32)
        f_oT = at(124, [P, 2, N], F32)
        ts = at(140, [P, T, D], F32)
        zero_tile = at(201, [P, D], F32)
        xn = at(156, [P, 2, D], F32)
        tT = at(158, [P, 2, KC, P], F32)
        logits, choice, one_hot, rank = (at(160 + i / 2, [P, T, EXPERTS], F32) for i in range(4))
        totals, run0, run1, place = (at(20 + i / 2, [P, T, EXPERTS], F32) for i in range(4))
        slot_of = at(22, [P, SLOTS, EXPERTS], F32)
        b2_rows = at(24, [EXPERTS, D], F32)
        b1_rows = at(25, [EXPERTS * FC, P], F32)
        gate_w = at(25.5, [P, KC, EXPERTS], F32)
        gate_b = at(25.625, [P, EXPERTS], F32)
        sorted_in = at(124, [P, 2, D], F32)
        sTh = at(126, [P, 2, KC, P], F16)
        sTl = at(127, [P, 2, KC, P], F16)
        hid = at(128, [P, 2, FC, P], F32)
        hid_h = at(136, [P, 2, FC, P], F16)
        hid_l = at(140, [P, 2, FC, P], F16)
        y_out = at(144, [P, 2, D], F32)
        y_in = at(146, [P, 4, D], F32)
        res = at(150, [P, 4, D], F32)
        one_hot_T = at(154, [EXPERTS, T, P], F32)

        small = sb("small", [P, 128], F32)
        ident = sb("ident", [P, P], F32)
        identb = sb("identb", [P, P], BF16)
        identt = sb("identt", [P, P], BF16)
        ones = sb("ones", [P, P], F32)
        ps = ctx.enter_context(nc.psum_tensor("ps", [P, 8, BLOCK], F32))

        sorted_d = dram("sorted_tokens", [SLOTS * P, D], F32)
        y_d = dram("expert_out", [SLOTS * P, D], F32)

        def scratch(name, width):
            d = Names()
            d.qh, d.ql, d.kh, d.kl = (dram(f"{name}_{part}", [width, N], F16) for part in ("qh", "ql", "kh", "kl"))
            d.v = dram(name + "_v", [P, T, width], F32)
            d.o = dram(name + "_o", [width, N], F32)
            return d

        def attention_sems(name):
            s = Names()
            s.ln = sem(name + "_ln")
            s.sqrt = sem(name + "_sqrt")
            s.nx = sem(name + "_nx")
            s.hi = sem(name + "_hi")
            s.qk_stored = [sem(name + f"_qk_stored{i}") for i in range(2)]
            s.v_stored = [sem(name + f"_v_stored{i}") for i in range(2)]
            s.loaded = [sem(name + f"_loaded{i}") for i in range(2)]
            s.ones_row = sem(name + "_ones_row")
            s.scores = sem(name + "_scores")
            s.exp = sem(name + "_exp")
            s.pv = sem(name + "_pv")
            s.summed = sem(name + "_summed")
            s.evac = sem(name + "_evac")
            s.evac_step = sem(name + "_evac_step")
            s.job = sem(name + "_job")
            s.drained = sem(name + "_drained")
            s.top = sem(name + "_top")
            s.row_in = sem(name + "_row_in")
            s.o_stored = [sem(name + f"_o_stored{i}") for i in range(2)]
            s.o_in = sem(name + "_o_in")
            s.proj = sem(name + "_proj")
            s.proj_used = sem(name + "_proj_used")
            return s

        amax = sb("amax", [P, T, NB], F32)
        top = sb("top", [P, T], F32)
        neg_top = sb("neg_top", [T, P], F16)

        G = Names()
        G.masked, G.dim, G.chunks, G.scale, G.max_rows = True, 64, 4, 64 ** -0.5, P
        G.jobs, G.top_job = T * NB + 1 + QP, T * NB + 1
        G.d, G.s = scratch("gnn", 512), attention_sems("gnn")
        G.ka = [at(124 + 16 * i, [P, N], F16) for i in range(2)]
        G.kb = [at(128 + 16 * i, [65, N], F16) for i in range(2)]
        G.qa = [at(132 + 16 * i, [P, N], F16) for i in range(2)]
        G.qb = [at(136 + 16 * i, [65, N], F16) for i in range(2)]
        G.v = [at(156 + 4 * i, [P, T, 64], F32) for i in range(2)]
        G.p = at(164, [P, RING, GQ], F32)
        G.sum = at(180, [P, 2, GQ], F32)
        G.r = at(188, [P, BLOCK], F32)
        G.o = at(190, [P, 2, BLOCK], F32)
        G.junk = at(194, [P, 2, BLOCK], BF16)
        G.row = [G.qb[i][64:65, :] for i in range(2)]
        G.ones_row = [G.kb[i][64:65, :] for i in range(2)]
        G.oT = at(124, [P, 4, N], F32)
        G.loads = 7
        G.wq, G.wk, G.wv = gwqkv
        F = Names()
        F.masked, F.dim, F.chunks, F.scale, F.max_rows = False, 32, 2, 32 ** -0.5, 96
        F.jobs, F.top_job = T * NB + 1, T * NB
        F.d, F.s = scratch("ffn", 256), attention_sems("ffn")
        F.ka = [at(124 + 8 * i, [97, N], F16) for i in range(2)]
        F.qa = [at(128 + 8 * i, [97, N], F16) for i in range(2)]
        F.v = [at(140 + 2 * i, [P, T, 32], F32) for i in range(2)]
        F.p = at(144, [P, RING, GQ], F32)
        F.r = at(160, [P, BLOCK], F32)
        F.o = at(20, [P, 2, BLOCK], F32)
        F.row = [F.qa[i][96:97, :] for i in range(2)]
        F.ones_row = [F.ka[i][96:97, :] for i in range(2)]
        F.oT = f_oT
        F.loads = 7
        F.wq, F.wk, F.wv = fwq, fwk, fwv
        bq_cols = sb("bq_cols", [P, 2], F32)
        bk_cols = sb("bk_cols", [P, 2], F32)

        b1_cols = sb("b1_cols", [P, EXPERTS * FC], F32)
        b1_tile = sb("b1_tile", [P, 2, FC], F32)
        before = sb("before", [P, P], F32)
        e_iota = sb("e_iota", [P, EXPERTS], F32)
        slot_iota = sb("slot_iota", [P, SLOTS], F32)
        counts = sb("counts", [P, 3, EXPERTS], F32)
        counts_i = sb("counts_i", [P, EXPERTS], I32)
        gate = sb("gate", [P, T], F32)
        slot_row = sb("slot_row", [P, T], I32)
        slot_expert = sb("slot_expert", [P, SLOTS], I32)
        slot_expert_f = sb("slot_expert_f", [P, SLOTS], F32)
        mv2 = sb("mv2", [P, T, 2], F32)
        stats = sb("stats", [P, T, 6], F32)
        mv = sb("mv", [P, T, 2], F32)
        veps = small[:, 0:16]
        std = small[:, 16:32]
        rstd = small[:, 32:48]
        tmp = small[:, 48:64]

        s_x = [sem(f"x_in{i}") for i in range(2)]
        s_w = sem("gnn_weights_in")
        s_fw = sem("ffn_weights_in")
        s_adj = [sem(f"adj_in{i}") for i in range(2)]
        s_adj_diag = sem("adj_diag")
        s_mask = sem("mask_rows_raw")
        s_mask_scaled = sem("mask_rows_scaled")
        s_const = sem("constants")
        s_const2 = sem("constants_derived")
        s_mmA = sem("bank_for_scalar_full")
        s_evA = sem("bank_for_scalar_free")
        s_mmD = sem("bank_for_vector_full")
        s_evD = sem("bank_for_vector_free")
        s_moe_w = sem("moe_vectors_in")
        s_moe_const = sem("moe_constants")
        s_zero = sem("sorted_zeroed")
        s_w_in = [sem(f"expert_weights_in{i}") for i in range(2)]
        s_w_split = sem("expert_weights_split")
        s_hsum = sem("attention_residual")
        s_ln2 = sem("second_norm")
        s_sqrt2 = sem("second_norm_root")
        s_h = sem("hidden_tile")
        s_hT = sem("hidden_turned")
        s_tT = sem("hidden_turned_out")
        s_lg = sem("logits_full")
        s_lg_out = sem("logits_out")
        s_route = sem("routing")
        s_route_exp = sem("routing_exp")
        s_prefix = sem("prefix_counts")
        s_one_hot = sem("one_hot")
        s_turn8 = sem("one_hot_turned")
        s_turn8_out = sem("one_hot_turned_out")
        s_b1 = sem("b1_turned")
        s_b1_out = sem("b1_turned_out")
        s_zero_in = sem("zero_tile")
        s_placed = sem("tokens_placed")
        s_sorted_in = [sem(f"sorted_in{i}") for i in range(2)]
        s_sT = sem("sorted_turned")
        s_sT_out = sem("sorted_split")
        s_up = sem("up_products")
        s_gelu = sem("gelu")
        s_b1_tile = sem("b1_of_tile")
        s_hid = sem("hidden_split")
        s_down = sem("down_products")
        s_y = sem("expert_tile_out")
        s_y_stored = [sem(f"expert_tile_stored{i}") for i in range(2)]
        s_y_in = [sem(f"token_rows_in{i}") for i in range(4)]
        s_b2 = sem("b2_selected")
        s_sum = sem("expert_sum")
        s_res = sem("result_tile")
        s_out = [sem(f"result_stored{i}") for i in range(4)]

        block = ctx.enter_context(nc.Block())

        XT = T // 2
        A_GNN = XT + 2 * T
        A_ALL = A_GNN + XT
        D_QK = 2 * 4 * NB
        D_GNN = D_QK + T
        FD_QK = 2 * 2 * NB

        @block.sync
        def _(sp):
            for i in range(2):
                sp.dma_start(xs[:, 8 * i:8 * i + 8, :],
                             x[1024 * i:1024 * i + 1024, :].rearrange("(t p) d -> p t d", p=P)).then_inc(s_x[i], 16)
            for w, a in zip(gwqkv, (gW["Wqs"], gW["Wks"], gW["Wvs"])):
                for c in range(KC):
                    sp.dma_start(w[:, c, :].rearrange("p (h k) -> p h k", h=HEADS),
                                 a[:, c * P:(c + 1) * P, :].rearrange("h p k -> p h k")).then_inc(s_w, 16)
            sp.dma_start(gwo, gW["Wo"].rearrange("h k o -> (h k) o").rearrange("(c p) o -> p c o", p=P)).then_inc(s_w, 16)
            for t in range(T):
                if t >= 2:
                    sp.wait_ge(s_mask, t - 1)
                sp.dma_start(adj_in[:, t % 2, :], adj[t * P:(t + 1) * P, :]).then_inc(s_adj[t % 2], 16)
            for w, a in zip((fwq, fwk, fwv, fwo), (fW["Wq"], fW["Wk"], fW["Wv"], fW["Wo"])):
                sp.dma_start(w, a.rearrange("(c p) n -> p c n", p=P)).then_inc(s_fw, 16)
            sp.dma_start(bq_cols[:, :], fW["bq"].rearrange("(c p) -> p c", p=P), allow_slow_non_contiguous=True).then_inc(s_fw, 16)
            sp.dma_start(bk_cols[:, :], fW["bk"].rearrange("(c p) -> p c", p=P), allow_slow_non_contiguous=True).then_inc(s_fw, 16)

            def store_projections(A, d_base):
                n = 0
                for w in range(2):
                    hi, lo = ((A.d.qh, A.d.ql), (A.d.kh, A.d.kl))[w]
                    for c in range(A.chunks):
                        sp.wait_ge(s_evD, d_base + NB * (n + 1))
                        rows = slice(c * P, (c + 1) * P)
                        sp.dma_start(hi[rows, :], hi_st[:, n % 2, :]).then_inc(A.s.qk_stored[n % 2], 16)
                        sp.dma_start(lo[rows, :], lo_st[:, n % 2, :]).then_inc(A.s.qk_stored[n % 2], 16)
                        n += 1
                width = A.chunks * P
                for t in range(T):
                    sp.wait_ge(s_evD, d_base + NB * n + t + 1)
                    sp.dma_start(A.d.v[:, t, :], v_st[:, t % 2, 0:width]).then_inc(A.s.v_stored[t % 2], 16)
                for i in range(2):
                    sp.wait_ge(A.s.qk_stored[i], 16 * 2 * n // 2)
                    sp.wait_ge(A.s.v_stored[i], 16 * T // 2)

            def load_head(A, h, p):
                d = A.dim
                kh, kl, qh, ql = (a[bass.ds(h * d, d), :] for a in (A.d.kh, A.d.kl, A.d.qh, A.d.ql))
                if A.masked:
                    pairs = [(A.ka[p][0:d, :], kh), (A.ka[p][d:2 * d, :], kl), (A.qa[p][0:d, :], qh),
                             (A.qa[p][d:2 * d, :], qh), (A.kb[p][0:d, :], kh), (A.qb[p][0:d, :], ql)]
                else:
                    pairs = [(A.ka[p][0:d, :], kh), (A.ka[p][d:2 * d, :], kl), (A.ka[p][2 * d:3 * d, :], kh),
                             (A.qa[p][0:d, :], qh), (A.qa[p][d:2 * d, :], qh), (A.qa[p][2 * d:3 * d, :], ql)]
                for dst, src in pairs:
                    sp.dma_start(dst, src).then_inc(A.s.loaded[p], 16)
                sp.dma_start(A.v[p], A.d.v[:, :, bass.ds(h * d, d)]).then_inc(A.s.loaded[p], 16)

            def store_group(A, i, p, qp):
                h = 2 * i + p
                sp.wait_ge(A.s.evac, i * 4 + (2 * p + qp + 3))
                for half in range(2):
                    rows = A.o[64 * half:64 * half + A.dim, qp, :]
                    col = qp * GQ + half * BLOCK
                    sp.dma_start(A.d.o[bass.ds(h * A.dim, A.dim), col:col + BLOCK], rows)\
                        .then_inc(A.s.o_stored[qp], 16)

            def attention(A):
                load_head(A, 0, 0)
                load_head(A, 1, 1)
                sp.wait_ge(A.s.drained, T * NB + 1)
                sp.dma_start(A.row[0].rearrange("a (t q) -> a t q", t=T), neg_top[:, :]).then_inc(A.s.row_in, 16)

                def heads(i, last):
                    for p in range(2):
                        store_group(A, i, p, 0)
                        if not (last and p == 1):
                            sp.wait_ge(A.s.drained, i * (2 * A.jobs) + (T * NB + 1 + p * A.jobs + A.top_job + 1))
                            sp.dma_start(A.row[1 - p].rearrange("a (t q) -> a t q", t=T), neg_top[:, :])\
                                .then_inc(A.s.row_in, 16)
                        store_group(A, i, p, 1)
                        if not last:
                            sp.wait_ge(A.s.pv, i * (2 * UNITS) + (RING + UNITS * (p + 1)))
                            load_head(A, 2 * i + (2 + p), p)

                with sp.Fori(0, PAIRS - 1) as i:
                    heads(i, False)
                heads(PAIRS - 1, True)
                for qp in range(2):
                    sp.wait_ge(A.s.o_stored[qp], 32 * (HEADS + 1))
                sp.dma_start(A.oT, A.d.o.rearrange("(c p) n -> p c n", p=P)).then_inc(A.s.o_in, 16)

            store_projections(G, 0)
            attention(G)
            sp.wait_ge(G.s.proj_used, T)
            for dst, src in ((bias_v, fW["bv"]), (bias_o, fW["bo"]), (ln_g, fW["ln1_g"]), (ln_b, fW["ln1_b"])):
                sp.dma_start(dst, src.partition_broadcast(P)).then_inc(s_fw, 16)
            store_projections(F, D_GNN)
            for dst, src in ((b2_rows, fW["b2"]), (b1_rows, fW["b1"].rearrange("e (c p) -> (e c) p", p=P)),
                             (gate_w, fW["gate_W"].rearrange("(c p) e -> p c e", p=P)),
                             (gate_b, fW["gate_b"].partition_broadcast(P))):
                sp.dma_start(dst, src).then_inc(s_moe_w, 16)
            attention(F)

            sp.wait_ge(s_placed, 16 * T)

            def load_sorted(j, p):
                sp.dma_start(sorted_in[:, p, :], sorted_d[bass.ds(j * P, P), :]).then_inc(s_sorted_in[p], 16)

            load_sorted(0, 0)
            load_sorted(1, 1)
            with sp.Fori(0, TILE_PAIRS - 1) as i:
                for p in range(2):
                    sp.wait_ge(s_sT, i * 2 + (p + 1))
                    load_sorted(2 * i + (2 + p), p)
            sp.wait_ge(s_sT, SLOTS - 2)
            load_sorted(SLOTS - 1, 0)
            for t in range(T):
                sp.wait_ge(s_res, t + 1)
                sp.dma_start(out[t * P:(t + 1) * P, :], res[:, t % 4, :]).then_inc(s_out[t % 4], 16)
            for i in range(4):
                sp.wait_ge(s_out[i], 4 * T)

        @block.gpsimd
        def _(pool):
            pool.memset(ident[:, :], 0.0).then_inc(s_const, 1)
            pool.memset(ones[:, :], 1.0).then_inc(s_const, 1)
            for s in (G.s, F.s):
                pool.sem_inc(s.exp, SCORE_SLOTS)
                pool.sem_inc(s.pv, RING)
                pool.sem_inc(s.summed, SUMS)
                pool.sem_inc(s.evac, 2)
                pool.sem_inc(s.o_stored[0], 32)
                pool.sem_inc(s.o_stored[1], 32)
            for s in s_y_stored:
                pool.sem_inc(s, 16)
            pool.sem_inc(s_hid, 4)
            pool.sem_inc(s_sT_out, 4)
            pool.sem_inc(s_up, 2)
            pool.sem_inc(s_gelu, 2)
            pool.sem_inc(s_down, 2)
            pool.sem_inc(s_y, 2)
            pool.memset(before[:, :], 1.0).then_inc(s_moe_const, 1)
            pool.memset(zero_tile, 0.0).then_inc(s_zero_in, 1)
            pool.iota(e_iota[:, :], [[-1, EXPERTS]], base=EXPERTS, channel_multiplier=0,
                      allow_small_or_imprecise_dtypes=True).then_inc(s_moe_const, 1)
            pool.iota(slot_iota[:, :], [[1, SLOTS]], base=0, channel_multiplier=0,
                      allow_small_or_imprecise_dtypes=True).then_inc(s_moe_const, 1)
            pool.wait_ge(s_moe_const, 3)
            pool.affine_select(out=before[:, :], in_=before[:, :], compare_op=ALU.is_gt, fill=0.0,
                               base=0, pattern=[[1, P]], channel_multiplier=-1).then_inc(s_moe_const, 1)
            pool.wait_ge(s_zero_in, 1)
            pool.dma_start(sorted_d.rearrange("(j p) d -> p j d", p=P),
                           zero_tile.unsqueeze(1).to_broadcast([P, SLOTS, D])).then_inc(s_zero, 16)
            pool.wait_ge(s_const, 1)
            pool.affine_select(out=ident[:, :], in_=ident[:, :], compare_op=ALU.not_equal, fill=1.0,
                               base=0, pattern=[[-1, P]], channel_multiplier=1).then_inc(s_const, 1)

            def ones_rows(A):
                for i in range(2):
                    pool.memset(A.ones_row[i], 1.0).then_inc(A.s.ones_row, 1)

            def add_probabilities(A):
                def heads(i):
                    for g in range(4):
                        for kt in range(1, SUM_TILES):
                            n = T * g + kt
                            if kt == 1:
                                pool.wait_ge(A.s.evac, i * 4 + (g + 1))
                            pool.wait_ge(A.s.exp, i * (4 * T) + (SCORE_SLOTS + n + 1))
                            total = A.sum[:, g % 2, :]
                            if kt == 1:
                                first = A.p[:, (n - 1) % RING, :]
                            else:
                                pool.wait_ge(A.s.summed, i * (4 * SUMS) + (SUMS * (g + 1) + kt - 1))
                                first = total
                            pool.tensor_tensor(total, first, A.p[:, n % RING, :], ALU.add).then_inc(A.s.summed, 1)
                with pool.Fori(0, PAIRS) as i:
                    heads(i)

            pool.wait_ge(s_evD, D_GNN)
            for i in range(2):
                pool.wait_ge(G.s.qk_stored[i], 16 * 8)
            ones_rows(G)
            add_probabilities(G)
            def split_weights(first, src, hi, lo, width):
                for c in range(2 * EXPERTS):
                    n = first + c
                    if n >= 2:
                        pool.wait_ge(s_w_split, 2 * (n - 1))
                    pool.dma_start(w_in[:, n % 2, :].rearrange("p (a b) -> p a b", b=width), src(c))\
                        .then_inc(s_w_in[n % 2], 16)
                    if c:
                        split(n - 1, hi, lo, c - 1)
                split(first + 2 * EXPERTS - 1, hi, lo, 2 * EXPERTS - 1)

            def split(n, hi, lo, c):
                cols = slice(c * 1024, (c + 1) * 1024)
                pool.wait_ge(s_w_in[n % 2], 16 * (n // 2 + 1))
                pool.tensor_copy(hi[:, cols], w_in[:, n % 2, :]).then_inc(s_w_split, 1)
                pool.wait_ge(s_w_split, 2 * n + 1)
                pool.tensor_tensor(lo[:, cols], w_in[:, n % 2, :], hi[:, cols], ALU.subtract)\
                    .then_inc(s_w_split, 1)

            pool.wait_ge(G.s.proj_used, T)
            pool.wait_ge(s_zero, 16)
            split_weights(0, lambda c: fW["W1"][c // 2, (c % 2) * P:(c % 2 + 1) * P, :].unsqueeze(1),
                          w1h, w1l, FF)
            pool.wait_ge(s_w_split, 4 * EXPERTS)
            pool.wait_ge(s_evD, D_GNN + FD_QK + T)
            for i in range(2):
                pool.wait_ge(F.s.qk_stored[i], 64)
                pool.wait_ge(F.s.v_stored[i], 8 * T)
            ones_rows(F)
            pool.wait_ge(F.s.ones_row, 2)
            split_weights(2 * EXPERTS,
                          lambda c: fW["W2"][c // 2, (c % 2) * 512:(c % 2 + 1) * 512, :].rearrange(
                              "(c p) d -> p c d", p=P),
                          w2h, w2l, D)
            pool.wait_ge(s_route, ROUTE_ROWS)
            for t in range(T):
                pool.indirect_dma_start(
                    out=sorted_d, out_offset=bass.IndirectOffsetOnAxis(ap=slot_row[:, t:t + 1].bitcast(U32), axis=0),
                    in_=ts[:, t, :], in_offset=None).then_inc(s_placed, 16)

            pool.wait_ge(s_y_stored[0], 16 * (TILE_PAIRS + 2))
            pool.wait_ge(s_y_stored[1], 16 * (TILE_PAIRS + 1))
            for t in range(T):
                if t >= 4:
                    pool.wait_ge(s_res, t - 3)
                pool.indirect_dma_start(
                    out=y_in[:, t % 4, :], out_offset=None, in_=y_d,
                    in_offset=bass.IndirectOffsetOnAxis(ap=slot_row[:, t:t + 1].bitcast(U32), axis=0))\
                    .then_inc(s_y_in[t % 4], 16)

        @block.scalar
        def _(act):
            def root(A):
                act.wait_ge(A.s.ln, 2 * T + 1)
                nc.scalar.activation(std, veps, ACT.Sqrt).then_inc(A.s.sqrt, 1)

            def transposed_input(base):
                for u in range(XT):
                    act.wait_ge(s_mmA, base + u + 1)
                    nc.scalar.activation(nT[:, :, u * 256:(u + 1) * 256],
                                         ps[:, (base + u) % 4, :].rearrange("p (k n) -> p k n", k=KC),
                                         ACT.Copy).then_inc(s_evA, 1)

            def high_halves(A, d_base, biased):
                for n in range(2 * A.chunks):
                    if n >= 2:
                        act.wait_ge(A.s.qk_stored[n % 2], 32 * (n // 2))
                    for b in range(NB):
                        j = d_base + NB * n + b
                        act.wait_ge(s_mmD, j + 1)
                        bank, dst = ps[:, 4 + j % 4, :], hi_st[:, n % 2, b * BLOCK:(b + 1) * BLOCK]
                        if biased:
                            col = (bq_cols, bk_cols)[n // A.chunks][:, n % A.chunks:n % A.chunks + 1]
                            nc.scalar.activation(dst, bank, ACT.Identity, bias=col).then_inc(A.s.hi, 1)
                        else:
                            nc.scalar.activation(dst, bank, ACT.Copy).then_inc(A.s.hi, 1)

            def exps(A):
                def heads(i):
                    for n in range(2 * UNITS):
                        act.wait_ge(A.s.scores, i * (2 * UNITS) + (n + 1))
                        act.wait_ge(A.s.pv, i * (2 * UNITS) + (n + 1))
                        if A.masked:
                            m = n - RING
                            got = SUMS * (m // T) + min(max(m % T, 1), SUMS)
                            act.wait_ge(A.s.summed, i * (4 * SUMS) + (SUMS + got))
                        slot = 2 * (n % SCORE_SLOTS)
                        nc.scalar.activation(A.p[:, n % RING, :].rearrange("p (a b) -> p a b", a=2),
                                             ps[:, slot:slot + 2, :], ACT.Exp, scale=A.scale).then_inc(A.s.exp, 1)
                with act.Fori(0, PAIRS) as i:
                    heads(i)

            root(G)
            transposed_input(0)
            for t in range(T):
                for half in range(2):
                    j = XT + 2 * t + half
                    act.wait_ge(s_mmA, j + 1)
                    nc.scalar.activation(mask_cols[:, 8 * half:8 * half + 8, t * P:(t + 1) * P],
                                         ps[:, j % 4, :].bitcast(BF16).rearrange("p (a b) -> p a b", a=8),
                                         ACT.Copy, saturate=False).then_inc(s_evA, 1)
            high_halves(G, 0, False)
            exps(G)
            root(F)
            transposed_input(A_GNN)
            act.wait_ge(s_fw, 16 * 10)
            high_halves(F, D_GNN, True)
            exps(F)

            act.wait_ge(s_ln2, 2 * T + 1)
            nc.scalar.activation(std, veps, ACT.Sqrt).then_inc(s_sqrt2, 1)
            for t in range(T):
                act.wait_ge(s_hT, t + 1)
                if t >= 2:
                    act.wait_ge(s_lg, t - 1)
                nc.scalar.activation(tT[:, t % 2, :, :], ps[:, t % 2, 0:D].rearrange("p (k n) -> p k n", k=KC),
                                     ACT.Copy).then_inc(s_tT, 1)
            act.wait_ge(s_b1, 1)
            nc.scalar.activation(b1_cols[:, :], ps[:, 4, 0:EXPERTS * FC], ACT.Copy).then_inc(s_b1_out, 1)
            act.wait_ge(s_route, ROUTE_EXP)
            nc.scalar.activation(choice, choice, ACT.Exp).then_inc(s_route_exp, 1)
            act.wait_ge(s_turn8, 1)
            act.wait_ge(s_placed, 16 * T)
            nc.scalar.activation(one_hot_T.rearrange("e (a t) n -> e a (t n)", a=4), ps[0:EXPERTS, 0:4, :],
                                 ACT.Copy).then_inc(s_turn8_out, 1)

            def gelus(p, n):
                act.wait_ge(s_up, n + 3)
                act.wait_ge(s_b1_tile, n + 1)
                act.wait_ge(s_hid, n * 2 + 2)
                for c in range(FC):
                    m = nc.scalar.activation(
                        hid[:, p, c, :], ps[:, 2 * p + c // 4, (c % 4) * P:(c % 4 + 1) * P],
                        ACT.Gelu_apprx_tanh, bias=b1_tile[:, p, c:c + 1])
                m.then_inc(s_gelu, 1)

            def store_expert(p, j):
                act.wait_ge(s_y, j + 3)
                act.dma_start(y_d[bass.ds(j * P, P), :], y_out[:, p, :]).then_inc(s_y_stored[p], 16)

            gelus(0, 0)
            gelus(1, 1)
            with act.Fori(0, TILE_PAIRS - 1) as i:
                for p in range(2):
                    gelus(p, 2 * i + (2 + p))
                    store_expert(p, 2 * i + p)
            gelus(0, SLOTS - 1)
            for j in range(SLOTS - 3, SLOTS):
                store_expert(j % 2, j)

        @block.tensor
        def _(pe):
            pe.wait_ge(s_const2, 3)

            def transpose_input(A, base):
                for u in range(XT):
                    j = base + u
                    if j >= 4:
                        pe.wait_ge(s_evA, j - 3)
                    pe.wait_ge(A.s.nx, 2 * u + 2)
                    for k in range(KC):
                        for t in range(2):
                            m = pe.transpose(ps[:, j % 4, k * 256 + t * P:k * 256 + (t + 1) * P],
                                             nx[:, (2 * u + t) % 4, k * P:(k + 1) * P], ident[:, :])
                    m.then_inc(s_mmA, 1)

            def project(A, d_base):
                j = d_base
                for w in (A.wq, A.wk):
                    for c in range(A.chunks):
                        for b in range(NB):
                            if j >= 4:
                                pe.wait_ge(s_evD, j - 3)
                            for k in range(KC):
                                m = pe.matmul(ps[:, 4 + j % 4, :], w[:, k, c * P:(c + 1) * P],
                                              nT[:, k, b * BLOCK:(b + 1) * BLOCK], start=k == 0, stop=k == KC - 1)
                            m.then_inc(s_mmD, 1)
                            j += 1
                for t in range(T):
                    pe.wait_ge(s_evD, j - 3)
                    for k in range(KC):
                        m = pe.matmul(ps[:, 4 + j % 4, 0:A.chunks * P], nT[:, k, t * P:(t + 1) * P],
                                      A.wv[:, k, :], start=k == 0, stop=k == KC - 1)
                    m.then_inc(s_mmD, 1)
                    j += 1

            def attention(A):
                def max_block(p, u, job, value):
                    if value is not None:
                        pe.wait_ge(A.s.drained, value)
                    qt, mb = u // NB, u % NB
                    pe.matmul(ps[:, 6 + job % 2, :], A.qa[p][0:A.max_rows, qt * P:(qt + 1) * P],
                              A.ka[p][0:A.max_rows, mb * BLOCK:(mb + 1) * BLOCK],
                              start=True, stop=True).then_inc(A.s.job, 1)

                def turn_maxima(job, drained, tops):
                    pe.wait_ge(A.s.drained, drained)
                    pe.wait_ge(A.s.top, tops)
                    pe.transpose(ps[0:T, 6 + job % 2, 0:P], top[:, :], ident[:, :]).then_inc(A.s.job, 1)

                pe.wait_ge(A.s.loaded[0], 16 * A.loads)
                for u in range(T * NB):
                    max_block(0, u, u, u - 1 if u >= 2 else None)
                turn_maxima(T * NB, T * NB - 1, 1)
                first = T * NB + 1

                def heads(i, last):
                    job = first
                    for p in range(2):
                        final = last and p == 1
                        pe.wait_ge(A.s.row_in, i * 32 + 16 * (p + 1))
                        pe.wait_ge(A.s.loaded[p], i * (16 * A.loads) + 16 * A.loads)
                        if not final:
                            nxt = i + p if isinstance(i, int) else (i if p == 0 else i + 1)
                            pe.wait_ge(A.s.loaded[1 - p], nxt * (16 * A.loads) + 16 * A.loads)

                        def scores(j):
                            n = UNITS * p + j
                            qp, kt = j // T, j % T
                            pe.wait_ge(A.s.exp, i * (2 * UNITS) + (n + 1))
                            keys = slice(kt * P, (kt + 1) * P)
                            for half in range(2):
                                bank = ps[:, 2 * (n % SCORE_SLOTS) + half, :]
                                cols = slice(qp * GQ + half * BLOCK, qp * GQ + (half + 1) * BLOCK)
                                if A.masked:
                                    pe.matmul(bank, A.ka[p][:, keys], A.qa[p][:, cols], start=True, stop=False)
                                    pe.matmul(bank, identb[:, :], mask_cols[:, kt, cols], start=False, stop=False)
                                    m = pe.matmul(bank, A.kb[p][:, keys], A.qb[p][:, cols], start=False, stop=True)
                                else:
                                    m = pe.matmul(bank, A.ka[p][:, keys], A.qa[p][:, cols], start=True, stop=True)
                            m.then_inc(A.s.scores, 1)

                        def values(j):
                            nonlocal job
                            n = UNITS * p + j
                            g, kt = 2 * p + j // T, j % T
                            if kt == 0:
                                pe.wait_ge(A.s.evac, i * 4 + (g + 1))
                            pe.wait_ge(A.s.exp, i * (2 * UNITS) + (n + SCORE_SLOTS + 1))
                            acc = ps[:, 4 + g % 2, :]
                            first_kt, last_kt = kt == 0, kt == T - 1
                            for half in range(2):
                                pr = A.p[:, n % RING, half * BLOCK:(half + 1) * BLOCK]
                                m = pe.matmul(acc[64 * half:64 * half + A.dim, :], A.v[p][:, kt, :], pr,
                                              start=first_kt, stop=last_kt)
                                if not A.masked:
                                    m = pe.matmul(acc[64 * half + 32:64 * half + 64, :], ones[:, 0:32], pr,
                                                  start=first_kt, stop=last_kt)
                            if A.masked and kt >= SUM_TILES:
                                if kt == SUM_TILES:
                                    pe.wait_ge(A.s.drained, i * (2 * A.jobs) + (job - 1))
                                den = ps[:, 6 + job % 2, :]
                                for half in range(2):
                                    m = pe.matmul(den[64 * half:64 * half + 64, :], ones[:, 0:64],
                                                  A.p[:, n % RING, half * BLOCK:(half + 1) * BLOCK],
                                                  start=kt == SUM_TILES, stop=False)
                            m.then_inc(A.s.pv, 1)
                            if A.masked and last_kt:
                                pe.wait_ge(A.s.summed, i * (4 * SUMS) + SUMS * (g + 2))
                                for half in range(2):
                                    m = pe.matmul(den[64 * half:64 * half + 64, :], ones[:, 0:64],
                                                  A.sum[:, g % 2, half * BLOCK:(half + 1) * BLOCK],
                                                  start=False, stop=True)
                                m.then_inc(A.s.job, 1)
                                job += 1

                        for j in range(UNITS):
                            scores(j)
                            if not final:
                                for u in max_units(j):
                                    max_block(1 - p, u, job, i * (2 * A.jobs) + (job - 1))
                                    job += 1
                                if j == TOP_STEP:
                                    turn_maxima(job, i * (2 * A.jobs) + (job - 1), i * 2 + (p + 2))
                                    job += 1
                            if j >= 1:
                                values(j - 1)
                        values(UNITS - 1)

                with pe.Fori(0, PAIRS - 1) as i:
                    heads(i, False)
                heads(PAIRS - 1, True)

            def output_projection(A, wo):
                pe.wait_ge(A.s.o_in, 16)
                for t in range(T):
                    if t >= 2:
                        pe.wait_ge(A.s.proj_used, t - 1)
                    for c in range(A.chunks):
                        m = pe.matmul(ps[:, 6 + t % 2, 0:D], A.oT[:, c, t * P:(t + 1) * P], wo[:, c, :],
                                      start=c == 0, stop=c == A.chunks - 1)
                    m.then_inc(A.s.proj, 1)

            transpose_input(G, 0)
            for t in range(T):
                pe.wait_ge(s_mask, t + 1)
                for half in range(2):
                    j = XT + 2 * t + half
                    pe.wait_ge(s_evA, j - 3)
                    for m8 in range(8):
                        m = pe.transpose(ps[:, j % 4, :].bitcast(BF16)[:, m8 * P:(m8 + 1) * P],
                                         mask_rows[:, t, (8 * half + m8) * P:(8 * half + m8 + 1) * P], identt[:, :])
                    m.then_inc(s_mmA, 1)
            pe.wait_ge(s_w, 16 * 7)
            pe.wait_ge(s_evA, XT)
            project(G, 0)
            pe.wait_ge(s_evA, A_GNN)
            pe.wait_ge(s_evD, D_GNN)
            pe.wait_ge(s_mask_scaled, T)
            pe.wait_ge(G.s.ones_row, 2)
            attention(G)
            pe.wait_ge(G.s.drained, T * NB + 1 + 3 * 2 * G.jobs + G.jobs + 2)
            output_projection(G, gwo)
            transpose_input(F, A_GNN)
            pe.wait_ge(s_fw, 16 * 10)
            pe.wait_ge(s_evA, A_ALL)
            project(F, D_GNN)
            pe.wait_ge(s_evD, D_GNN + FD_QK + T)
            pe.wait_ge(F.s.ones_row, 2)
            attention(F)
            pe.wait_ge(F.s.drained, T * NB + 1 + 3 * 2 * F.jobs + F.jobs)
            output_projection(F, fwo)
            pe.wait_ge(s_moe_w, 16 * 4)

            def logits(t):
                pe.wait_ge(s_tT, t + 1)
                if t >= 2:
                    pe.wait_ge(s_lg_out, t - 1)
                for k in range(KC):
                    m = pe.matmul(ps[:, 2 + t % 2, 0:EXPERTS], tT[:, t % 2, k, :], gate_w[:, k, :],
                                  start=k == 0, stop=k == KC - 1)
                m.then_inc(s_lg, 1)

            for t in range(T):
                pe.wait_ge(s_h, t + 1)
                if t >= 2:
                    pe.wait_ge(s_tT, t - 1)
                for k in range(KC):
                    m = pe.transpose(ps[:, t % 2, k * P:(k + 1) * P], ts[:, t, k * P:(k + 1) * P], ident[:, :])
                m.then_inc(s_hT, 1)
                if t >= 1:
                    logits(t - 1)
            logits(T - 1)
            pe.transpose(ps[:, 4, 0:EXPERTS * FC], b1_rows, ident[0:EXPERTS * FC, 0:EXPERTS * FC]).then_inc(s_b1, 1)
            pe.wait_ge(s_route, ROUTE_ONE_HOT)
            flat = one_hot.rearrange("p t e -> p (t e)")
            pe.matmul(ps[:, 5, 0:P], before[:, :], flat, start=True, stop=True).then_inc(s_prefix, 1)
            pe.matmul(ps[:, 6, 0:P], ones[:, :], flat, start=True, stop=True).then_inc(s_prefix, 1)
            pe.wait_ge(s_lg_out, T)
            for t in range(T):
                m = pe.transpose(ps[0:EXPERTS, t // 4, (t % 4) * P:(t % 4 + 1) * P], one_hot[:, t, :], ident[:, :])
            m.then_inc(s_turn8, 1)

            def turn(p, j):
                pe.wait_ge(s_sorted_in[p], (j - p) * 8 + 16)
                pe.wait_ge(s_sT_out, j * 2 + 2)
                for k in range(KC):
                    m = pe.transpose(ps[:, 6 + p, k * P:(k + 1) * P], sorted_in[:, p, k * P:(k + 1) * P], ident[:, :])
                m.then_inc(s_sT, 1)

            def up(p, j):
                expert = pe.value_load(slot_expert[0:1, bass.ds(j, 1)], min_val=0, max_val=EXPERTS - 1)
                pe.wait_ge(s_sT_out, j * 2 + 6)
                pe.wait_ge(s_gelu, j + 1)
                for c in range(FC):
                    bank = ps[:, 2 * p + c // 4, (c % 4) * P:(c % 4 + 1) * P]
                    for k in range(KC):
                        cols = bass.ds(expert * (KC * FF) + (k * FF + c * P), P)
                        pe.matmul(bank, w1h[:, cols], sTh[:, p, k, :], start=k == 0, stop=False)
                        pe.matmul(bank, w1h[:, cols], sTl[:, p, k, :], start=False, stop=False)
                        m = pe.matmul(bank, w1l[:, cols], sTh[:, p, k, :], start=False, stop=k == KC - 1)
                m.then_inc(s_up, 1)

            def down(p, j):
                expert = pe.value_load(slot_expert[0:1, bass.ds(j, 1)], min_val=0, max_val=EXPERTS - 1)
                pe.wait_ge(s_hid, j * 2 + 6)
                pe.wait_ge(s_y, j + 1)
                bank = ps[:, 4 + p, 0:D]
                for c in range(FC):
                    cols = bass.ds(expert * (FC * D) + c * D, D)
                    pe.matmul(bank, hid_h[:, p, c, :], w2h[:, cols], start=c == 0, stop=False)
                    pe.matmul(bank, hid_l[:, p, c, :], w2h[:, cols], start=False, stop=False)
                    m = pe.matmul(bank, hid_h[:, p, c, :], w2l[:, cols], start=False, stop=c == FC - 1)
                m.then_inc(s_down, 1)

            pe.wait_ge(s_turn8_out, 1)
            pe.wait_ge(s_b1_out, 1)
            pe.wait_ge(s_route, ROUTE_DONE)
            pe.wait_ge(s_w_split, 2 * 4 * EXPERTS)
            turn(0, 0)
            turn(1, 1)
            up(0, 0)
            with pe.Fori(0, TILE_PAIRS - 1) as i:
                turn(0, 2 * i + 2)
                up(1, 2 * i + 1)
                down(0, 2 * i)
                turn(1, 2 * i + 3)
                up(0, 2 * i + 2)
                down(1, 2 * i + 1)
            turn(0, SLOTS - 1)
            up(1, SLOTS - 2)
            down(0, SLOTS - 3)
            up(0, SLOTS - 1)
            down(1, SLOTS - 2)
            down(0, SLOTS - 1)
            pe.wait_ge(s_sT_out, 2 * SLOTS + 4)
            for t in range(T):
                if t >= 2:
                    pe.wait_ge(s_sum, t - 1)
                pe.matmul(ps[:, 6 + t % 2, 0:D], one_hot_T[:, t, :], b2_rows, start=True, stop=True)\
                    .then_inc(s_b2, 1)

        @block.vector
        def _(dve):
            dve.wait_ge(s_const, 3)
            nc.vector.tensor_scalar(identb[:, :], ident[:, :], MASKED, None, ALU.mult).then_inc(s_const2, 1)
            nc.vector.tensor_copy(identt[:, :], ident[:, :]).then_inc(s_const2, 1)
            nc.vector.memset(amax[:, :, :], 0.0).then_inc(s_const2, 1)

            def layer_norm(A):
                n = [0]

                def link(ins):
                    ins.then_inc(A.s.ln, 1)
                    n[0] += 1
                    dve.wait_ge(A.s.ln, n[0])

                for t in range(T):
                    if A is G and t % 8 == 0:
                        dve.wait_ge(s_x[t // 8], 16)
                    if A is F:
                        dve.wait_ge(G.s.proj_used, t + 1)
                    nc.vector.bn_stats(stats[:, t, :], xs[:, t, :]).then_inc(A.s.ln, 1)
                n[0] += T
                dve.wait_ge(A.s.ln, n[0])
                for t in range(T):
                    nc.vector.bn_aggr(mv[:, t, :], stats[:, t, :]).then_inc(A.s.ln, 1)
                n[0] += T
                dve.wait_ge(A.s.ln, n[0])
                link(nc.vector.tensor_scalar(veps, mv[:, :, 1], EPS, None, ALU.add))
                dve.wait_ge(A.s.sqrt, 1)
                link(nc.vector.reciprocal(rstd, std))
                link(nc.vector.tensor_tensor(tmp, rstd, rstd, ALU.mult))
                link(nc.vector.tensor_tensor(tmp, tmp, veps, ALU.mult))
                link(nc.vector.tensor_scalar(tmp, tmp, -0.5, 1.5, ALU.mult, ALU.add))
                link(nc.vector.tensor_tensor(rstd, rstd, tmp, ALU.mult))
                base = 0 if A is G else A_GNN
                for t in range(T):
                    if t >= 4:
                        dve.wait_ge(s_mmA, base + (t - 4) // 2 + 1)
                    nc.vector.tensor_scalar(nx[:, t % 4, :], xs[:, t, :], mv[:, t, 0:1], rstd[:, t:t + 1],
                                            ALU.subtract, ALU.mult).then_inc(A.s.nx, 1)

            def low_halves(A, d_base, biased):
                for n in range(2 * A.chunks):
                    if n >= 2:
                        dve.wait_ge(A.s.qk_stored[n % 2], 32 * (n // 2))
                    for b in range(NB):
                        j = d_base + NB * n + b
                        dve.wait_ge(s_mmD, j + 1)
                        dve.wait_ge(A.s.hi, NB * n + b + 1)
                        cols = slice(b * BLOCK, (b + 1) * BLOCK)
                        if biased:
                            col = (bq_cols, bk_cols)[n // A.chunks][:, n % A.chunks:n % A.chunks + 1]
                            nc.vector.scalar_tensor_tensor(
                                out=lo_st[:, n % 2, cols], in0=ps[:, 4 + j % 4, :], scalar=col,
                                in1=hi_st[:, n % 2, cols], op0=ALU.add, op1=ALU.subtract).then_inc(s_evD, 1)
                        else:
                            nc.vector.tensor_tensor(lo_st[:, n % 2, cols], ps[:, 4 + j % 4, :],
                                                    hi_st[:, n % 2, cols], ALU.subtract).then_inc(s_evD, 1)
                width = A.chunks * P
                for t in range(T):
                    j = d_base + NB * 2 * A.chunks + t
                    dve.wait_ge(s_mmD, j + 1)
                    if t >= 2:
                        dve.wait_ge(A.s.v_stored[t % 2], 16 * (t // 2))
                    if biased:
                        nc.vector.tensor_tensor(v_st[:, t % 2, 0:width], ps[:, 4 + j % 4, 0:width], bias_v,
                                                ALU.add).then_inc(s_evD, 1)
                    else:
                        nc.vector.tensor_copy(v_st[:, t % 2, 0:width], ps[:, 4 + j % 4, 0:width]).then_inc(s_evD, 1)

            def attention(A):
                def block_max(u, job, value):
                    qt, mb = u // NB, u % NB
                    dve.wait_ge(A.s.job, value)
                    bank = ps[:, 6 + job % 2, :]
                    if A.masked:
                        nc.vector.tensor_tensor_reduce(
                            out=A.junk[:, u % 2, :], in0=bank, in1=mask_rows[:, qt, mb * BLOCK:(mb + 1) * BLOCK],
                            scale=1.0, scalar=-3e38, op0=ALU.add, op1=ALU.max,
                            accum_out=amax[:, qt, mb:mb + 1]).wait_op(s_mask_scaled, T, "sem-ge")\
                            .then_inc(A.s.drained, 1)
                    else:
                        nc.vector.tensor_reduce(amax[:, qt, mb:mb + 1], bank, AX.X, ALU.max)\
                            .then_inc(A.s.drained, 1)

                def head_max(drained):
                    dve.wait_ge(A.s.drained, drained)
                    nc.vector.tensor_reduce(top[:, :], amax[:, :, :], AX.X, ALU.max).then_inc(A.s.top, 1)

                def negate(job, value, row_in):
                    dve.wait_ge(A.s.job, value)
                    if row_in is not None:
                        dve.wait_ge(A.s.row_in, row_in)
                    nc.vector.tensor_scalar(neg_top[:, :], ps[0:T, 6 + job % 2, 0:P], -1.0, None, ALU.mult)\
                        .then_inc(A.s.drained, 1)

                for u in range(T * NB):
                    block_max(u, u, u + 1)
                head_max(T * NB)
                negate(T * NB, T * NB + 1, None)
                first = T * NB + 1

                def heads(i, last):
                    job = first
                    for p in range(2):
                        final = last and p == 1

                        def group_out(qp):
                            nonlocal job
                            g = 2 * p + qp
                            acc, o = ps[:, 4 + g % 2, :], A.o[:, qp, :]
                            if A.masked:
                                dve.wait_ge(A.s.job, i * (2 * A.jobs) + (job + 1))
                                dve.wait_ge(A.s.evac, i * 4 + (g + 2))
                                nc.vector.reciprocal(A.r, ps[:, 6 + job % 2, :]).then_inc(A.s.drained, 1)
                                job += 1
                                dve.wait_ge(A.s.drained, i * (2 * A.jobs) + job)
                                dve.wait_ge(A.s.pv, i * (2 * UNITS) + (RING + T * (g + 1)))
                                dve.wait_ge(A.s.o_stored[qp], i * 64 + 32 * (p + 1))
                                nc.vector.tensor_tensor(o, acc, A.r, ALU.mult).then_inc(A.s.evac, 1)
                            else:
                                dve.wait_ge(A.s.pv, i * (2 * UNITS) + (RING + T * (g + 1)))
                                dve.wait_ge(A.s.evac, i * 4 + (g + 2))
                                for half in range(2):
                                    r = slice(64 * half, 64 * half + 32)
                                    den = slice(64 * half + 32, 64 * half + 64)
                                    nc.vector.reciprocal(A.r[r, :], acc[den, :]).then_inc(A.s.evac_step, 1)
                                dve.wait_ge(A.s.evac_step, i * 12 + (3 * g + 2))
                                dve.wait_ge(A.s.o_stored[qp], i * 64 + 32 * (p + 1))
                                nc.vector.tensor_tensor(o[0:32, :], acc[0:32, :], A.r[0:32, :], ALU.mult)\
                                    .then_inc(A.s.evac_step, 1)
                                nc.vector.tensor_tensor(o[64:96, :], acc[64:96, :], A.r[64:96, :], ALU.mult)\
                                    .then_inc(A.s.evac, 1)

                        for j in range(UNITS):
                            if not final:
                                for u in max_units(j):
                                    block_max(u, job, i * (2 * A.jobs) + (job + 1))
                                    job += 1
                                    if u == T * NB - 1:
                                        head_max(i * (2 * A.jobs) + job)
                                if j == TOP_STEP:
                                    negate(job, i * (2 * A.jobs) + (job + 1), i * 32 + 16 * (p + 1))
                                    job += 1
                            if j == T:
                                group_out(0)
                        group_out(1)

                with dve.Fori(0, PAIRS - 1) as i:
                    heads(i, False)
                heads(PAIRS - 1, True)

            layer_norm(G)
            for t in range(T):
                dve.wait_ge(s_adj[t % 2], 16 * (t // 2 + 1))
                diag = adj_in[:, t % 2, t * P:(t + 1) * P]
                nc.vector.tensor_tensor(diag, diag, ident[:, :], ALU.max).then_inc(s_adj_diag, 1)
                dve.wait_ge(s_adj_diag, t + 1)
                nc.vector.tensor_scalar(mask_rows[:, t, :], adj_in[:, t % 2, :], -1.0, None, ALU.add)\
                    .then_inc(s_mask, 1)
            dve.wait_ge(s_w, 16)
            low_halves(G, 0, False)
            for t in range(T):
                dve.wait_ge(s_mmA, XT + 2 * t + 2)
                nc.vector.tensor_scalar(mask_rows[:, t, :], mask_rows[:, t, :], MASKED, None, ALU.mult)\
                    .then_inc(s_mask_scaled, 1)
            dve.wait_ge(s_mask_scaled, T)
            attention(G)
            for t in range(T):
                dve.wait_ge(G.s.proj, t + 1)
                nc.vector.tensor_tensor(xs[:, t, :], ps[:, 6 + t % 2, 0:D], xs[:, t, :], ALU.add)\
                    .then_inc(G.s.proj_used, 1)
            layer_norm(F)
            dve.wait_ge(s_fw, 16 * 10)
            low_halves(F, D_GNN, True)
            attention(F)

            for t in range(T):
                dve.wait_ge(F.s.proj, t + 1)
                nc.vector.tensor_scalar(xn[:, t % 2, :], xs[:, t, :], mv[:, t, 0:1], rstd[:, t:t + 1],
                                        ALU.subtract, ALU.mult).then_inc(s_hsum, 1)
                dve.wait_ge(s_hsum, 2 * t + 1)
                nc.vector.tensor_tensor(xn[:, t % 2, :], xn[:, t % 2, :], bias_o, ALU.add).then_inc(s_hsum, 1)
                dve.wait_ge(s_hsum, 2 * t + 2)
                nc.vector.tensor_tensor(ts[:, t, :], ps[:, 6 + t % 2, 0:D], xn[:, t % 2, :], ALU.add)\
                    .then_inc(F.s.proj_used, 1)
            n = [0]

            def link2(ins):
                ins.then_inc(s_ln2, 1)
                n[0] += 1
                dve.wait_ge(s_ln2, n[0])

            for t in range(T):
                dve.wait_ge(F.s.proj_used, t + 1)
                nc.vector.bn_stats(stats[:, t, :], ts[:, t, :]).then_inc(s_ln2, 1)
            n[0] += T
            dve.wait_ge(s_ln2, n[0])
            for t in range(T):
                nc.vector.bn_aggr(mv2[:, t, :], stats[:, t, :]).then_inc(s_ln2, 1)
            n[0] += T
            dve.wait_ge(s_ln2, n[0])
            link2(nc.vector.tensor_scalar(veps, mv2[:, :, 1], EPS, None, ALU.add))
            dve.wait_ge(s_sqrt2, 1)
            link2(nc.vector.reciprocal(rstd, std))
            link2(nc.vector.tensor_tensor(tmp, rstd, rstd, ALU.mult))
            link2(nc.vector.tensor_tensor(tmp, tmp, veps, ALU.mult))
            link2(nc.vector.tensor_scalar(tmp, tmp, -0.5, 1.5, ALU.mult, ALU.add))
            link2(nc.vector.tensor_tensor(rstd, rstd, tmp, ALU.mult))
            for t in range(T):
                link2(nc.vector.scalar_tensor_tensor(out=ts[:, t, :], in0=ts[:, t, :], scalar=mv2[:, t, 0:1],
                                                     in1=ln_g, op0=ALU.subtract, op1=ALU.mult))
                nc.vector.scalar_tensor_tensor(out=ts[:, t, :], in0=ts[:, t, :], scalar=rstd[:, t:t + 1],
                                               in1=ln_b, op0=ALU.mult, op1=ALU.add).then_inc(s_h, 1)
            for t in range(T):
                dve.wait_ge(s_lg, t + 1)
                nc.vector.tensor_tensor(logits[:, t, :], ps[:, 2 + t % 2, 0:EXPERTS], gate_b, ALU.add)\
                    .then_inc(s_lg_out, 1)
            dve.wait_ge(s_lg_out, T)

            r = [0]

            def link(ins):
                ins.then_inc(s_route, 1)
                r[0] += 1
                dve.wait_ge(s_route, r[0])

            def wide(a):
                return a.unsqueeze(2).to_broadcast([P, T, EXPERTS])

            def tiles(a, n):
                return a.unsqueeze(1).to_broadcast([P, n, EXPERTS])

            link(nc.vector.tensor_reduce(tmp, logits, AX.X, ALU.max))
            link(nc.vector.tensor_tensor(choice, logits, wide(tmp), ALU.subtract))
            assert r[0] == ROUTE_EXP
            link(nc.vector.tensor_tensor(one_hot, logits, wide(tmp), ALU.is_equal))
            link(nc.vector.tensor_tensor(one_hot, one_hot, tiles(e_iota[:, :], T), ALU.mult))
            link(nc.vector.tensor_reduce(tmp, one_hot, AX.X, ALU.max))
            link(nc.vector.tensor_tensor(one_hot, one_hot, wide(tmp), ALU.is_equal))
            assert r[0] == ROUTE_ONE_HOT
            dve.wait_ge(s_route_exp, 1)
            link(nc.vector.tensor_reduce(tmp, choice, AX.X, ALU.add))
            link(nc.vector.reciprocal(gate[:, :], tmp))
            dve.wait_ge(s_prefix, 2)
            link(nc.vector.tensor_copy(totals, ps[:, 6, 0:P].rearrange("p (t e) -> p t e", t=T)))
            src, dst = totals, run0
            for step in (1, 2, 4, 8):
                link(nc.vector.tensor_copy(dst[:, 0:step, :], src[:, 0:step, :]))
                link(nc.vector.tensor_tensor(dst[:, step:T, :], src[:, step:T, :], src[:, 0:T - step, :], ALU.add))
                src, dst = dst, (run1 if dst is run0 else run0)
            link(nc.vector.tensor_tensor(place, src, totals, ALU.subtract))
            link(nc.vector.tensor_tensor(rank, ps[:, 5, 0:P].rearrange("p (t e) -> p t e", t=T), place, ALU.add))
            link(nc.vector.tensor_scalar(counts[:, 0, :], src[:, T - 1, :], float(P - 1), None, ALU.add))
            link(nc.vector.tensor_copy(counts_i[:, :], counts[:, 0, :]))
            link(nc.vector.tensor_scalar(counts_i[:, :], counts_i[:, :], P.bit_length() - 1, None,
                                         ALU.logical_shift_right))
            link(nc.vector.tensor_copy(counts[:, 0, :], counts_i[:, :]))
            for step, a, b in ((1, 0, 1), (2, 1, 2), (4, 2, 1)):
                link(nc.vector.tensor_copy(counts[:, b, 0:step], counts[:, a, 0:step]))
                link(nc.vector.tensor_tensor(counts[:, b, step:EXPERTS], counts[:, a, step:EXPERTS],
                                             counts[:, a, 0:EXPERTS - step], ALU.add))
            link(nc.vector.tensor_tensor(counts[:, 2, :], counts[:, 1, :], counts[:, 0, :], ALU.subtract))
            link(nc.vector.tensor_scalar(counts[:, 2, :], counts[:, 2, :], float(P), None, ALU.mult))
            link(nc.vector.tensor_tensor(rank, rank, tiles(counts[:, 2, :], T), ALU.add))
            link(nc.vector.tensor_tensor(rank, rank, one_hot, ALU.mult))
            link(nc.vector.tensor_reduce(tmp, rank, AX.X, ALU.add))
            link(nc.vector.tensor_copy(slot_row[:, :], tmp))
            assert r[0] == ROUTE_ROWS, r[0]
            link(nc.vector.tensor_tensor(slot_of, tiles(counts[:, 1, :], SLOTS),
                                         slot_iota[:, :].unsqueeze(2).to_broadcast([P, SLOTS, EXPERTS]), ALU.is_le))
            link(nc.vector.tensor_reduce(slot_expert_f[:, :], slot_of, AX.X, ALU.add))
            link(nc.vector.tensor_scalar(slot_expert_f[:, :], slot_expert_f[:, :], float(EXPERTS - 1), None, ALU.min))
            link(nc.vector.tensor_copy(slot_expert[:, :], slot_expert_f[:, :]))
            assert r[0] == ROUTE_DONE, r[0]

            dve.wait_ge(s_b1_out, 1)
            dve.wait_ge(s_placed, 16 * T)

            def split_input(p, j):
                dve.wait_ge(s_sT, j + 1)
                dve.wait_ge(s_up, j + 1)
                bank = ps[:, 6 + p, 0:D].rearrange("p (k n) -> p k n", k=KC)
                nc.vector.tensor_copy(sTh[:, p, :, :], bank).then_inc(s_sT_out, 1)
                dve.wait_ge(s_sT_out, j * 2 + 5)
                nc.vector.tensor_tensor(sTl[:, p, :, :], bank, sTh[:, p, :, :], ALU.subtract).then_inc(s_sT_out, 1)

            def first_bias(p, j):
                expert = dve.value_load(slot_expert[0:1, bass.ds(j, 1)], min_val=0, max_val=EXPERTS - 1)
                dve.wait_ge(s_gelu, j + 1)
                nc.vector.tensor_copy(b1_tile[:, p, :], b1_cols[:, bass.ds(expert * FC, FC)]).then_inc(s_b1_tile, 1)

            def split_hidden(p, j):
                dve.wait_ge(s_gelu, j + 3)
                dve.wait_ge(s_down, j + 1)
                nc.vector.tensor_copy(hid_h[:, p, :, :], hid[:, p, :, :]).then_inc(s_hid, 1)
                dve.wait_ge(s_hid, j * 2 + 5)
                nc.vector.tensor_tensor(hid_l[:, p, :, :], hid[:, p, :, :], hid_h[:, p, :, :], ALU.subtract)\
                    .then_inc(s_hid, 1)

            def expert_out(p, j):
                dve.wait_ge(s_down, j + 3)
                dve.wait_ge(s_y_stored[p], (j - p) * 8 + 16)
                nc.vector.tensor_copy(y_out[:, p, :], ps[:, 4 + p, 0:D]).then_inc(s_y, 1)

            def tile(p, j, more):
                if more:
                    split_input(p, j + 2)
                first_bias(1 - p, j + 1)
                split_hidden(p, j)
                expert_out(p, j)

            first_bias(0, 0)
            split_input(0, 0)
            split_input(1, 1)
            with dve.Fori(0, TILE_PAIRS - 1) as i:
                for p in range(2):
                    tile(p, 2 * i + p, True)
            tile(0, SLOTS - 3, True)
            tile(1, SLOTS - 2, False)
            split_hidden(0, SLOTS - 1)
            expert_out(0, SLOTS - 1)
            for t in range(T):
                dve.wait_ge(s_y_in[t % 4], 16 * (t // 4 + 1))
                dve.wait_ge(s_b2, t + 1)
                nc.vector.tensor_tensor(y_in[:, t % 4, :], ps[:, 6 + t % 2, 0:D], y_in[:, t % 4, :], ALU.add)\
                    .then_inc(s_sum, 1)
                dve.wait_ge(s_sum, t + 1)
                if t >= 4:
                    dve.wait_ge(s_out[t % 4], 16 * (t // 4))
                nc.vector.scalar_tensor_tensor(out=res[:, t % 4, :], in0=y_in[:, t % 4, :], scalar=gate[:, t:t + 1],
                                               in1=xs[:, t, :], op0=ALU.mult, op1=ALU.add).then_inc(s_res, 1)


_INS = ['x', 'adj', 'L0_gnn_Wks', 'L0_gnn_Wqs', 'L0_gnn_Wvs', 'L0_gnn_Wo', 'L0_ffn_ln1_g', 'L0_ffn_ln1_b',
        'L0_ffn_Wq', 'L0_ffn_bq', 'L0_ffn_Wk', 'L0_ffn_bk', 'L0_ffn_Wv', 'L0_ffn_bv', 'L0_ffn_Wo', 'L0_ffn_bo',
        'L0_ffn_gate_W', 'L0_ffn_gate_b', 'L0_ffn_W1', 'L0_ffn_b1', 'L0_ffn_W2', 'L0_ffn_b2']


def kernel(**inputs):
    import numpy as np
    import concourse.bacc as bacc
    from concourse.bass_utils import run_bass_kernel_spmd

    nc = bacc.Bacc("TRN2", target_bir_lowering=False, num_devices=1)
    arrays, aps = {}, {}
    for name in _INS:
        a = np.ascontiguousarray(inputs[name])
        arrays["in_" + name] = a
        aps[name] = nc.dram_tensor("in_" + name, a.shape, mybir.dt.from_np(a.dtype), kind="ExternalInput").ap()
    out = nc.dram_tensor("out", (N, D), F32, kind="ExternalOutput").ap()
    gnn = {k[len("L0_gnn_"):]: v for k, v in aps.items() if k.startswith("L0_gnn_")}
    ffn = {k[len("L0_ffn_"):]: v for k, v in aps.items() if k.startswith("L0_ffn_")}
    fused_graph_ffn(nc, aps["x"], aps["adj"], gnn, ffn, out)
    r = run_bass_kernel_spmd(nc, [arrays], core_ids=[0])
    return r.results[0]["out"]
```

```python
from contextlib import ExitStack

import concourse.bass as bass
from concourse import mybir

F32 = mybir.dt.float32
F16 = mybir.dt.float16
BF16 = mybir.dt.bfloat16
F8 = mybir.dt.float8e5
I32 = mybir.dt.int32
U32 = mybir.dt.uint32
ALU = mybir.AluOpType
ACT = mybir.ActivationFunctionType
AX = mybir.AxisListType


class Names:
    pass


P = 128
N = 2048
D = 256
T = N // P
KC = D // P
HEADS = 8
EXPERTS = 8
FF = 4 * D
FC = FF // P
EPS = 1e-5
BLOCK = 512
NB = N // BLOCK
SLOTS = (N - EXPERTS) // P + EXPERTS
MASKED = 8e16

QP = 2
GQ = N // QP
UNITS = QP * T
RING = 4
SCORE_SLOTS = 2
PAIRS = HEADS // 2
TOP_STEP = 28




def max_units(A, step):
    if step not in A.max_steps:
        return range(0)
    at, n = A.max_steps.index(step), len(A.max_steps)
    return range(at * T * NB // n, (at + 1) * T * NB // n)


TILE_PAIRS = (SLOTS - 1) // 2
SUM_TILES = T - 2
SUMS = SUM_TILES - 1

KB = 1024

ROUTE_EXP, ROUTE_ONE_HOT, ROUTE_ROWS, ROUTE_DONE = 2, 6, 35, 39


def fused_graph_ffn(nc, x, adj, gW, fW, out):
    ctx = ExitStack()
    with ctx:
        def sb(name, shape, dt):
            return ctx.enter_context(nc.sbuf_tensor(name, shape, dt))

        def sem(name):
            return ctx.enter_context(nc.semaphore(name))

        def dram(name, shape, dt):
            return nc.dram_tensor(name, shape, dt, kind="Internal").ap()

        arena = sb("arena", [P, 202 * KB // 4], F32)
        size = {F32: 4, I32: 4, U32: 4, F16: 2, BF16: 2, F8: 1}

        def at(kb, shape, dt):
            n = 1
            for s in shape[1:]:
                n *= s
            words = n * size[dt] // 4
            a = arena[0:shape[0], int(kb * KB) // 4:int(kb * KB) // 4 + words]
            if dt != F32:
                a = a.bitcast(dt)
            if len(shape) == 3:
                a = a.rearrange("p (a b) -> p a b", a=shape[1])
            if len(shape) == 4:
                a = a.rearrange("p (a b c) -> p a b c", a=shape[1], b=shape[2])
            return a

        xs = at(0, [P, T, D], F32)
        gwo = at(16, [P, 4, D], F32)
        bias_v, bias_o, ln_g, ln_b = (at(16 + i, [P, D], F32) for i in range(4))
        fwq, fwk, fwv, fwo = (at(20 + 2 * i, [P, KC, D], F32) for i in range(4))
        mask_rows = at(28, [P, T, N], BF16)
        mask_cols = at(92, [P, T, N], F8)
        w1h = at(28, [P, EXPERTS * KC * FF], F16)
        w1l = at(60, [P, EXPERTS * KC * FF], F16)
        w2h = at(92, [P, EXPERTS * FC * D], F16)
        w2l = at(162, [P, EXPERTS * FC * D], F16)
        hi_st = at(124, [P, 2, N], F16)
        lo_st = at(132, [P, 2, N], F16)
        gwq, gwk, gwv = (at(kb, [P, KC, HEADS * 64], F32) for kb in (140, 144, 180))
        adj_in = at(148, [P, 2, N], F32)
        nT = at(164, [P, KC, N], F32)
        v_st = at(184, [P, 2, BLOCK], F32)
        nx = at(188, [P, 4, D], F32)
        w_in = at(194, [P, 2, 1024], F32)
        f_oT = at(124, [P, 2, N], F32)
        ts = at(140, [P, T, D], F32)
        zero_tile = at(201, [P, D], F32)
        xn = at(156, [P, 2, D], F32)
        tT = at(158, [P, 2, KC, P], F32)
        logits, choice, one_hot, rank = (at(160 + i / 2, [P, T, EXPERTS], F32) for i in range(4))
        totals, run0, run1, place = (at(20 + i / 2, [P, T, EXPERTS], F32) for i in range(4))
        slot_of = at(22, [P, SLOTS, EXPERTS], F32)
        b2_rows = at(24, [EXPERTS, D], F32)
        b1_rows = at(25, [EXPERTS * FC, P], F32)
        gate_w = at(25.5, [P, KC, EXPERTS], F32)
        gate_b = at(25.625, [P, EXPERTS], F32)
        sorted_in = at(124, [P, 2, D], F32)
        sTh = at(126, [P, 2, KC, P], F16)
        sTl = at(127, [P, 2, KC, P], F16)
        hid = at(128, [P, 2, FC, P], F32)
        hid_h = at(136, [P, 2, FC, P], F16)
        hid_l = at(140, [P, 2, FC, P], F16)
        y_out = at(144, [P, 2, D], F32)
        y_in = at(146, [P, 4, D], F32)
        res = at(150, [P, 4, D], F32)
        one_hot_T = at(154, [EXPERTS, T, P], F32)

        small = sb("small", [P, 128], F32)
        ident = sb("ident", [P, P], F32)
        identb = sb("identb", [P, P], BF16)
        identt = sb("identt", [P, P], BF16)
        ones = sb("ones", [P, P], F32)
        ps = ctx.enter_context(nc.psum_tensor("ps", [P, 8, BLOCK], F32))

        sorted_d = dram("sorted_tokens", [SLOTS * P, D], F32)
        y_d = dram("expert_out", [SLOTS * P, D], F32)

        def scratch(name, width):
            d = Names()
            d.q = dram(name + "_q", [HEADS, 2, width // HEADS, N], F16)
            d.k = dram(name + "_k", [HEADS, 2, width // HEADS, N], F16)
            d.v = dram(name + "_v", [P, T, width], F32)
            d.o = dram(name + "_o", [width, N], F32)
            return d

        def attention_sems(name):
            s = Names()
            s.ln = sem(name + "_ln")
            s.sqrt = sem(name + "_sqrt")
            s.nx = sem(name + "_nx")
            s.hi = sem(name + "_hi")
            s.qk_stored = [sem(name + f"_qk_stored{i}") for i in range(2)]
            s.v_stored = [sem(name + f"_v_stored{i}") for i in range(2)]
            s.loaded = [sem(name + f"_loaded{i}") for i in range(2)]
            s.rest = [sem(name + f"_rest{i}") for i in range(2)]
            s.ones_row = sem(name + "_ones_row")
            s.v_full = sem(name + "_v_full")
            s.v_out = sem(name + "_v_out")
            s.scores = sem(name + "_scores")
            s.exp = sem(name + "_exp")
            s.pv = sem(name + "_pv")
            s.summed = sem(name + "_summed")
            s.evac = sem(name + "_evac")
            s.evac_step = sem(name + "_evac_step")
            s.job = sem(name + "_job")
            s.drained = sem(name + "_drained")
            s.top = sem(name + "_top")
            s.row_in = sem(name + "_row_in")
            s.o_stored = [sem(name + f"_o_stored{i}") for i in range(2)]
            s.o_in = sem(name + "_o_in")
            s.proj = sem(name + "_proj")
            s.proj_used = sem(name + "_proj_used")
            return s

        amax = sb("amax", [P, T, NB], F32)
        top = sb("top", [P, T], F32)
        neg_top = sb("neg_top", [T, P], F16)

        G = Names()
        G.masked, G.dim, G.chunks, G.scale, G.max_rows = True, 64, 4, 64 ** -0.5, P
        G.max_steps = [j for j in range(4, TOP_STEP - 1) if j not in (T - 1, T, T + 1)]
        G.jobs, G.top_job = T * NB + 1 + QP, T * NB + 1
        G.d, G.s = scratch("gnn", 512), attention_sems("gnn")
        G.ka = [at(124 + 16 * i, [P, N], F16) for i in range(2)]
        G.kb = [at(128 + 16 * i, [65, N], F16) for i in range(2)]
        G.qa = [at(132 + 16 * i, [P, N], F16) for i in range(2)]
        G.qb = [at(136 + 16 * i, [65, N], F16) for i in range(2)]
        G.v = [at(156 + 4 * i, [P, T, 64], F32) for i in range(2)]
        G.p = at(164, [P, RING, GQ], F32)
        G.sum = at(180, [P, 2, GQ], F32)
        G.r = at(188, [P, BLOCK], F32)
        G.o = at(190, [P, 2, BLOCK], F32)
        G.junk = at(194, [P, 2, BLOCK], BF16)
        G.row = [G.qb[i][64:65, :] for i in range(2)]
        G.ones_row = [G.kb[i][64:65, :] for i in range(2)]
        G.oT = at(124, [P, 4, N], F32)
        G.loads, G.rests = 3, 3
        G.wq, G.wk, G.wv = gwq, gwk, gwv
        F = Names()
        F.masked, F.dim, F.chunks, F.scale, F.max_rows = False, 32, 2, 32 ** -0.5, 96
        F.max_steps = [j for j in range(5, TOP_STEP - 1) if j not in (T + 1, T + 2)]
        F.jobs, F.top_job = T * NB + 1, T * NB
        F.d, F.s = scratch("ffn", 256), attention_sems("ffn")
        F.ka = [at(124 + 8 * i, [97, N], F16) for i in range(2)]
        F.qa = [at(128 + 8 * i, [97, N], F16) for i in range(2)]
        F.v = [at(140 + 2 * i, [P, T, 32], F32) for i in range(2)]
        F.p = at(144, [P, RING, GQ], F32)
        F.r = at(160, [P, BLOCK], F32)
        F.o = at(20, [P, 2, BLOCK], F32)
        F.row = [F.qa[i][96:97, :] for i in range(2)]
        F.ones_row = [F.ka[i][96:97, :] for i in range(2)]
        F.oT = f_oT
        F.loads, F.rests = 4, 1
        F.wq, F.wk, F.wv = fwq, fwk, fwv
        bq_cols = sb("bq_cols", [P, 2], F32)
        bk_cols = sb("bk_cols", [P, 2], F32)

        b1_cols = sb("b1_cols", [P, EXPERTS * FC], F32)
        b1_tile = sb("b1_tile", [P, 2, FC], F32)
        before = sb("before", [P, P], F32)
        e_iota = sb("e_iota", [P, EXPERTS], F32)
        slot_iota = sb("slot_iota", [P, SLOTS], F32)
        counts = sb("counts", [P, 3, EXPERTS], F32)
        counts_i = sb("counts_i", [P, EXPERTS], I32)
        gate = sb("gate", [P, T], F32)
        slot_row = sb("slot_row", [P, T], I32)
        slot_expert = sb("slot_expert", [P, SLOTS], I32)
        slot_expert_f = sb("slot_expert_f", [P, SLOTS], F32)
        mv2 = sb("mv2", [P, T, 2], F32)
        stats = sb("stats", [P, T, 6], F32)
        mv = sb("mv", [P, T, 2], F32)
        veps = small[:, 0:16]
        std = small[:, 16:32]
        rstd = small[:, 32:48]
        tmp = small[:, 48:64]

        s_x = [sem(f"x_in{i}") for i in range(2)]
        s_w = sem("gnn_weights_in")
        s_fw = sem("ffn_weights_in")
        s_adj = [sem(f"adj_in{i}") for i in range(2)]
        s_adj_diag = sem("adj_diag")
        s_mask = sem("mask_rows_raw")
        s_mask_scaled = sem("mask_rows_scaled")
        s_const = sem("constants")
        s_const2 = sem("constants_derived")
        s_mmA = sem("bank_for_scalar_full")
        s_evA = sem("bank_for_scalar_free")
        s_mmD = sem("bank_for_vector_full")
        s_evD = sem("bank_for_vector_free")
        s_moe_w = sem("moe_vectors_in")
        s_moe_const = sem("moe_constants")
        s_zero = sem("sorted_zeroed")
        s_w_in = [sem(f"expert_weights_in{i}") for i in range(2)]
        s_w_split = sem("expert_weights_split")
        s_hsum = sem("attention_residual")
        s_ln2 = sem("second_norm")
        s_sqrt2 = sem("second_norm_root")
        s_h = sem("hidden_tile")
        s_hT = sem("hidden_turned")
        s_tT = sem("hidden_turned_out")
        s_lg = sem("logits_full")
        s_lg_out = sem("logits_out")
        s_route = sem("routing")
        s_route_exp = sem("routing_exp")
        s_prefix = sem("prefix_counts")
        s_one_hot = sem("one_hot")
        s_turn8 = sem("one_hot_turned")
        s_turn8_out = sem("one_hot_turned_out")
        s_b1 = sem("b1_turned")
        s_b1_out = sem("b1_turned_out")
        s_zero_in = sem("zero_tile")
        s_placed = sem("tokens_placed")
        s_sorted_in = [sem(f"sorted_in{i}") for i in range(2)]
        s_sT = sem("sorted_turned")
        s_sT_out = sem("sorted_split")
        s_up = sem("up_products")
        s_gelu = sem("gelu")
        s_b1_tile = sem("b1_of_tile")
        s_hid = sem("hidden_split")
        s_down = sem("down_products")
        s_y = sem("expert_tile_out")
        s_y_stored = [sem(f"expert_tile_stored{i}") for i in range(2)]
        s_y_in = [sem(f"token_rows_in{i}") for i in range(4)]
        s_b2 = sem("b2_selected")
        s_sum = sem("expert_sum")
        s_res = sem("result_tile")
        s_out = [sem(f"result_stored{i}") for i in range(4)]

        block = ctx.enter_context(nc.Block())

        XT = T // 2
        A_GNN = XT + 2 * T
        A_ALL = A_GNN + XT
        D_QK = 2 * 4 * NB
        D_GNN = D_QK
        FD_QK = 2 * 2 * NB

        @block.sync
        def _(sp):
            for i in range(2):
                sp.dma_start(xs[:, 8 * i:8 * i + 8, :],
                             x[1024 * i:1024 * i + 1024, :].rearrange("(t p) d -> p t d", p=P)).then_inc(s_x[i], 16)
            for w, a in zip((gwq, gwk, gwv), (gW["Wqs"], gW["Wks"], gW["Wvs"])):
                for c in range(KC):
                    sp.dma_start(w[:, c, :].rearrange("p (h k) -> p h k", h=HEADS),
                                 a[:, c * P:(c + 1) * P, :].rearrange("h p k -> p h k")).then_inc(s_w, 16)
            sp.dma_start(gwo, gW["Wo"].rearrange("h k o -> (h k) o").rearrange("(c p) o -> p c o", p=P)).then_inc(s_w, 16)
            def store_chunk(A, d_base, n):
                sp.wait_ge(s_evD, d_base + NB * (n + 1))
                dst, c, per = (A.d.q, A.d.k)[n % 2], n // 2, P // A.dim
                for part, src in ((n % 2, hi_st), (1 - n % 2, lo_st)):
                    sp.dma_start(dst[c * per:(c + 1) * per, part, :, :], src[:, n % 2, :])\
                        .then_inc(A.s.qk_stored[n % 2], 16)

            for t in range(T):
                if t >= 2:
                    sp.wait_ge(s_mask, t - 1)
                sp.dma_start(adj_in[:, t % 2, :], adj[t * P:(t + 1) * P, :]).then_inc(s_adj[t % 2], 16)
                if t % 2 and t >= 3:
                    store_chunk(G, 0, (t - 3) // 2)
            for w, a in zip((fwq, fwk, fwv, fwo), (fW["Wq"], fW["Wk"], fW["Wv"], fW["Wo"])):
                sp.dma_start(w, a.rearrange("(c p) n -> p c n", p=P)).then_inc(s_fw, 16)
            sp.dma_start(bq_cols[:, :], fW["bq"].rearrange("(c p) -> p c", p=P), allow_slow_non_contiguous=True).then_inc(s_fw, 16)
            sp.dma_start(bk_cols[:, :], fW["bk"].rearrange("(c p) -> p c", p=P), allow_slow_non_contiguous=True).then_inc(s_fw, 16)

            def load_keys(A, h, p):
                d, k, q = A.dim, A.d.k[bass.ds(h, 1)], A.d.q[bass.ds(h, 1)]
                if A.masked:
                    pairs = [(A.ka[p][0:2 * d, :], k), (A.qa[p][0:d, :], q[:, 0]), (A.qa[p][d:2 * d, :], q[:, 0])]
                else:
                    pairs = [(A.ka[p][0:2 * d, :], k), (A.ka[p][2 * d:3 * d, :], k[:, 1]),
                             (A.qa[p][0:d, :], q[:, 0]), (A.qa[p][d:3 * d, :], q)]
                for dst, src in pairs:
                    src = src.rearrange("a s d n -> (a s d) n") if len(src.shape) == 4 else \
                        src.rearrange("a d n -> (a d) n")
                    sp.dma_start(dst, src).then_inc(A.s.loaded[p], 16)

            def load_rest(A, h, p, second=True, values=True):
                if A.masked and second:
                    for dst, src in ((A.kb[p], A.d.k), (A.qb[p], A.d.q)):
                        sp.dma_start(dst[0:A.dim, :], src[bass.ds(h, 1), 1].rearrange("a d n -> (a d) n"))\
                            .then_inc(A.s.rest[p], 16)
                if values:
                    sp.dma_start(A.v[p], A.d.v[:, :, bass.ds(h * A.dim, A.dim)]).then_inc(A.s.rest[p], 16)

            def load_gate_vectors():
                for dst, src in ((b2_rows, fW["b2"]), (b1_rows, fW["b1"].rearrange("e (c p) -> (e c) p", p=P)),
                                 (gate_w, fW["gate_W"].rearrange("(c p) e -> p c e", p=P)),
                                 (gate_b, fW["gate_b"].partition_broadcast(P))):
                    sp.dma_start(dst, src).then_inc(s_moe_w, 16)

            def store_group(A, i, p, qp):
                h = 2 * i + p
                sp.wait_ge(A.s.evac, i * 4 + (2 * p + qp + 3))
                for half in range(2):
                    rows = A.o[A.dim * half:A.dim * (half + 1), qp, :]
                    col = qp * GQ + half * BLOCK
                    sp.dma_start(A.d.o[bass.ds(h * A.dim, A.dim), col:col + BLOCK], rows)\
                        .then_inc(A.s.o_stored[qp], 16)

            def attention(A):
                for i in range(2):
                    sp.wait_ge(A.s.qk_stored[i], 32 * A.chunks)
                for h in range(2):
                    load_keys(A, h, h)
                    load_rest(A, h, h, values=False)
                for t in range(T):
                    sp.wait_ge(A.s.v_out, t + 1)
                    sp.dma_start(A.d.v[:, t, :], v_st[:, t % 2, 0:A.chunks * P]).then_inc(A.s.v_stored[t % 2], 16)
                for i in range(2):
                    sp.wait_ge(A.s.v_stored[i], 16 * T // 2)
                for h in range(2):
                    load_rest(A, h, h, second=False)
                if A is F:
                    load_gate_vectors()
                sp.wait_ge(A.s.drained, T * NB + 1)
                sp.dma_start(A.row[0].rearrange("a (t q) -> a t q", t=T), neg_top[:, :]).then_inc(A.s.row_in, 16)

                def heads(i, last):
                    for p in range(2):
                        store_group(A, i, p, 0)
                        if not (last and p == 1):
                            sp.wait_ge(A.s.drained, i * (2 * A.jobs) + (T * NB + 1 + p * A.jobs + A.top_job + 1))
                            sp.dma_start(A.row[1 - p].rearrange("a (t q) -> a t q", t=T), neg_top[:, :])\
                                .then_inc(A.s.row_in, 16)
                        if not last:
                            sp.wait_ge(A.s.pv, i * (2 * UNITS) + (RING + UNITS * (p + 1)))
                            load_keys(A, 2 * i + (2 + p), p)
                        store_group(A, i, p, 1)
                        if not last:
                            load_rest(A, 2 * i + (2 + p), p)

                with sp.Fori(0, PAIRS - 1) as i:
                    heads(i, False)
                heads(PAIRS - 1, True)
                for qp in range(2):
                    sp.wait_ge(A.s.o_stored[qp], 32 * (HEADS + 1))
                sp.dma_start(A.oT, A.d.o.rearrange("(c p) n -> p c n", p=P)).then_inc(A.s.o_in, 16)

            store_chunk(G, 0, 2 * G.chunks - 1)
            attention(G)
            sp.wait_ge(G.s.proj_used, T)
            for dst, src in ((bias_v, fW["bv"]), (bias_o, fW["bo"]), (ln_g, fW["ln1_g"]), (ln_b, fW["ln1_b"])):
                sp.dma_start(dst, src.partition_broadcast(P)).then_inc(s_fw, 16)
            for n in range(2 * F.chunks):
                store_chunk(F, D_GNN, n)
            attention(F)

            sp.wait_ge(s_placed, 16 * T)

            def load_sorted(j, p):
                sp.dma_start(sorted_in[:, p, :], sorted_d[bass.ds(j * P, P), :]).then_inc(s_sorted_in[p], 16)

            load_sorted(0, 0)
            load_sorted(1, 1)
            with sp.Fori(0, TILE_PAIRS - 1) as i:
                for p in range(2):
                    sp.wait_ge(s_sT, i * 2 + (p + 1))
                    load_sorted(2 * i + (2 + p), p)
            sp.wait_ge(s_sT, SLOTS - 2)
            load_sorted(SLOTS - 1, 0)
            for t in range(T):
                sp.wait_ge(s_res, t + 1)
                sp.dma_start(out[t * P:(t + 1) * P, :], res[:, t % 4, :]).then_inc(s_out[t % 4], 16)
            for i in range(4):
                sp.wait_ge(s_out[i], 4 * T)

        @block.gpsimd
        def _(pool):
            pool.memset(ident[:, :], 0.0).then_inc(s_const, 1)
            pool.memset(ones[:, :], 1.0).then_inc(s_const, 1)
            for s in (G.s, F.s):
                pool.sem_inc(s.exp, SCORE_SLOTS)
                pool.sem_inc(s.pv, RING)
                pool.sem_inc(s.summed, SUMS)
                pool.sem_inc(s.evac, 2)
                pool.sem_inc(s.o_stored[0], 32)
                pool.sem_inc(s.o_stored[1], 32)
            for s in s_y_stored:
                pool.sem_inc(s, 16)
            pool.sem_inc(s_hid, 4)
            pool.sem_inc(s_sT_out, 4)
            pool.sem_inc(s_up, 2)
            pool.sem_inc(s_gelu, 2)
            pool.sem_inc(s_down, 2)
            pool.sem_inc(s_y, 2)
            pool.memset(before[:, :], 1.0).then_inc(s_moe_const, 1)
            pool.memset(zero_tile, 0.0).then_inc(s_zero_in, 1)
            pool.iota(e_iota[:, :], [[-1, EXPERTS]], base=EXPERTS, channel_multiplier=0,
                      allow_small_or_imprecise_dtypes=True).then_inc(s_moe_const, 1)
            pool.iota(slot_iota[:, :], [[1, SLOTS]], base=0, channel_multiplier=0,
                      allow_small_or_imprecise_dtypes=True).then_inc(s_moe_const, 1)
            pool.wait_ge(s_moe_const, 3)
            pool.affine_select(out=before[:, :], in_=before[:, :], compare_op=ALU.is_gt, fill=0.0,
                               base=0, pattern=[[1, P]], channel_multiplier=-1).then_inc(s_moe_const, 1)
            pool.wait_ge(s_zero_in, 1)
            pool.dma_start(sorted_d.rearrange("(j p) d -> p j d", p=P),
                           zero_tile.unsqueeze(1).to_broadcast([P, SLOTS, D])).then_inc(s_zero, 16)
            pool.wait_ge(s_const, 1)
            pool.affine_select(out=ident[:, :], in_=ident[:, :], compare_op=ALU.not_equal, fill=1.0,
                               base=0, pattern=[[-1, P]], channel_multiplier=1).then_inc(s_const, 1)

            def add_probabilities(A):
                def heads(i):
                    for g in range(4):
                        for kt in range(1, SUM_TILES):
                            n = T * g + kt
                            if kt == 1:
                                pool.wait_ge(A.s.evac, i * 4 + (g + 1))
                            pool.wait_ge(A.s.exp, i * (4 * T) + (SCORE_SLOTS + n + 1))
                            total = A.sum[:, g % 2, :]
                            if kt == 1:
                                first = A.p[:, (n - 1) % RING, :]
                            else:
                                pool.wait_ge(A.s.summed, i * (4 * SUMS) + (SUMS * (g + 1) + kt - 1))
                                first = total
                            pool.tensor_tensor(total, first, A.p[:, n % RING, :], ALU.add).then_inc(A.s.summed, 1)
                with pool.Fori(0, PAIRS) as i:
                    heads(i)

            add_probabilities(G)
            def split_weights(first, src, hi, lo, width):
                for c in range(2 * EXPERTS):
                    n = first + c
                    if n >= 2:
                        pool.wait_ge(s_w_split, 2 * (n - 1))
                    pool.dma_start(w_in[:, n % 2, :].rearrange("p (a b) -> p a b", b=width), src(c))\
                        .then_inc(s_w_in[n % 2], 16)
                    if c:
                        split(n - 1, hi, lo, c - 1)
                split(first + 2 * EXPERTS - 1, hi, lo, 2 * EXPERTS - 1)

            def split(n, hi, lo, c):
                cols = slice(c * 1024, (c + 1) * 1024)
                pool.wait_ge(s_w_in[n % 2], 16 * (n // 2 + 1))
                pool.tensor_copy(hi[:, cols], w_in[:, n % 2, :]).then_inc(s_w_split, 1)
                pool.wait_ge(s_w_split, 2 * n + 1)
                pool.tensor_tensor(lo[:, cols], w_in[:, n % 2, :], hi[:, cols], ALU.subtract)\
                    .then_inc(s_w_split, 1)

            pool.wait_ge(G.s.proj_used, T)
            pool.wait_ge(s_zero, 16)
            split_weights(0, lambda c: fW["W1"][c // 2, (c % 2) * P:(c % 2 + 1) * P, :].unsqueeze(1),
                          w1h, w1l, FF)
            pool.wait_ge(F.s.v_full, T)
            for i in range(2):
                pool.wait_ge(F.s.v_stored[i], 8 * T)
            split_weights(2 * EXPERTS,
                          lambda c: fW["W2"][c // 2, (c % 2) * 512:(c % 2 + 1) * 512, :].rearrange(
                              "(c p) d -> p c d", p=P),
                          w2h, w2l, D)
            pool.wait_ge(s_route, ROUTE_ROWS)
            for t in range(T):
                pool.indirect_dma_start(
                    out=sorted_d, out_offset=bass.IndirectOffsetOnAxis(ap=slot_row[:, t:t + 1].bitcast(U32), axis=0),
                    in_=ts[:, t, :], in_offset=None).then_inc(s_placed, 16)

            pool.wait_ge(s_y_stored[0], 16 * (TILE_PAIRS + 2))
            pool.wait_ge(s_y_stored[1], 16 * (TILE_PAIRS + 1))
            for t in range(T):
                if t >= 4:
                    pool.wait_ge(s_res, t - 3)
                pool.indirect_dma_start(
                    out=y_in[:, t % 4, :], out_offset=None, in_=y_d,
                    in_offset=bass.IndirectOffsetOnAxis(ap=slot_row[:, t:t + 1].bitcast(U32), axis=0))\
                    .then_inc(s_y_in[t % 4], 16)

        @block.scalar
        def _(act):
            def root(A):
                act.wait_ge(A.s.ln, 2 * T + 1)
                nc.scalar.activation(std, veps, ACT.Sqrt).then_inc(A.s.sqrt, 1)

            def transposed_input(base):
                for u in range(XT):
                    act.wait_ge(s_mmA, base + u + 1)
                    nc.scalar.activation(nT[:, :, u * 256:(u + 1) * 256],
                                         ps[:, (base + u) % 4, :].rearrange("p (k n) -> p k n", k=KC),
                                         ACT.Copy).then_inc(s_evA, 1)

            def high_half(A, d_base, k):
                n, b, j = k // NB, k % NB, d_base + k
                if n >= 2 and b == 0:
                    act.wait_ge(A.s.qk_stored[n % 2], 32 * (n // 2))
                act.wait_ge(s_mmD, j + 1)
                bank, dst = ps[:, 4 + j % 4, :], hi_st[:, n % 2, b * BLOCK:(b + 1) * BLOCK]
                if A is F:
                    col = (bq_cols, bk_cols)[n % 2][:, n // 2:n // 2 + 1]
                    nc.scalar.activation(dst, bank, ACT.Identity, bias=col).then_inc(A.s.hi, 1)
                else:
                    nc.scalar.activation(dst, bank, ACT.Copy).then_inc(A.s.hi, 1)

            def values_out(A):
                width = A.chunks * P
                for t in range(T):
                    act.wait_ge(A.s.v_full, t + 1)
                    if t >= 2:
                        act.wait_ge(A.s.v_stored[t % 2], 16 * (t // 2))
                    nc.scalar.activation(v_st[:, t % 2, 0:width], ps[:, 4 + t % 2, 0:width], ACT.Copy)\
                        .then_inc(A.s.v_out, 1)

            def exps(A):
                def heads(i):
                    for n in range(2 * UNITS):
                        act.wait_ge(A.s.scores, i * (2 * UNITS) + (n + 1))
                        act.wait_ge(A.s.pv, i * (2 * UNITS) + (n + 1))
                        if A.masked:
                            m = n - RING
                            got = SUMS * (m // T) + min(max(m % T, 1), SUMS)
                            act.wait_ge(A.s.summed, i * (4 * SUMS) + (SUMS + got))
                        slot = 2 * (n % SCORE_SLOTS)
                        nc.scalar.activation(A.p[:, n % RING, :].rearrange("p (a b) -> p a b", a=2),
                                             ps[:, slot:slot + 2, :], ACT.Exp, scale=A.scale).then_inc(A.s.exp, 1)
                with act.Fori(0, PAIRS) as i:
                    heads(i)

            root(G)
            transposed_input(0)
            for t in range(T):
                for k in (2 * t, 2 * t + 1):
                    high_half(G, 0, k)
                for half in range(2):
                    j = XT + 2 * t + half
                    act.wait_ge(s_mmA, j + 1)
                    nc.scalar.activation(mask_cols[:, 8 * half:8 * half + 8, t * P:(t + 1) * P],
                                         ps[:, j % 4, :].bitcast(BF16).rearrange("p (a b) -> p a b", a=8),
                                         ACT.Copy, saturate=False).then_inc(s_evA, 1)
            values_out(G)
            exps(G)
            root(F)
            transposed_input(A_GNN)
            act.wait_ge(s_fw, 16 * 10)
            for k in range(FD_QK):
                high_half(F, D_GNN, k)
            values_out(F)
            exps(F)

            act.wait_ge(s_ln2, 2 * T + 1)
            nc.scalar.activation(std, veps, ACT.Sqrt).then_inc(s_sqrt2, 1)
            for t in range(T):
                act.wait_ge(s_hT, t + 1)
                if t >= 2:
                    act.wait_ge(s_lg, t - 1)
                nc.scalar.activation(tT[:, t % 2, :, :], ps[:, t % 2, 0:D].rearrange("p (k n) -> p k n", k=KC),
                                     ACT.Copy).then_inc(s_tT, 1)
            act.wait_ge(s_b1, 1)
            nc.scalar.activation(b1_cols[:, :], ps[:, 4, 0:EXPERTS * FC], ACT.Copy).then_inc(s_b1_out, 1)
            act.wait_ge(s_route, ROUTE_EXP)
            nc.scalar.activation(choice, choice, ACT.Exp).then_inc(s_route_exp, 1)
            act.wait_ge(s_turn8, 1)
            act.wait_ge(s_placed, 16 * T)
            nc.scalar.activation(one_hot_T.rearrange("e (a t) n -> e a (t n)", a=4), ps[0:EXPERTS, 0:4, :],
                                 ACT.Copy).then_inc(s_turn8_out, 1)

            def gelus(p, n):
                act.wait_ge(s_up, n + 3)
                act.wait_ge(s_b1_tile, n + 1)
                act.wait_ge(s_hid, n * 2 + 2)
                for c in range(FC):
                    m = nc.scalar.activation(
                        hid[:, p, c, :], ps[:, 2 * p + c // 4, (c % 4) * P:(c % 4 + 1) * P],
                        ACT.Gelu_apprx_tanh, bias=b1_tile[:, p, c:c + 1])
                m.then_inc(s_gelu, 1)

            def store_expert(p, j):
                act.wait_ge(s_y, j + 3)
                act.dma_start(y_d[bass.ds(j * P, P), :], y_out[:, p, :]).then_inc(s_y_stored[p], 16)

            gelus(0, 0)
            gelus(1, 1)
            with act.Fori(0, TILE_PAIRS - 1) as i:
                for p in range(2):
                    gelus(p, 2 * i + (2 + p))
                    store_expert(p, 2 * i + p)
            gelus(0, SLOTS - 1)
            for j in range(SLOTS - 3, SLOTS):
                store_expert(j % 2, j)

        @block.tensor
        def _(pe):
            pe.wait_ge(s_const2, 3)

            def transpose_input(A, base):
                for u in range(XT):
                    j = base + u
                    if j >= 4:
                        pe.wait_ge(s_evA, j - 3)
                    pe.wait_ge(A.s.nx, 2 * u + 2)
                    for k in range(KC):
                        for t in range(2):
                            m = pe.transpose(ps[:, j % 4, k * 256 + t * P:k * 256 + (t + 1) * P],
                                             nx[:, (2 * u + t) % 4, k * P:(k + 1) * P], ident[:, :])
                    m.then_inc(s_mmA, 1)

            def project(A, d_base, k):
                n, b, j = k // NB, k % NB, d_base + k
                w, c = (A.wq, A.wk)[n % 2], n // 2
                if j >= 4:
                    pe.wait_ge(s_evD, j - 3)
                for kc in range(KC):
                    m = pe.matmul(ps[:, 4 + j % 4, :], w[:, kc, c * P:(c + 1) * P],
                                  nT[:, kc, b * BLOCK:(b + 1) * BLOCK], start=kc == 0, stop=kc == KC - 1)
                m.then_inc(s_mmD, 1)

            def project_values(A, t):
                if t >= 2:
                    pe.wait_ge(A.s.v_out, t - 1)
                bank = ps[:, 4 + t % 2, 0:A.chunks * P]
                for kc in range(KC):
                    m = pe.matmul(bank, nT[:, kc, t * P:(t + 1) * P], A.wv[:, kc, :],
                                  start=kc == 0, stop=kc == KC - 1 and A is G)
                if A is F:
                    m = pe.matmul(bank, ones[0:1, :], bias_v[0:1, :], start=False, stop=True)
                m.then_inc(A.s.v_full, 1)

            def attention(A):
                def max_block(p, u, job, value):
                    if value is not None:
                        pe.wait_ge(A.s.drained, value)
                    qt, mb = u // NB, u % NB
                    pe.matmul(ps[:, 6 + job % 2, :], A.qa[p][0:A.max_rows, qt * P:(qt + 1) * P],
                              A.ka[p][0:A.max_rows, mb * BLOCK:(mb + 1) * BLOCK],
                              start=True, stop=True).then_inc(A.s.job, 1)

                def turn_maxima(job, drained, tops):
                    pe.wait_ge(A.s.drained, drained)
                    pe.wait_ge(A.s.top, tops)
                    pe.transpose(ps[0:T, 6 + job % 2, 0:P], top[:, :], ident[:, :]).then_inc(A.s.job, 1)

                pe.wait_ge(A.s.loaded[0], 16 * A.loads)
                for u in range(T * NB):
                    if u % NB == 0:
                        project_values(A, u // NB)
                    max_block(0, u, u, u - 1 if u >= 2 else None)
                pe.wait_ge(A.s.v_out, T)
                turn_maxima(T * NB, T * NB - 1, 1)
                pe.wait_ge(A.s.ones_row, 2)
                first = T * NB + 1

                def heads(i, last):
                    job = first
                    for p in range(2):
                        final = last and p == 1
                        pe.wait_ge(A.s.row_in, i * 32 + 16 * (p + 1))
                        pe.wait_ge(A.s.rest[p], i * (16 * A.rests) + 16 * A.rests)

                        def scores(j):
                            n = UNITS * p + j
                            qp, kt = j // T, j % T
                            pe.wait_ge(A.s.exp, i * (2 * UNITS) + (n + 1))
                            keys = slice(kt * P, (kt + 1) * P)
                            for half in range(2):
                                next_max()
                                bank = ps[:, 2 * (n % SCORE_SLOTS) + half, :]
                                cols = slice(qp * GQ + half * BLOCK, qp * GQ + (half + 1) * BLOCK)
                                if A.masked:
                                    pe.matmul(bank, A.ka[p][:, keys], A.qa[p][:, cols], start=True, stop=False)
                                    pe.matmul(bank, identb[:, :], mask_cols[:, kt, cols], start=False, stop=False)
                                    m = pe.matmul(bank, A.kb[p][:, keys], A.qb[p][:, cols], start=False, stop=True)
                                else:
                                    m = pe.matmul(bank, A.ka[p][:, keys], A.qa[p][:, cols], start=True, stop=True)
                            m.then_inc(A.s.scores, 1)

                        def values(j):
                            nonlocal job
                            n = UNITS * p + j
                            g, kt = 2 * p + j // T, j % T
                            if kt == 0:
                                pe.wait_ge(A.s.evac, i * 4 + (g + 1))
                            pe.wait_ge(A.s.exp, i * (2 * UNITS) + (n + SCORE_SLOTS + 1))
                            acc = ps[:, 4 + g % 2, :]
                            first_kt, last_kt = kt == 0, kt == T - 1
                            for half in range(2):
                                pr = A.p[:, n % RING, half * BLOCK:(half + 1) * BLOCK]
                                m = pe.matmul(acc[A.dim * half:A.dim * (half + 1), :], A.v[p][:, kt, :], pr,
                                              start=first_kt, stop=last_kt)
                                if not A.masked:
                                    m = pe.matmul(acc[64 + 32 * half:96 + 32 * half, :], ones[:, 0:32], pr,
                                                  start=first_kt, stop=last_kt)
                            if A.masked and kt >= SUM_TILES:
                                if kt == SUM_TILES:
                                    pe.wait_ge(A.s.drained, i * (2 * A.jobs) + (job - 1))
                                den = ps[:, 6 + job % 2, :]
                                for half in range(2):
                                    m = pe.matmul(den[64 * half:64 * half + 64, :], ones[:, 0:64],
                                                  A.p[:, n % RING, half * BLOCK:(half + 1) * BLOCK],
                                                  start=kt == SUM_TILES, stop=False)
                            m.then_inc(A.s.pv, 1)
                            if A.masked and last_kt:
                                pe.wait_ge(A.s.summed, i * (4 * SUMS) + SUMS * (g + 2))
                                for half in range(2):
                                    m = pe.matmul(den[64 * half:64 * half + 64, :], ones[:, 0:64],
                                                  A.sum[:, g % 2, half * BLOCK:(half + 1) * BLOCK],
                                                  start=False, stop=True)
                                m.then_inc(A.s.job, 1)
                                job += 1

                        def next_max():
                            nonlocal job
                            if left:
                                max_block(1 - p, left.pop(0), job, i * (2 * A.jobs) + (job - 1))
                                job += 1

                        for j in range(UNITS):
                            left = [] if final else list(max_units(A, j))
                            if left and left[0] == 0:
                                pe.wait_ge(A.s.loaded[1 - p], i * (16 * A.loads) + 16 * A.loads * (p + 1))
                            scores(j)
                            while left:
                                next_max()
                            if not final:
                                if j == TOP_STEP:
                                    turn_maxima(job, i * (2 * A.jobs) + (job - 1), i * 2 + (p + 2))
                                    job += 1
                            if j >= 1:
                                values(j - 1)
                        values(UNITS - 1)

                with pe.Fori(0, PAIRS - 1) as i:
                    heads(i, False)
                heads(PAIRS - 1, True)

            def output_projection(A, wo):
                pe.wait_ge(A.s.o_in, 16)
                for t in range(T):
                    if t >= 2:
                        pe.wait_ge(A.s.proj_used, t - 1)
                    for c in range(A.chunks):
                        m = pe.matmul(ps[:, 6 + t % 2, 0:D], A.oT[:, c, t * P:(t + 1) * P], wo[:, c, :],
                                      start=c == 0, stop=c == A.chunks - 1)
                    m.then_inc(A.s.proj, 1)

            transpose_input(G, 0)
            pe.wait_ge(s_w, 16 * 7)
            pe.wait_ge(s_evA, XT)
            for t in range(T):
                for k in (2 * t, 2 * t + 1):
                    project(G, 0, k)
                pe.wait_ge(s_mask, t + 1)
                for half in range(2):
                    j = XT + 2 * t + half
                    pe.wait_ge(s_evA, j - 3)
                    for m8 in range(8):
                        m = pe.transpose(ps[:, j % 4, :].bitcast(BF16)[:, m8 * P:(m8 + 1) * P],
                                         mask_rows[:, t, (8 * half + m8) * P:(8 * half + m8 + 1) * P], identt[:, :])
                    m.then_inc(s_mmA, 1)
            pe.wait_ge(s_evA, A_GNN)
            pe.wait_ge(s_evD, D_GNN)
            attention(G)
            pe.wait_ge(G.s.drained, T * NB + 1 + 3 * 2 * G.jobs + G.jobs + 2)
            output_projection(G, gwo)
            transpose_input(F, A_GNN)
            pe.wait_ge(s_fw, 16 * 10)
            pe.wait_ge(s_evA, A_ALL)
            for k in range(FD_QK):
                project(F, D_GNN, k)
            pe.wait_ge(s_evD, D_GNN + FD_QK)
            attention(F)
            pe.wait_ge(F.s.drained, T * NB + 1 + 3 * 2 * F.jobs + F.jobs)
            output_projection(F, fwo)
            pe.wait_ge(s_moe_w, 16 * 4)

            def logits(t):
                pe.wait_ge(s_tT, t + 1)
                if t >= 2:
                    pe.wait_ge(s_lg_out, t - 1)
                for k in range(KC):
                    m = pe.matmul(ps[:, 2 + t % 2, 0:EXPERTS], tT[:, t % 2, k, :], gate_w[:, k, :],
                                  start=k == 0, stop=k == KC - 1)
                m.then_inc(s_lg, 1)

            for t in range(T):
                pe.wait_ge(s_h, t + 1)
                if t >= 2:
                    pe.wait_ge(s_tT, t - 1)
                for k in range(KC):
                    m = pe.transpose(ps[:, t % 2, k * P:(k + 1) * P], ts[:, t, k * P:(k + 1) * P], ident[:, :])
                m.then_inc(s_hT, 1)
                if t >= 1:
                    logits(t - 1)
            logits(T - 1)
            pe.transpose(ps[:, 4, 0:EXPERTS * FC], b1_rows, ident[0:EXPERTS * FC, 0:EXPERTS * FC]).then_inc(s_b1, 1)
            pe.wait_ge(s_route, ROUTE_ONE_HOT)
            flat = one_hot.rearrange("p t e -> p (t e)")
            pe.matmul(ps[:, 5, 0:P], before[:, :], flat, start=True, stop=True).then_inc(s_prefix, 1)
            pe.matmul(ps[:, 6, 0:P], ones[:, :], flat, start=True, stop=True).then_inc(s_prefix, 1)
            pe.wait_ge(s_lg_out, T)
            for t in range(T):
                m = pe.transpose(ps[0:EXPERTS, t // 4, (t % 4) * P:(t % 4 + 1) * P], one_hot[:, t, :], ident[:, :])
            m.then_inc(s_turn8, 1)

            def turn(p, j):
                pe.wait_ge(s_sorted_in[p], (j - p) * 8 + 16)
                pe.wait_ge(s_sT_out, j * 2 + 2)
                for k in range(KC):
                    m = pe.transpose(ps[:, 6 + p, k * P:(k + 1) * P], sorted_in[:, p, k * P:(k + 1) * P], ident[:, :])
                m.then_inc(s_sT, 1)

            def up(p, j):
                expert = pe.value_load(slot_expert[0:1, bass.ds(j, 1)], min_val=0, max_val=EXPERTS - 1)
                pe.wait_ge(s_sT_out, j * 2 + 6)
                pe.wait_ge(s_gelu, j + 1)
                for c in range(FC):
                    bank = ps[:, 2 * p + c // 4, (c % 4) * P:(c % 4 + 1) * P]
                    for k in range(KC):
                        cols = bass.ds(expert * (KC * FF) + (k * FF + c * P), P)
                        pe.matmul(bank, w1h[:, cols], sTh[:, p, k, :], start=k == 0, stop=False)
                        pe.matmul(bank, w1h[:, cols], sTl[:, p, k, :], start=False, stop=False)
                        m = pe.matmul(bank, w1l[:, cols], sTh[:, p, k, :], start=False, stop=k == KC - 1)
                m.then_inc(s_up, 1)

            def down(p, j):
                expert = pe.value_load(slot_expert[0:1, bass.ds(j, 1)], min_val=0, max_val=EXPERTS - 1)
                pe.wait_ge(s_hid, j * 2 + 6)
                pe.wait_ge(s_y, j + 1)
                bank = ps[:, 4 + p, 0:D]
                for c in range(FC):
                    cols = bass.ds(expert * (FC * D) + c * D, D)
                    pe.matmul(bank, hid_h[:, p, c, :], w2h[:, cols], start=c == 0, stop=False)
                    pe.matmul(bank, hid_l[:, p, c, :], w2h[:, cols], start=False, stop=False)
                    m = pe.matmul(bank, hid_h[:, p, c, :], w2l[:, cols], start=False, stop=c == FC - 1)
                m.then_inc(s_down, 1)

            pe.wait_ge(s_turn8_out, 1)
            pe.wait_ge(s_b1_out, 1)
            pe.wait_ge(s_route, ROUTE_DONE)
            pe.wait_ge(s_w_split, 2 * 4 * EXPERTS)
            turn(0, 0)
            turn(1, 1)
            up(0, 0)
            with pe.Fori(0, TILE_PAIRS - 1) as i:
                turn(0, 2 * i + 2)
                up(1, 2 * i + 1)
                down(0, 2 * i)
                turn(1, 2 * i + 3)
                up(0, 2 * i + 2)
                down(1, 2 * i + 1)
            turn(0, SLOTS - 1)
            up(1, SLOTS - 2)
            down(0, SLOTS - 3)
            up(0, SLOTS - 1)
            down(1, SLOTS - 2)
            down(0, SLOTS - 1)
            pe.wait_ge(s_sT_out, 2 * SLOTS + 4)
            for t in range(T):
                if t >= 2:
                    pe.wait_ge(s_sum, t - 1)
                pe.matmul(ps[:, 6 + t % 2, 0:D], one_hot_T[:, t, :], b2_rows, start=True, stop=True)\
                    .then_inc(s_b2, 1)

        @block.vector
        def _(dve):
            dve.wait_ge(s_const, 3)
            nc.vector.tensor_scalar(identb[:, :], ident[:, :], MASKED, None, ALU.mult).then_inc(s_const2, 1)
            nc.vector.tensor_copy(identt[:, :], ident[:, :]).then_inc(s_const2, 1)
            nc.vector.memset(amax[:, :, :], 0.0).then_inc(s_const2, 1)

            def layer_norm(A):
                n = [0]

                def link(ins):
                    ins.then_inc(A.s.ln, 1)
                    n[0] += 1
                    dve.wait_ge(A.s.ln, n[0])

                for t in range(T):
                    if A is G and t % 8 == 0:
                        dve.wait_ge(s_x[t // 8], 16)
                    if A is F:
                        dve.wait_ge(G.s.proj_used, t + 1)
                    nc.vector.bn_stats(stats[:, t, :], xs[:, t, :]).then_inc(A.s.ln, 1)
                n[0] += T
                dve.wait_ge(A.s.ln, n[0])
                for t in range(T):
                    nc.vector.bn_aggr(mv[:, t, :], stats[:, t, :]).then_inc(A.s.ln, 1)
                n[0] += T
                dve.wait_ge(A.s.ln, n[0])
                link(nc.vector.tensor_scalar(veps, mv[:, :, 1], EPS, None, ALU.add))
                dve.wait_ge(A.s.sqrt, 1)
                link(nc.vector.reciprocal(rstd, std))
                link(nc.vector.tensor_tensor(tmp, rstd, rstd, ALU.mult))
                link(nc.vector.tensor_tensor(tmp, tmp, veps, ALU.mult))
                link(nc.vector.tensor_scalar(tmp, tmp, -0.5, 1.5, ALU.mult, ALU.add))
                link(nc.vector.tensor_tensor(rstd, rstd, tmp, ALU.mult))
                base = 0 if A is G else A_GNN
                for t in range(T):
                    if t >= 4:
                        dve.wait_ge(s_mmA, base + (t - 4) // 2 + 1)
                    nc.vector.tensor_scalar(nx[:, t % 4, :], xs[:, t, :], mv[:, t, 0:1], rstd[:, t:t + 1],
                                            ALU.subtract, ALU.mult).then_inc(A.s.nx, 1)

            def low_half(A, d_base, k):
                n, b, j = k // NB, k % NB, d_base + k
                if n >= 2 and b == 0:
                    dve.wait_ge(A.s.qk_stored[n % 2], 32 * (n // 2))
                dve.wait_ge(s_mmD, j + 1)
                dve.wait_ge(A.s.hi, k + 1)
                cols = slice(b * BLOCK, (b + 1) * BLOCK)
                bank, hi, lo = ps[:, 4 + j % 4, :], hi_st[:, n % 2, cols], lo_st[:, n % 2, cols]
                if A is F:
                    col = (bq_cols, bk_cols)[n % 2][:, n // 2:n // 2 + 1]
                    nc.vector.scalar_tensor_tensor(out=lo, in0=bank, scalar=col, in1=hi, op0=ALU.add,
                                                   op1=ALU.subtract).then_inc(s_evD, 1)
                else:
                    nc.vector.tensor_tensor(lo, bank, hi, ALU.subtract).then_inc(s_evD, 1)

            def attention(A):
                def block_max(u, job, value):
                    qt, mb = u // NB, u % NB
                    dve.wait_ge(A.s.job, value)
                    bank = ps[:, 6 + job % 2, :]
                    if A.masked:
                        nc.vector.tensor_tensor_reduce(
                            out=A.junk[:, u % 2, :], in0=bank, in1=mask_rows[:, qt, mb * BLOCK:(mb + 1) * BLOCK],
                            scale=1.0, scalar=-3e38, op0=ALU.add, op1=ALU.max,
                            accum_out=amax[:, qt, mb:mb + 1]).wait_op(s_mask_scaled, T, "sem-ge")\
                            .then_inc(A.s.drained, 1)
                    else:
                        nc.vector.tensor_reduce(amax[:, qt, mb:mb + 1], bank, AX.X, ALU.max)\
                            .then_inc(A.s.drained, 1)

                def head_max(drained):
                    dve.wait_ge(A.s.drained, drained)
                    nc.vector.tensor_reduce(top[:, :], amax[:, :, :], AX.X, ALU.max).then_inc(A.s.top, 1)

                def negate(job, value, row_in):
                    dve.wait_ge(A.s.job, value)
                    if row_in is not None:
                        dve.wait_ge(A.s.row_in, row_in)
                    nc.vector.tensor_scalar(neg_top[:, :], ps[0:T, 6 + job % 2, 0:P], -1.0, None, ALU.mult)\
                        .then_inc(A.s.drained, 1)

                for u in range(T * NB):
                    block_max(u, u, u + 1)
                head_max(T * NB)
                for i in range(2):
                    dve.wait_ge(A.s.qk_stored[i], 32 * A.chunks)
                for i in range(2):
                    nc.vector.memset(A.ones_row[i], 1.0).then_inc(A.s.ones_row, 1)
                negate(T * NB, T * NB + 1, None)
                first = T * NB + 1

                def heads(i, last):
                    job = first
                    for p in range(2):
                        final = last and p == 1

                        def group_out(qp):
                            nonlocal job
                            g = 2 * p + qp
                            acc, o = ps[:, 4 + g % 2, :], A.o[:, qp, :]
                            if A.masked:
                                dve.wait_ge(A.s.job, i * (2 * A.jobs) + (job + 1))
                                dve.wait_ge(A.s.evac, i * 4 + (g + 2))
                                nc.vector.reciprocal(A.r, ps[:, 6 + job % 2, :]).then_inc(A.s.drained, 1)
                                job += 1
                                dve.wait_ge(A.s.drained, i * (2 * A.jobs) + job)
                                dve.wait_ge(A.s.pv, i * (2 * UNITS) + (RING + T * (g + 1)))
                                dve.wait_ge(A.s.o_stored[qp], i * 64 + 32 * (p + 1))
                                nc.vector.tensor_tensor(o, acc, A.r, ALU.mult).then_inc(A.s.evac, 1)
                            else:
                                dve.wait_ge(A.s.pv, i * (2 * UNITS) + (RING + T * (g + 1)))
                                dve.wait_ge(A.s.evac, i * 4 + (g + 2))
                                nc.vector.reciprocal(A.r[0:64, :], acc[64:128, :]).then_inc(A.s.evac_step, 1)
                                dve.wait_ge(A.s.evac_step, i * 4 + (g + 1))
                                dve.wait_ge(A.s.o_stored[qp], i * 64 + 32 * (p + 1))
                                nc.vector.tensor_tensor(o[0:64, :], acc[0:64, :], A.r[0:64, :], ALU.mult)\
                                    .then_inc(A.s.evac, 1)

                        for j in range(UNITS):
                            if not final:
                                for u in max_units(A, j):
                                    block_max(u, job, i * (2 * A.jobs) + (job + 1))
                                    job += 1
                                    if u == T * NB - 1:
                                        head_max(i * (2 * A.jobs) + job)
                                if j == TOP_STEP:
                                    negate(job, i * (2 * A.jobs) + (job + 1), i * 32 + 16 * (p + 1))
                                    job += 1
                            if j == T:
                                group_out(0)
                        group_out(1)

                with dve.Fori(0, PAIRS - 1) as i:
                    heads(i, False)
                heads(PAIRS - 1, True)

            layer_norm(G)
            def scale_mask(t):
                dve.wait_ge(s_mmA, XT + 2 * t + 2)
                nc.vector.tensor_scalar(mask_rows[:, t, :], mask_rows[:, t, :], MASKED, None, ALU.mult)\
                    .then_inc(s_mask_scaled, 1)

            for t in range(T):
                dve.wait_ge(s_adj[t % 2], 16 * (t // 2 + 1))
                diag = adj_in[:, t % 2, t * P:(t + 1) * P]
                nc.vector.tensor_tensor(diag, diag, ident[:, :], ALU.max).then_inc(s_adj_diag, 1)
                dve.wait_ge(s_adj_diag, t + 1)
                nc.vector.tensor_scalar(mask_rows[:, t, :], adj_in[:, t % 2, :], -1.0, None, ALU.add)\
                    .then_inc(s_mask, 1)
                for k in (2 * t, 2 * t + 1):
                    low_half(G, 0, k)
                if t >= 1:
                    scale_mask(t - 1)
            scale_mask(T - 1)
            attention(G)
            for t in range(T):
                dve.wait_ge(G.s.proj, t + 1)
                nc.vector.tensor_tensor(xs[:, t, :], ps[:, 6 + t % 2, 0:D], xs[:, t, :], ALU.add)\
                    .then_inc(G.s.proj_used, 1)
            layer_norm(F)
            dve.wait_ge(s_fw, 16 * 10)
            for k in range(FD_QK):
                low_half(F, D_GNN, k)
            attention(F)

            for t in range(T):
                dve.wait_ge(F.s.proj, t + 1)
                nc.vector.tensor_scalar(xn[:, t % 2, :], xs[:, t, :], mv[:, t, 0:1], rstd[:, t:t + 1],
                                        ALU.subtract, ALU.mult).then_inc(s_hsum, 1)
                dve.wait_ge(s_hsum, 2 * t + 1)
                nc.vector.tensor_tensor(xn[:, t % 2, :], xn[:, t % 2, :], bias_o, ALU.add).then_inc(s_hsum, 1)
                dve.wait_ge(s_hsum, 2 * t + 2)
                nc.vector.tensor_tensor(ts[:, t, :], ps[:, 6 + t % 2, 0:D], xn[:, t % 2, :], ALU.add)\
                    .then_inc(F.s.proj_used, 1)
            n = [0]

            def link2(ins):
                ins.then_inc(s_ln2, 1)
                n[0] += 1
                dve.wait_ge(s_ln2, n[0])

            for t in range(T):
                dve.wait_ge(F.s.proj_used, t + 1)
                nc.vector.bn_stats(stats[:, t, :], ts[:, t, :]).then_inc(s_ln2, 1)
            n[0] += T
            dve.wait_ge(s_ln2, n[0])
            for t in range(T):
                nc.vector.bn_aggr(mv2[:, t, :], stats[:, t, :]).then_inc(s_ln2, 1)
            n[0] += T
            dve.wait_ge(s_ln2, n[0])
            link2(nc.vector.tensor_scalar(veps, mv2[:, :, 1], EPS, None, ALU.add))
            dve.wait_ge(s_sqrt2, 1)
            link2(nc.vector.reciprocal(rstd, std))
            link2(nc.vector.tensor_tensor(tmp, rstd, rstd, ALU.mult))
            link2(nc.vector.tensor_tensor(tmp, tmp, veps, ALU.mult))
            link2(nc.vector.tensor_scalar(tmp, tmp, -0.5, 1.5, ALU.mult, ALU.add))
            link2(nc.vector.tensor_tensor(rstd, rstd, tmp, ALU.mult))
            for t in range(T):
                link2(nc.vector.scalar_tensor_tensor(out=ts[:, t, :], in0=ts[:, t, :], scalar=mv2[:, t, 0:1],
                                                     in1=ln_g, op0=ALU.subtract, op1=ALU.mult))
                nc.vector.scalar_tensor_tensor(out=ts[:, t, :], in0=ts[:, t, :], scalar=rstd[:, t:t + 1],
                                               in1=ln_b, op0=ALU.mult, op1=ALU.add).then_inc(s_h, 1)
            for t in range(T):
                dve.wait_ge(s_lg, t + 1)
                nc.vector.tensor_tensor(logits[:, t, :], ps[:, 2 + t % 2, 0:EXPERTS], gate_b, ALU.add)\
                    .then_inc(s_lg_out, 1)
            dve.wait_ge(s_lg_out, T)

            r = [0]

            def link(ins):
                ins.then_inc(s_route, 1)
                r[0] += 1
                dve.wait_ge(s_route, r[0])

            def wide(a):
                return a.unsqueeze(2).to_broadcast([P, T, EXPERTS])

            def tiles(a, n):
                return a.unsqueeze(1).to_broadcast([P, n, EXPERTS])

            link(nc.vector.tensor_reduce(tmp, logits, AX.X, ALU.max))
            link(nc.vector.tensor_tensor(choice, logits, wide(tmp), ALU.subtract))
            assert r[0] == ROUTE_EXP
            link(nc.vector.tensor_tensor(one_hot, logits, wide(tmp), ALU.is_equal))
            link(nc.vector.tensor_tensor(one_hot, one_hot, tiles(e_iota[:, :], T), ALU.mult))
            link(nc.vector.tensor_reduce(tmp, one_hot, AX.X, ALU.max))
            link(nc.vector.tensor_tensor(one_hot, one_hot, wide(tmp), ALU.is_equal))
            assert r[0] == ROUTE_ONE_HOT
            dve.wait_ge(s_route_exp, 1)
            link(nc.vector.tensor_reduce(tmp, choice, AX.X, ALU.add))
            link(nc.vector.reciprocal(gate[:, :], tmp))
            dve.wait_ge(s_prefix, 2)
            link(nc.vector.tensor_copy(totals, ps[:, 6, 0:P].rearrange("p (t e) -> p t e", t=T)))
            src, dst = totals, run0
            for step in (1, 2, 4, 8):
                link(nc.vector.tensor_copy(dst[:, 0:step, :], src[:, 0:step, :]))
                link(nc.vector.tensor_tensor(dst[:, step:T, :], src[:, step:T, :], src[:, 0:T - step, :], ALU.add))
                src, dst = dst, (run1 if dst is run0 else run0)
            link(nc.vector.tensor_tensor(place, src, totals, ALU.subtract))
            link(nc.vector.tensor_tensor(rank, ps[:, 5, 0:P].rearrange("p (t e) -> p t e", t=T), place, ALU.add))
            link(nc.vector.tensor_scalar(counts[:, 0, :], src[:, T - 1, :], float(P - 1), None, ALU.add))
            link(nc.vector.tensor_copy(counts_i[:, :], counts[:, 0, :]))
            link(nc.vector.tensor_scalar(counts_i[:, :], counts_i[:, :], P.bit_length() - 1, None,
                                         ALU.logical_shift_right))
            link(nc.vector.tensor_copy(counts[:, 0, :], counts_i[:, :]))
            for step, a, b in ((1, 0, 1), (2, 1, 2), (4, 2, 1)):
                link(nc.vector.tensor_copy(counts[:, b, 0:step], counts[:, a, 0:step]))
                link(nc.vector.tensor_tensor(counts[:, b, step:EXPERTS], counts[:, a, step:EXPERTS],
                                             counts[:, a, 0:EXPERTS - step], ALU.add))
            link(nc.vector.tensor_tensor(counts[:, 2, :], counts[:, 1, :], counts[:, 0, :], ALU.subtract))
            link(nc.vector.tensor_scalar(counts[:, 2, :], counts[:, 2, :], float(P), None, ALU.mult))
            link(nc.vector.tensor_tensor(rank, rank, tiles(counts[:, 2, :], T), ALU.add))
            link(nc.vector.tensor_tensor(rank, rank, one_hot, ALU.mult))
            link(nc.vector.tensor_reduce(tmp, rank, AX.X, ALU.add))
            link(nc.vector.tensor_copy(slot_row[:, :], tmp))
            assert r[0] == ROUTE_ROWS, r[0]
            link(nc.vector.tensor_tensor(slot_of, tiles(counts[:, 1, :], SLOTS),
                                         slot_iota[:, :].unsqueeze(2).to_broadcast([P, SLOTS, EXPERTS]), ALU.is_le))
            link(nc.vector.tensor_reduce(slot_expert_f[:, :], slot_of, AX.X, ALU.add))
            link(nc.vector.tensor_scalar(slot_expert_f[:, :], slot_expert_f[:, :], float(EXPERTS - 1), None, ALU.min))
            link(nc.vector.tensor_copy(slot_expert[:, :], slot_expert_f[:, :]))
            assert r[0] == ROUTE_DONE, r[0]

            dve.wait_ge(s_b1_out, 1)
            dve.wait_ge(s_placed, 16 * T)

            def split_input(p, j):
                dve.wait_ge(s_sT, j + 1)
                dve.wait_ge(s_up, j + 1)
                bank = ps[:, 6 + p, 0:D].rearrange("p (k n) -> p k n", k=KC)
                nc.vector.tensor_copy(sTh[:, p, :, :], bank).then_inc(s_sT_out, 1)
                dve.wait_ge(s_sT_out, j * 2 + 5)
                nc.vector.tensor_tensor(sTl[:, p, :, :], bank, sTh[:, p, :, :], ALU.subtract).then_inc(s_sT_out, 1)

            def first_bias(p, j):
                expert = dve.value_load(slot_expert[0:1, bass.ds(j, 1)], min_val=0, max_val=EXPERTS - 1)
                dve.wait_ge(s_gelu, j + 1)
                nc.vector.tensor_copy(b1_tile[:, p, :], b1_cols[:, bass.ds(expert * FC, FC)]).then_inc(s_b1_tile, 1)

            def split_hidden(p, j):
                dve.wait_ge(s_gelu, j + 3)
                dve.wait_ge(s_down, j + 1)
                nc.vector.tensor_copy(hid_h[:, p, :, :], hid[:, p, :, :]).then_inc(s_hid, 1)
                dve.wait_ge(s_hid, j * 2 + 5)
                nc.vector.tensor_tensor(hid_l[:, p, :, :], hid[:, p, :, :], hid_h[:, p, :, :], ALU.subtract)\
                    .then_inc(s_hid, 1)

            def expert_out(p, j):
                dve.wait_ge(s_down, j + 3)
                dve.wait_ge(s_y_stored[p], (j - p) * 8 + 16)
                nc.vector.tensor_copy(y_out[:, p, :], ps[:, 4 + p, 0:D]).then_inc(s_y, 1)

            def tile(p, j, more):
                if more:
                    split_input(p, j + 2)
                first_bias(1 - p, j + 1)
                split_hidden(p, j)
                expert_out(p, j)

            first_bias(0, 0)
            split_input(0, 0)
            split_input(1, 1)
            with dve.Fori(0, TILE_PAIRS - 1) as i:
                for p in range(2):
                    tile(p, 2 * i + p, True)
            tile(0, SLOTS - 3, True)
            tile(1, SLOTS - 2, False)
            split_hidden(0, SLOTS - 1)
            expert_out(0, SLOTS - 1)
            for t in range(T):
                dve.wait_ge(s_y_in[t % 4], 16 * (t // 4 + 1))
                dve.wait_ge(s_b2, t + 1)
                nc.vector.tensor_tensor(y_in[:, t % 4, :], ps[:, 6 + t % 2, 0:D], y_in[:, t % 4, :], ALU.add)\
                    .then_inc(s_sum, 1)
                dve.wait_ge(s_sum, t + 1)
                if t >= 4:
                    dve.wait_ge(s_out[t % 4], 16 * (t // 4))
                nc.vector.scalar_tensor_tensor(out=res[:, t % 4, :], in0=y_in[:, t % 4, :], scalar=gate[:, t:t + 1],
                                               in1=xs[:, t, :], op0=ALU.mult, op1=ALU.add).then_inc(s_res, 1)


_INS = ['x', 'adj', 'L0_gnn_Wks', 'L0_gnn_Wqs', 'L0_gnn_Wvs', 'L0_gnn_Wo', 'L0_ffn_ln1_g', 'L0_ffn_ln1_b',
        'L0_ffn_Wq', 'L0_ffn_bq', 'L0_ffn_Wk', 'L0_ffn_bk', 'L0_ffn_Wv', 'L0_ffn_bv', 'L0_ffn_Wo', 'L0_ffn_bo',
        'L0_ffn_gate_W', 'L0_ffn_gate_b', 'L0_ffn_W1', 'L0_ffn_b1', 'L0_ffn_W2', 'L0_ffn_b2']


def kernel(**inputs):
    import numpy as np
    import concourse.bacc as bacc
    from concourse.bass_utils import run_bass_kernel_spmd

    nc = bacc.Bacc("TRN2", target_bir_lowering=False, num_devices=1)
    arrays, aps = {}, {}
    for name in _INS:
        a = np.ascontiguousarray(inputs[name])
        arrays["in_" + name] = a
        aps[name] = nc.dram_tensor("in_" + name, a.shape, mybir.dt.from_np(a.dtype), kind="ExternalInput").ap()
    out = nc.dram_tensor("out", (N, D), F32, kind="ExternalOutput").ap()
    gnn = {k[len("L0_gnn_"):]: v for k, v in aps.items() if k.startswith("L0_gnn_")}
    ffn = {k[len("L0_ffn_"):]: v for k, v in aps.items() if k.startswith("L0_ffn_")}
    fused_graph_ffn(nc, aps["x"], aps["adj"], gnn, ffn, out)
    r = run_bass_kernel_spmd(nc, [arrays], core_ids=[0])
    return r.results[0]["out"]
```

```python
from contextlib import ExitStack

import concourse.bass as bass
from concourse import mybir

F32 = mybir.dt.float32
F16 = mybir.dt.float16
BF16 = mybir.dt.bfloat16
F8 = mybir.dt.float8e5
I32 = mybir.dt.int32
U32 = mybir.dt.uint32
ALU = mybir.AluOpType
ACT = mybir.ActivationFunctionType
AX = mybir.AxisListType


class Names:
    pass


P = 128
N = 2048
D = 256
T = N // P
KC = D // P
HEADS = 8
EXPERTS = 8
FF = 4 * D
FC = FF // P
EPS = 1e-5
BLOCK = 512
NB = N // BLOCK
SLOTS = (N - EXPERTS) // P + EXPERTS
MASKED = 8e16

QP = 2
GQ = N // QP
UNITS = QP * T
RING = 4
SCORE_SLOTS = 2
PAIRS = HEADS // 2
TURN_NEXT, TURN_OWN = 20, 3


def max_units(A, step):
    if step not in A.max_steps:
        return range(0)
    at, n = A.max_steps.index(step), len(A.max_steps)
    return range(at * T * NB // n, (at + 1) * T * NB // n)


TURN_UNIT = T * NB // 2
FIRST_JOBS = T * NB + 1

TILE_PAIRS = (SLOTS - 1) // 2
SUM_TILES = T - 1
SUMS = SUM_TILES - 1

KB = 1024

HALF = T // 2
NORM_ROOT = 2 * HALF + 1
NORM_STEPS = NORM_ROOT + 5

ROUTE_EXP, ROUTE_ONE_HOT, ROUTE_ROWS, ROUTE_DONE = 2, 6, 37, 41

ROW = D + 2


def fused_graph_ffn(nc, x, adj, gW, fW, out):
    ctx = ExitStack()
    with ctx:
        def sb(name, shape, dt):
            return ctx.enter_context(nc.sbuf_tensor(name, shape, dt))

        def sem(name):
            return ctx.enter_context(nc.semaphore(name))

        def dram(name, shape, dt):
            return nc.dram_tensor(name, shape, dt, kind="Internal").ap()

        arena = sb("arena", [P, 202 * KB // 4], F32)
        size = {F32: 4, I32: 4, U32: 4, F16: 2, BF16: 2, F8: 1}

        def at(kb, shape, dt):
            n = 1
            for s in shape[1:]:
                n *= s
            words = n * size[dt] // 4
            a = arena[0:shape[0], int(kb * KB) // 4:int(kb * KB) // 4 + words]
            if dt != F32:
                a = a.bitcast(dt)
            if len(shape) == 3:
                a = a.rearrange("p (a b) -> p a b", a=shape[1])
            if len(shape) == 4:
                a = a.rearrange("p (a b c) -> p a b c", a=shape[1], b=shape[2])
            return a

        xs = at(0, [P, T, D], F32)
        gwo = at(16, [P, 4, D], F32)
        bias_v, bias_o, ln_g, ln_b = (at(16 + i, [P, D], F32) for i in range(4))
        fwq, fwk, fwv, fwo = (at(20 + 2 * i, [P, KC, D], F32) for i in range(4))
        mask_rows = at(28, [P, T, N], BF16)
        mask_cols = at(92, [P, T, N], F8)
        w1h = at(28, [P, EXPERTS * KC * FF], F16)
        w1l = at(60, [P, EXPERTS * KC * FF], F16)
        w2h = at(92, [P, EXPERTS * FC * D], F16)
        w2l = at(162, [P, EXPERTS * FC * D], F16)
        hi_st = at(124, [P, 2, N], F16)
        lo_st = at(132, [P, 2, N], F16)
        gwq, gwk, gwv = (at(kb, [P, KC, HEADS * 64], F32) for kb in (140, 144, 180))
        adj_in = at(148, [P, 2, N], F32)
        nT = at(164, [P, KC, N], F32)
        v_st = at(184, [P, 2, BLOCK], F32)
        nx = at(188, [P, 4, D], F32)
        w_in = at(194, [P, 2, 1024], F32)
        token_rows = at(140, [P, T, ROW], F32)
        ts = token_rows[:, :, 0:D]
        unused_rows = at(200, [P, ROW], F32)
        tT = at(132, [P, 4, KC, P], F32)
        logits, choice, one_hot, rank = (at(160 + i / 2, [P, T, EXPERTS], F32) for i in range(4))
        totals, run0, run1, place = (at(20 + i / 2, [P, T, EXPERTS], F32) for i in range(4))
        slot_of = at(22, [P, SLOTS, EXPERTS], F32)
        b1_rows = at(25, [EXPERTS * FC, P], F32)
        gate_w = at(25.5, [P, KC, EXPERTS], F32)
        gate_b = at(25.625, [P, EXPERTS], F32)
        sorted_in = at(124, [P, 2, D], F32)
        sTh = at(126, [P, 2, KC, P], F16)
        sTl = at(127, [P, 2, KC, P], F16)
        hid = at(128, [P, 2, FC, P], F32)
        hid_h = at(136, [P, 2, FC, P], F16)
        hid_l = at(140, [P, 2, FC, P], F16)
        x_in = at(144, [P, 2, D], F32)
        b2_all = at(146, [P, EXPERTS * D], F32)
        res = at(154, [P, 2, D], F32)

        small = sb("small", [P, 128], F32)
        ident = sb("ident", [P, P], F32)
        identb = sb("identb", [P, P], BF16)
        identt = sb("identt", [P, P], BF16)
        ones = sb("ones", [P, P], F32)
        ps = ctx.enter_context(nc.psum_tensor("ps", [P, 8, BLOCK], F32))

        sorted_d = dram("sorted_tokens", [SLOTS * P, ROW], F32)
        x1_d = dram("residual_stream", [N, D], F32)

        def scratch(name, width):
            d = Names()
            d.q = dram(name + "_q", [HEADS, 2, width // HEADS, N], F16)
            d.k = dram(name + "_k", [HEADS, 2, width // HEADS, N], F16)
            d.v = dram(name + "_v", [P, T, width], F32)
            d.o = dram(name + "_o", [width, N], F32)
            return d

        def attention_sems(name):
            s = Names()
            s.ln = sem(name + "_ln")
            s.sqrt = sem(name + "_sqrt")
            s.nx = sem(name + "_nx")
            s.hi = sem(name + "_hi")
            s.qk_stored = [sem(name + f"_qk_stored{i}") for i in range(2)]
            s.v_stored = [sem(name + f"_v_stored{i}") for i in range(2)]
            s.loaded = [sem(name + f"_loaded{i}") for i in range(2)]
            s.rest = [sem(name + f"_rest{i}") for i in range(2)]
            s.ones_row = sem(name + "_ones_row")
            s.v_full = sem(name + "_v_full")
            s.v_out = sem(name + "_v_out")
            s.scores = sem(name + "_scores")
            s.exp = sem(name + "_exp")
            s.pv = sem(name + "_pv")
            s.summed = sem(name + "_summed")
            s.evac = sem(name + "_evac")
            s.evac_step = sem(name + "_evac_step")
            s.job = sem(name + "_job")
            s.drained = sem(name + "_drained")
            s.top = sem(name + "_top")
            s.row_in = [sem(name + f"_row_in{i}") for i in range(QP)]
            s.o_stored = [sem(name + f"_o_stored{i}") for i in range(2)]
            s.o_in = sem(name + "_o_in")
            s.proj = sem(name + "_proj")
            s.proj_used = sem(name + "_proj_used")
            return s

        amax = sb("amax", [P, T, NB], F32)
        top = sb("top", [P, T], F32)
        neg_top = [sb(f"neg_top{i}", [T // QP, P], F16) for i in range(QP)]

        G = Names()
        G.masked, G.dim, G.chunks, G.scale, G.max_rows = True, 64, 4, 64 ** -0.5, P
        G.max_steps = [j for j in range(4, UNITS) if j not in (T, T + 1, T + 2)]
        G.jobs = T * NB + 2 + QP
        G.d, G.s = scratch("gnn", 512), attention_sems("gnn")
        G.ka = [at(124 + 16 * i, [P, N], F16) for i in range(2)]
        G.kb = [at(128 + 16 * i, [65, N], F16) for i in range(2)]
        G.qa = [at(132 + 16 * i, [P, N], F16) for i in range(2)]
        G.qb = [at(136 + 16 * i, [65, N], F16) for i in range(2)]
        G.v = [at(156 + 4 * i, [P, T, 64], F32) for i in range(2)]
        G.p = at(164, [P, RING, GQ], F32)
        G.sum = at(180, [P, 2, GQ], F32)
        G.r = at(188, [P, BLOCK], F32)
        G.o = at(190, [P, 2, BLOCK], F32)
        G.junk = at(194, [P, 2, BLOCK], BF16)
        G.row = [G.qb[i][64:65, :] for i in range(2)]
        G.ones_row = [G.kb[i][64:65, :] for i in range(2)]
        G.oT = [at(60 + 8 * c, [P, N], F32) for c in range(4)]
        G.loads, G.rests, G.early = 3, 3, 5
        G.wq, G.wk, G.wv = gwq, gwk, gwv
        F = Names()
        F.masked, F.dim, F.chunks, F.scale, F.max_rows = False, 32, 2, 32 ** -0.5, 96
        F.max_steps = [j for j in range(4, UNITS) if j not in (T + 1, T + 2, T + 3)]
        F.jobs = T * NB + 2
        for A in (G, F):
            A.turned = 2 + A.masked + sum(len(max_units(A, j)) for j in range(TURN_NEXT + 1))
        F.d, F.s = scratch("ffn", 256), attention_sems("ffn")
        F.ka = [at(124 + 8 * i, [97, N], F16) for i in range(2)]
        F.qa = [at(128 + 8 * i, [97, N], F16) for i in range(2)]
        F.v = [at(140 + 2 * i, [P, T, 32], F32) for i in range(2)]
        F.p = at(144, [P, RING, GQ], F32)
        F.r = at(160, [P, BLOCK], F32)
        F.o = at(20, [P, 2, BLOCK], F32)
        F.row = [F.qa[i][96:97, :] for i in range(2)]
        F.ones_row = [F.ka[i][96:97, :] for i in range(2)]
        F.oT = [at(kb, [P, N], F32) for kb in (124, 194)]
        F.loads, F.rests, F.early = 4, 1, 7
        F.wq, F.wk, F.wv = fwq, fwk, fwv
        bq_cols = sb("bq_cols", [P, 2], F32)
        bk_cols = sb("bk_cols", [P, 2], F32)

        b1_cols = sb("b1_cols", [P, EXPERTS * FC], F32)
        b1_tile = sb("b1_tile", [P, 2, FC], F32)
        before = sb("before", [P, P], F32)
        e_iota = sb("e_iota", [P, EXPERTS], F32)
        slot_iota = sb("slot_iota", [P, SLOTS], F32)
        counts = sb("counts", [P, 3, EXPERTS], F32)
        counts_i = sb("counts_i", [P, EXPERTS], I32)
        gate = sb("gate", [P, T], F32)
        slot_row = sb("slot_row", [P, T], I32)
        token_number = sb("token_number", [P, T], I32)
        slot_meta = sb("slot_meta", [P, 2 * SLOTS], F32)
        slot_gate = sb("slot_gate", [P, 2], F32)
        slot_expert = sb("slot_expert", [P, SLOTS], I32)
        slot_expert_f = sb("slot_expert_f", [P, SLOTS], F32)
        mv2 = sb("mv2", [P, T, 2], F32)
        stats = sb("stats", [P, T, 6], F32)
        mv = sb("mv", [P, T, 2], F32)
        veps = small[:, 0:16]
        std = small[:, 16:32]
        rstd = small[:, 32:48]
        tmp = small[:, 48:64]
        shift = small[:, 64:80]
        rstd1 = small[:, 80:96]

        s_x = [sem(f"x_in{i}") for i in range(2)]
        s_w = sem("gnn_weights_in")
        s_fw = sem("ffn_weights_in")
        s_adj = [sem(f"adj_in{i}") for i in range(2)]
        s_adj_diag = sem("adj_diag")
        s_mask = sem("mask_rows_raw")
        s_mask_scaled = sem("mask_rows_scaled")
        s_const = sem("constants")
        s_const2 = sem("constants_derived")
        s_mmA = sem("bank_for_scalar_full")
        s_evA = sem("bank_for_scalar_free")
        s_mmD = sem("bank_for_vector_full")
        s_evD = sem("bank_for_vector_free")
        s_moe_w = sem("moe_vectors_in")
        s_moe_const = sem("moe_constants")
        s_zero = sem("sorted_zeroed")
        s_w_in = [sem(f"expert_weights_in{i}") for i in range(2)]
        s_w_split = sem("expert_weights_split")
        s_hsum = sem("attention_residual")
        s_ln2 = sem("second_norm")
        s_shift = sem("first_norm_factors_kept")
        s_centred = sem("centred_tile")
        s_sqrt2 = sem("second_norm_root")
        s_h = sem("hidden_tile")
        s_hT = sem("hidden_turned")
        s_tT = sem("hidden_turned_out")
        s_lg = sem("logits_full")
        s_lg_out = sem("logits_out")
        s_route = sem("routing")
        s_route_exp = sem("routing_exp")
        s_prefix = sem("prefix_counts")
        s_b1 = sem("b1_turned")
        s_b1_out = sem("b1_turned_out")
        s_zero_in = sem("unused_rows_written")
        s_placed = sem("tokens_placed")
        s_sorted_in = [sem(f"sorted_in{i}") for i in range(2)]
        s_sT = sem("sorted_turned")
        s_sT_out = sem("sorted_split")
        s_up = sem("up_products")
        s_gelu = sem("gelu")
        s_b1_tile = sem("b1_of_tile")
        s_hid = sem("hidden_split")
        s_down = sem("down_products")
        s_y = sem("expert_tile_out")
        s_x1 = sem("residual_stream_stored")
        s_meta = sem("gates_and_numbers_in")
        s_b2_in = sem("second_biases_in")
        s_numbers = sem("token_numbers")
        s_x_zero = sem("residual_buffers_zeroed")
        s_x_in = [sem(f"residual_rows_in{i}") for i in range(2)]
        s_gate = sem("gate_of_tile")
        s_sum = sem("expert_sum")
        s_res_out = [sem(f"result_stored{i}") for i in range(2)]
        s_res_free = sem("result_buffer_free")

        block = ctx.enter_context(nc.Block())

        XT = T // 2
        A_GNN = XT + 2 * T
        A_ALL = A_GNN + XT
        D_QK = 2 * 4 * NB
        D_GNN = D_QK
        FD_QK = 2 * 2 * NB

        @block.sync
        def _(sp):
            for i in range(2):
                sp.dma_start(xs[:, 8 * i:8 * i + 8, :],
                             x[1024 * i:1024 * i + 1024, :].rearrange("(t p) d -> p t d", p=P)).then_inc(s_x[i], 16)
            for w, a in zip((gwq, gwk, gwv), (gW["Wqs"], gW["Wks"], gW["Wvs"])):
                for c in range(KC):
                    sp.dma_start(w[:, c, :].rearrange("p (h k) -> p h k", h=HEADS),
                                 a[:, c * P:(c + 1) * P, :].rearrange("h p k -> p h k")).then_inc(s_w, 16)
            sp.dma_start(gwo, gW["Wo"].rearrange("h k o -> (h k) o").rearrange("(c p) o -> p c o", p=P)).then_inc(s_w, 16)
            def store_chunk(A, d_base, n):
                sp.wait_ge(s_evD, d_base + NB * (n + 1))
                dst, c, per = (A.d.q, A.d.k)[n % 2], n // 2, P // A.dim
                for part, src in ((n % 2, hi_st), (1 - n % 2, lo_st)):
                    sp.dma_start(dst[c * per:(c + 1) * per, part, :, :], src[:, n % 2, :])\
                        .then_inc(A.s.qk_stored[n % 2], 16)

            for t in range(T):
                if t >= 2:
                    sp.wait_ge(s_mask, t - 1)
                sp.dma_start(adj_in[:, t % 2, :], adj[t * P:(t + 1) * P, :]).then_inc(s_adj[t % 2], 16)
                if t % 2 and t >= 3:
                    store_chunk(G, 0, (t - 3) // 2)
            for w, a in zip((fwq, fwk, fwv, fwo), (fW["Wq"], fW["Wk"], fW["Wv"], fW["Wo"])):
                sp.dma_start(w, a.rearrange("(c p) n -> p c n", p=P)).then_inc(s_fw, 16)
            sp.dma_start(bq_cols[:, :], fW["bq"].rearrange("(c p) -> p c", p=P), allow_slow_non_contiguous=True).then_inc(s_fw, 16)
            sp.dma_start(bk_cols[:, :], fW["bk"].rearrange("(c p) -> p c", p=P), allow_slow_non_contiguous=True).then_inc(s_fw, 16)

            def load_keys(A, h, p):
                d, k, q = A.dim, A.d.k[bass.ds(h, 1)], A.d.q[bass.ds(h, 1)]
                if A.masked:
                    pairs = [(A.ka[p][0:2 * d, :], k), (A.qa[p][0:d, :], q[:, 0]), (A.qa[p][d:2 * d, :], q[:, 0])]
                else:
                    pairs = [(A.ka[p][0:2 * d, :], k), (A.ka[p][2 * d:3 * d, :], k[:, 1]),
                             (A.qa[p][0:d, :], q[:, 0]), (A.qa[p][d:3 * d, :], q)]
                for dst, src in pairs:
                    src = src.rearrange("a s d n -> (a s d) n") if len(src.shape) == 4 else \
                        src.rearrange("a d n -> (a d) n")
                    sp.dma_start(dst, src).then_inc(A.s.loaded[p], 16)

            def load_rest(A, h, p, second=True, values=True):
                if A.masked and second:
                    for dst, src in ((A.kb[p], A.d.k), (A.qb[p], A.d.q)):
                        sp.dma_start(dst[0:A.dim, :], src[bass.ds(h, 1), 1].rearrange("a d n -> (a d) n"))\
                            .then_inc(A.s.rest[p], 16)
                if values:
                    sp.dma_start(A.v[p], A.d.v[:, :, bass.ds(h * A.dim, A.dim)]).then_inc(A.s.rest[p], 16)

            def row_half(A, p, qp):
                sp.dma_start(A.row[p][:, qp * GQ:(qp + 1) * GQ].rearrange("a (t q) -> a t q", t=T // QP),
                             neg_top[qp][:, :])\
                    .then_inc(A.s.row_in[qp], 16)

            def load_gate_vectors():
                for dst, src in ((b1_rows, fW["b1"].rearrange("e (c p) -> (e c) p", p=P)),
                                 (gate_w, fW["gate_W"].rearrange("(c p) e -> p c e", p=P)),
                                 (gate_b, fW["gate_b"].partition_broadcast(P))):
                    sp.dma_start(dst, src).then_inc(s_moe_w, 16)

            def store_group(A, i, p, qp, last=False):
                h = 2 * i + p
                sp.wait_ge(A.s.evac, i * 4 + (2 * p + qp + 3))
                for half in range(2):
                    rows = A.o[A.dim * half:A.dim * (half + 1), qp, :]
                    col = qp * GQ + half * BLOCK
                    if last:
                        at_row = h * A.dim % P
                        dst = A.oT[-1][at_row:at_row + A.dim, col:col + BLOCK]
                    else:
                        dst = A.d.o[bass.ds(h * A.dim, A.dim), col:col + BLOCK]
                    sp.dma_start(dst, rows).then_inc(A.s.o_stored[qp], 16)

            def attention(A):
                for i in range(2):
                    sp.wait_ge(A.s.qk_stored[i], 32 * A.chunks)
                for h in range(2):
                    load_keys(A, h, h)
                    load_rest(A, h, h, values=False)
                for i in range(2):
                    sp.wait_ge(A.s.v_stored[i], 16 * T // 2)
                for h in range(2):
                    load_rest(A, h, h, second=False)
                if A is F:
                    load_gate_vectors()
                sp.wait_ge(A.s.drained, TURN_UNIT + 1)
                row_half(A, 0, 0)

                def own_row(i, p):
                    sp.wait_ge(A.s.drained, i * (2 * A.jobs) + (FIRST_JOBS + p * A.jobs + 1))
                    row_half(A, p, 1)

                def next_row(i, p):
                    sp.wait_ge(A.s.drained, i * (2 * A.jobs) + (FIRST_JOBS + p * A.jobs + A.turned))
                    row_half(A, 1 - p, 0)

                with sp.Fori(0, PAIRS - 1) as i:
                    for p in range(2):
                        own_row(i, p)
                        store_group(A, i, p, 0)
                        next_row(i, p)
                        sp.wait_ge(A.s.pv, i * (2 * UNITS) + (RING + UNITS * (p + 1)))
                        load_keys(A, 2 * i + (2 + p), p)
                        store_group(A, i, p, 1)
                        load_rest(A, 2 * i + (2 + p), p)
                i = PAIRS - 1
                own_row(i, 0)
                next_row(i, 0)
                own_row(i, 1)
                if not A.masked:
                    sp.wait_ge(s_w_split, 2 * 4 * EXPERTS)
                for qp in range(2):
                    store_group(A, i, 0, qp, last=True)
                for qp in range(2):
                    sp.wait_ge(A.s.o_stored[qp], 32 * (HEADS - 1))
                if not A.masked:
                    sp.wait_ge(A.s.pv, i * (2 * UNITS) + (RING + UNITS))
                for c in range(A.chunks):
                    rows = min(P, (HEADS - 2) * A.dim - c * P)
                    if rows:
                        sp.dma_start(A.oT[c][0:rows, :], A.d.o[c * P:c * P + rows, :]).then_inc(A.s.o_in, 16)
                for qp in range(2):
                    store_group(A, i, 1, qp, last=True)

            store_chunk(G, 0, 2 * G.chunks - 1)
            attention(G)
            sp.wait_ge(G.s.proj_used, T)
            for dst, src in ((bias_v, fW["bv"]), (bias_o, fW["bo"]), (ln_g, fW["ln1_g"]), (ln_b, fW["ln1_b"])):
                sp.dma_start(dst, src.partition_broadcast(P)).then_inc(s_fw, 16)
            sp.dma_start(x1_d.rearrange("(t p) d -> p t d", p=P), xs).then_inc(s_x1, 16)
            for n in range(2 * F.chunks):
                store_chunk(F, D_GNN, n)
            attention(F)

            sp.wait_ge(s_placed, 16 * T)

            def load_sorted(j, p):
                sp.dma_start(sorted_in[:, p, :], sorted_d[bass.ds(j * P, P), 0:D]).then_inc(s_sorted_in[p], 16)

            load_sorted(0, 0)
            load_sorted(1, 1)
            sp.dma_start(slot_meta[:, :].rearrange("p (j c) -> p j c", c=2),
                         sorted_d[:, D:ROW].rearrange("(j p) c -> p j c", p=P)).then_inc(s_meta, 16)
            sp.dma_start(b2_all, fW["b2"].rearrange("e d -> (e d)").partition_broadcast(P)).then_inc(s_b2_in, 16)
            with sp.Fori(0, TILE_PAIRS - 1) as i:
                for p in range(2):
                    sp.wait_ge(s_sT, i * 2 + (p + 1))
                    load_sorted(2 * i + (2 + p), p)
            sp.wait_ge(s_sT, SLOTS - 2)
            load_sorted(SLOTS - 1, 0)

        @block.gpsimd
        def _(pool):
            pool.memset(ident[:, :], 0.0).then_inc(s_const, 1)
            pool.memset(ones[:, :], 1.0).then_inc(s_const, 1)
            for s in (G.s, F.s):
                pool.sem_inc(s.exp, SCORE_SLOTS)
                pool.sem_inc(s.pv, RING)
                pool.sem_inc(s.summed, SUMS)
                pool.sem_inc(s.evac, 2)
                pool.sem_inc(s.row_in[1], 16)
                pool.sem_inc(s.o_stored[0], 32)
                pool.sem_inc(s.o_stored[1], 32)
            pool.sem_inc(s_hid, 4)
            pool.sem_inc(s_sT_out, 4)
            pool.sem_inc(s_up, 2)
            pool.sem_inc(s_gelu, 2)
            pool.sem_inc(s_down, 2)
            pool.sem_inc(s_y, 2)
            pool.sem_inc(s_res_free, 2)
            pool.memset(before[:, :], 1.0).then_inc(s_moe_const, 1)
            pool.memset(unused_rows[:, 0:D + 1], 0.0).then_inc(s_zero_in, 1)
            pool.memset(unused_rows[:, D + 1:ROW].bitcast(I32), N).then_inc(s_zero_in, 1)
            pool.iota(token_number[:, :], [[P, T]], base=0, channel_multiplier=1).then_inc(s_numbers, 1)
            pool.iota(e_iota[:, :], [[-1, EXPERTS]], base=EXPERTS, channel_multiplier=0,
                      allow_small_or_imprecise_dtypes=True).then_inc(s_moe_const, 1)
            pool.iota(slot_iota[:, :], [[1, SLOTS]], base=0, channel_multiplier=0,
                      allow_small_or_imprecise_dtypes=True).then_inc(s_moe_const, 1)
            pool.wait_ge(s_moe_const, 3)
            pool.affine_select(out=before[:, :], in_=before[:, :], compare_op=ALU.is_gt, fill=0.0,
                               base=0, pattern=[[1, P]], channel_multiplier=-1).then_inc(s_moe_const, 1)
            pool.wait_ge(s_zero_in, 2)
            pool.dma_start(sorted_d.rearrange("(j p) d -> p j d", p=P),
                           unused_rows.unsqueeze(1).to_broadcast([P, SLOTS, ROW])).then_inc(s_zero, 16)
            pool.wait_ge(s_const, 1)
            pool.affine_select(out=ident[:, :], in_=ident[:, :], compare_op=ALU.not_equal, fill=1.0,
                               base=0, pattern=[[-1, P]], channel_multiplier=1).then_inc(s_const, 1)

            def add_probabilities(A):
                def heads(i):
                    for g in range(4):
                        for kt in range(1, SUM_TILES):
                            n = T * g + kt
                            if kt == 1:
                                pool.wait_ge(A.s.evac, i * 4 + (g + 1))
                            pool.wait_ge(A.s.exp, i * (4 * T) + (SCORE_SLOTS + n + 1))
                            total = A.sum[:, g % 2, :]
                            if kt == 1:
                                first = A.p[:, (n - 1) % RING, :]
                            else:
                                pool.wait_ge(A.s.summed, i * (4 * SUMS) + (SUMS * (g + 1) + kt - 1))
                                first = total
                            pool.tensor_tensor(total, first, A.p[:, n % RING, :], ALU.add).then_inc(A.s.summed, 1)
                with pool.Fori(0, PAIRS) as i:
                    heads(i)

            add_probabilities(G)
            def split_weights(first, src, hi, lo, width):
                for c in range(2 * EXPERTS):
                    n = first + c
                    if n >= 2:
                        pool.wait_ge(s_w_split, 2 * (n - 1))
                    pool.dma_start(w_in[:, n % 2, :].rearrange("p (a b) -> p a b", b=width), src(c))\
                        .then_inc(s_w_in[n % 2], 16)
                    if c:
                        split(n - 1, hi, lo, c - 1)
                split(first + 2 * EXPERTS - 1, hi, lo, 2 * EXPERTS - 1)

            def split(n, hi, lo, c):
                cols = slice(c * 1024, (c + 1) * 1024)
                pool.wait_ge(s_w_in[n % 2], 16 * (n // 2 + 1))
                pool.tensor_copy(hi[:, cols], w_in[:, n % 2, :]).then_inc(s_w_split, 1)
                pool.wait_ge(s_w_split, 2 * n + 1)
                pool.tensor_tensor(lo[:, cols], w_in[:, n % 2, :], hi[:, cols], ALU.subtract)\
                    .then_inc(s_w_split, 1)

            pool.wait_ge(G.s.proj_used, T)
            pool.wait_ge(s_zero, 16)
            split_weights(0, lambda c: fW["W1"][c // 2, (c % 2) * P:(c % 2 + 1) * P, :].unsqueeze(1),
                          w1h, w1l, FF)
            pool.wait_ge(F.s.v_full, T)
            for i in range(2):
                pool.wait_ge(F.s.v_stored[i], 8 * T)
            split_weights(2 * EXPERTS,
                          lambda c: fW["W2"][c // 2, (c % 2) * 512:(c % 2 + 1) * 512, :].rearrange(
                              "(c p) d -> p c d", p=P),
                          w2h, w2l, D)
            pool.wait_ge(s_route, ROUTE_ROWS)
            for t in range(T):
                pool.indirect_dma_start(
                    out=sorted_d, out_offset=bass.IndirectOffsetOnAxis(ap=slot_row[:, t:t + 1].bitcast(U32), axis=0),
                    in_=token_rows[:, t, :], in_offset=None).then_inc(s_placed, 16)
            pool.wait_ge(s_placed, 16 * T)
            pool.memset(x_in, 0.0).then_inc(s_x_zero, 1)
            pool.wait_ge(s_x_zero, 1)
            pool.wait_ge(s_x1, 16)
            pool.wait_ge(s_meta, 16)

            def tokens_of(j):
                return bass.IndirectOffsetOnAxis(ap=slot_meta[:, 2 * j + 1:2 * j + 2].bitcast(U32), axis=0)

            def store_result(j):
                pool.wait_ge(s_y, j + 3)
                pool.indirect_dma_start(out=out, out_offset=tokens_of(j), in_=res[:, j % 2, :], in_offset=None,
                                        bounds_check=N - 1, oob_is_err=False).then_inc(s_res_out[j % 2], 16)

            for j in range(SLOTS):
                if j >= 2:
                    pool.wait_ge(s_y, j + 1)
                pool.indirect_dma_start(out=x_in[:, j % 2, :], out_offset=None, in_=x1_d, in_offset=tokens_of(j),
                                        bounds_check=N - 1, oob_is_err=False).then_inc(s_x_in[j % 2], 16)
                if j >= 2:
                    pool.wait_ge(s_res_out[j % 2], 16 * (j // 2))
                    pool.sem_inc(s_res_free, 1)
                if j >= 1:
                    store_result(j - 1)
            store_result(SLOTS - 1)
            for p in range(2):
                pool.wait_ge(s_res_out[p], 16 * ((SLOTS + 1 - p) // 2))

        @block.scalar
        def _(act):
            def roots(steps, done):
                for half in range(2):
                    h = slice(half * HALF, (half + 1) * HALF)
                    act.wait_ge(steps, half * NORM_STEPS + NORM_ROOT)
                    nc.scalar.activation(std[:, h], veps[:, h], ACT.Sqrt).then_inc(done, 1)

            def transposed_input(base):
                for u in range(XT):
                    act.wait_ge(s_mmA, base + u + 1)
                    nc.scalar.activation(nT[:, :, u * 256:(u + 1) * 256],
                                         ps[:, (base + u) % 4, :].rearrange("p (k n) -> p k n", k=KC),
                                         ACT.Copy).then_inc(s_evA, 1)

            def high_half(A, d_base, k):
                n, b, j = k // NB, k % NB, d_base + k
                if n >= 2 and b == 0:
                    act.wait_ge(A.s.qk_stored[n % 2], 32 * (n // 2))
                act.wait_ge(s_mmD, j + 1)
                bank, dst = ps[:, 4 + j % 4, :], hi_st[:, n % 2, b * BLOCK:(b + 1) * BLOCK]
                if A is F:
                    col = (bq_cols, bk_cols)[n % 2][:, n // 2:n // 2 + 1]
                    nc.scalar.activation(dst, bank, ACT.Identity, bias=col).then_inc(A.s.hi, 1)
                else:
                    nc.scalar.activation(dst, bank, ACT.Copy).then_inc(A.s.hi, 1)

            def values_out(A):
                width = A.chunks * P
                for t in range(T):
                    act.wait_ge(A.s.v_full, t + 1)
                    if t >= 2:
                        act.wait_ge(A.s.v_stored[t % 2], 16 * (t // 2))
                    nc.scalar.activation(v_st[:, t % 2, 0:width], ps[:, 4 + t % 2, 0:width], ACT.Copy)\
                        .then_inc(A.s.v_out, 1)
                    act.wait_ge(A.s.v_out, t + 1)
                    act.dma_start(A.d.v[:, t, :], v_st[:, t % 2, 0:width]).then_inc(A.s.v_stored[t % 2], 16)

            def exps(A):
                def heads(i):
                    for n in range(2 * UNITS):
                        act.wait_ge(A.s.scores, i * (2 * UNITS) + (n + 1))
                        act.wait_ge(A.s.pv, i * (2 * UNITS) + (n + 1))
                        if A.masked:
                            m = n - RING
                            got = SUMS * (m // T) + min(max(m % T, 1), SUMS)
                            act.wait_ge(A.s.summed, i * (4 * SUMS) + (SUMS + got))
                        slot = 2 * (n % SCORE_SLOTS)
                        nc.scalar.activation(A.p[:, n % RING, :].rearrange("p (a b) -> p a b", a=2),
                                             ps[:, slot:slot + 2, :], ACT.Exp, scale=A.scale).then_inc(A.s.exp, 1)
                with act.Fori(0, PAIRS) as i:
                    heads(i)

            roots(G.s.ln, G.s.sqrt)
            transposed_input(0)
            for t in range(T):
                for k in (2 * t, 2 * t + 1):
                    high_half(G, 0, k)
                for half in range(2):
                    j = XT + 2 * t + half
                    act.wait_ge(s_mmA, j + 1)
                    nc.scalar.activation(mask_cols[:, 8 * half:8 * half + 8, t * P:(t + 1) * P],
                                         ps[:, j % 4, :].bitcast(BF16).rearrange("p (a b) -> p a b", a=8),
                                         ACT.Copy, saturate=False).then_inc(s_evA, 1)
            values_out(G)
            exps(G)
            roots(F.s.ln, F.s.sqrt)
            transposed_input(A_GNN)
            act.wait_ge(s_fw, 16 * 10)
            for k in range(FD_QK):
                high_half(F, D_GNN, k)
            values_out(F)
            exps(F)

            roots(s_ln2, s_sqrt2)
            for t in range(T):
                act.wait_ge(s_hT, t + 1)
                if t >= 4:
                    act.wait_ge(s_lg, t - 3)
                nc.scalar.activation(tT[:, t % 4, :, :], ps[:, t % 4, 0:D].rearrange("p (k n) -> p k n", k=KC),
                                     ACT.Copy).then_inc(s_tT, 1)
            act.wait_ge(s_b1, 1)
            nc.scalar.activation(b1_cols[:, :], ps[:, 4, 0:EXPERTS * FC], ACT.Copy).then_inc(s_b1_out, 1)
            act.wait_ge(s_route, ROUTE_EXP)
            nc.scalar.activation(choice, choice, ACT.Exp).then_inc(s_route_exp, 1)

            def gelus(p, n):
                act.wait_ge(s_up, n + 3)
                act.wait_ge(s_b1_tile, n + 1)
                act.wait_ge(s_hid, n * 2 + 2)
                for c in range(FC):
                    m = nc.scalar.activation(
                        hid[:, p, c, :], ps[:, 2 * p + c // 4, (c % 4) * P:(c % 4 + 1) * P],
                        ACT.Gelu_apprx_tanh, bias=b1_tile[:, p, c:c + 1])
                m.then_inc(s_gelu, 1)

            gelus(0, 0)
            gelus(1, 1)
            with act.Fori(0, TILE_PAIRS - 1) as i:
                for p in range(2):
                    gelus(p, 2 * i + (2 + p))
            gelus(0, SLOTS - 1)

        @block.tensor
        def _(pe):
            pe.wait_ge(s_const2, 3)

            def transpose_input(A, base):
                for u in range(XT):
                    j = base + u
                    if j >= 4:
                        pe.wait_ge(s_evA, j - 3)
                    pe.wait_ge(A.s.nx, 2 * u + 2)
                    for k in range(KC):
                        for t in range(2):
                            m = pe.transpose(ps[:, j % 4, k * 256 + t * P:k * 256 + (t + 1) * P],
                                             nx[:, (2 * u + t) % 4, k * P:(k + 1) * P], ident[:, :])
                    m.then_inc(s_mmA, 1)

            def project(A, d_base, k):
                n, b, j = k // NB, k % NB, d_base + k
                w, c = (A.wq, A.wk)[n % 2], n // 2
                if j >= 4:
                    pe.wait_ge(s_evD, j - 3)
                for kc in range(KC):
                    m = pe.matmul(ps[:, 4 + j % 4, :], w[:, kc, c * P:(c + 1) * P],
                                  nT[:, kc, b * BLOCK:(b + 1) * BLOCK], start=kc == 0, stop=kc == KC - 1)
                m.then_inc(s_mmD, 1)

            def project_values(A, t, part=None):
                if t >= 2 and part in (None, 0):
                    pe.wait_ge(A.s.v_out, t - 1)
                bank = ps[:, 4 + t % 2, 0:A.chunks * P]
                for kc in range(KC) if part is None else (part,):
                    m = pe.matmul(bank, nT[:, kc, t * P:(t + 1) * P], A.wv[:, kc, :],
                                  start=kc == 0, stop=kc == KC - 1 and A is G)
                if part == 0:
                    return
                if A is F:
                    m = pe.matmul(bank, ones[0:1, :], bias_v[0:1, :], start=False, stop=True)
                m.then_inc(A.s.v_full, 1)

            def attention(A):
                def max_block(p, u, job, value):
                    if value is not None:
                        pe.wait_ge(A.s.drained, value)
                    qt, mb = u // NB, u % NB
                    pe.matmul(ps[:, 6 + job % 2, :], A.qa[p][0:A.max_rows, qt * P:(qt + 1) * P],
                              A.ka[p][0:A.max_rows, mb * BLOCK:(mb + 1) * BLOCK],
                              start=True, stop=True).then_inc(A.s.job, 1)

                def turn_maxima(job, drained, tops, tiles):
                    pe.wait_ge(A.s.drained, drained)
                    pe.wait_ge(A.s.top, tops)
                    pe.transpose(ps[0:tiles.stop - tiles.start, 6 + job % 2, 0:P], top[:, tiles], ident[:, :])\
                        .then_inc(A.s.job, 1)

                for t in range(A.early):
                    project_values(A, t)
                pe.wait_ge(A.s.loaded[0], 16 * A.loads)
                for u in range(T * NB):
                    t, part = A.early + u // NB, u % NB // 2
                    if u % 2 == 0 and t < T:
                        project_values(A, t, part)
                    job = u + u // TURN_UNIT
                    max_block(0, u, job, job - 1 if job >= 2 else None)
                    if u == TURN_UNIT - 1:
                        turn_maxima(TURN_UNIT, TURN_UNIT - 1, 1, slice(0, T // 2))
                pe.wait_ge(A.s.v_out, T)
                pe.wait_ge(A.s.ones_row, 2)
                first = FIRST_JOBS

                def heads(i, last):
                    job = first
                    for p in range(2):
                        final = last and p == 1
                        pe.wait_ge(A.s.rest[p], i * (16 * A.rests) + 16 * A.rests)

                        def scores(j):
                            n = UNITS * p + j
                            qp, kt = j // T, j % T
                            if kt == 0:
                                pe.wait_ge(A.s.row_in[qp], i * 32 + 16 * (p + qp + 1))
                            pe.wait_ge(A.s.exp, i * (2 * UNITS) + (n + 1))
                            keys = slice(kt * P, (kt + 1) * P)
                            for half in range(2):
                                if A.masked or half == 0:
                                    next_max()
                                bank = ps[:, 2 * (n % SCORE_SLOTS) + half, :]
                                cols = slice(qp * GQ + half * BLOCK, qp * GQ + (half + 1) * BLOCK)
                                if A.masked:
                                    pe.matmul(bank, A.ka[p][:, keys], A.qa[p][:, cols], start=True, stop=False)
                                    pe.matmul(bank, identb[:, :], mask_cols[:, kt, cols], start=False, stop=False)
                                    m = pe.matmul(bank, A.kb[p][:, keys], A.qb[p][:, cols], start=False, stop=True)
                                else:
                                    m = pe.matmul(bank, A.ka[p][:, keys], A.qa[p][:, cols], start=True, stop=True)
                            m.then_inc(A.s.scores, 1)

                        def values(j):
                            nonlocal job
                            n = UNITS * p + j
                            g, kt = 2 * p + j // T, j % T
                            if kt == 0:
                                pe.wait_ge(A.s.evac, i * 4 + (g + 1))
                            pe.wait_ge(A.s.exp, i * (2 * UNITS) + (n + SCORE_SLOTS + 1))
                            acc = ps[:, 4 + g % 2, :]
                            first_kt, last_kt = kt == 0, kt == T - 1
                            for half in range(2):
                                pr = A.p[:, n % RING, half * BLOCK:(half + 1) * BLOCK]
                                m = pe.matmul(acc[A.dim * half:A.dim * (half + 1), :], A.v[p][:, kt, :], pr,
                                              start=first_kt, stop=last_kt)
                                if not A.masked:
                                    m = pe.matmul(acc[64 + 32 * half:96 + 32 * half, :], ones[:, 0:32], pr,
                                                  start=first_kt, stop=last_kt)
                            if A.masked and kt >= SUM_TILES:
                                if kt == SUM_TILES:
                                    pe.wait_ge(A.s.drained, i * (2 * A.jobs) + (job - 1))
                                den = ps[:, 6 + job % 2, :]
                                for half in range(2):
                                    m = pe.matmul(den[64 * half:64 * half + 64, :], ones[:, 0:64],
                                                  A.p[:, n % RING, half * BLOCK:(half + 1) * BLOCK],
                                                  start=kt == SUM_TILES, stop=False)
                            m.then_inc(A.s.pv, 1)
                            if A.masked and last_kt:
                                pe.wait_ge(A.s.summed, i * (4 * SUMS) + SUMS * (g + 2))
                                for half in range(2):
                                    m = pe.matmul(den[64 * half:64 * half + 64, :], ones[:, 0:64],
                                                  A.sum[:, g % 2, half * BLOCK:(half + 1) * BLOCK],
                                                  start=False, stop=True)
                                m.then_inc(A.s.job, 1)
                                job += 1

                        def next_max():
                            nonlocal job
                            if left:
                                max_block(1 - p, left.pop(0), job, i * (2 * A.jobs) + (job - 1))
                                job += 1

                        for j in range(UNITS):
                            left = [] if final else list(max_units(A, j))
                            if left and left[0] == 0:
                                pe.wait_ge(A.s.loaded[1 - p], i * (16 * A.loads) + 16 * A.loads * (p + 1))
                            scores(j)
                            if A.masked or len(left) < 3:
                                next_max()
                            if j >= 1:
                                values(j - 1)
                            while left:
                                next_max()
                            if j == TURN_OWN:
                                turn_maxima(job, i * (2 * A.jobs) + (job - 1), i * 4 + (2 * p + 2),
                                            slice(T // 2, T))
                                job += 1
                            if j == TURN_NEXT and not final:
                                turn_maxima(job, i * (2 * A.jobs) + (job - 1), i * 4 + (2 * p + 3),
                                            slice(0, T // 2))
                                job += 1
                        values(UNITS - 1)

                with pe.Fori(0, PAIRS - 1) as i:
                    heads(i, False)
                heads(PAIRS - 1, True)

            def output_projection(A, wo):
                pe.wait_ge(A.s.o_in, 16 * -(-(HEADS - 2) * A.dim // P))
                pe.wait_ge(A.s.exp, SCORE_SLOTS + HEADS * UNITS)
                for t in range(T):
                    if t % (T // 2) == 0:
                        pe.wait_ge(A.s.o_stored[t // (T // 2)], 32 * (HEADS + 1))
                    if t >= 4:
                        pe.wait_ge(A.s.proj_used, t - 3)
                    for c in range(A.chunks):
                        m = pe.matmul(ps[:, t % 4, 0:D], A.oT[c][:, t * P:(t + 1) * P], wo[:, c, :],
                                      start=c == 0, stop=c == A.chunks - 1)
                    m.then_inc(A.s.proj, 1)
                pe.wait_ge(A.s.proj_used, T)

            transpose_input(G, 0)
            pe.wait_ge(s_w, 16 * 7)
            pe.wait_ge(s_evA, XT)
            for t in range(T):
                for k in (2 * t, 2 * t + 1):
                    project(G, 0, k)
                pe.wait_ge(s_mask, t + 1)
                for half in range(2):
                    j = XT + 2 * t + half
                    pe.wait_ge(s_evA, j - 3)
                    for m8 in range(8):
                        m = pe.transpose(ps[:, j % 4, :].bitcast(BF16)[:, m8 * P:(m8 + 1) * P],
                                         mask_rows[:, t, (8 * half + m8) * P:(8 * half + m8 + 1) * P], identt[:, :])
                    m.then_inc(s_mmA, 1)
            pe.wait_ge(s_evA, A_GNN)
            pe.wait_ge(s_evD, D_GNN)
            attention(G)
            output_projection(G, gwo)
            transpose_input(F, A_GNN)
            pe.wait_ge(s_fw, 16 * 10)
            pe.wait_ge(s_evA, A_ALL)
            for k in range(FD_QK):
                project(F, D_GNN, k)
            pe.wait_ge(s_evD, D_GNN + FD_QK)
            attention(F)
            output_projection(F, fwo)
            pe.wait_ge(s_moe_w, 16 * 3)

            def logits(t):
                pe.wait_ge(s_tT, t + 1)
                for k in range(KC):
                    m = pe.matmul(ps[:, 5, t * EXPERTS:(t + 1) * EXPERTS], tT[:, t % 4, k, :], gate_w[:, k, :],
                                  start=k == 0, stop=k == KC - 1)
                m.then_inc(s_lg, 1)

            for t in range(T):
                pe.wait_ge(s_h, t + 1)
                if t >= 4:
                    pe.wait_ge(s_tT, t - 3)
                for k in range(KC):
                    m = pe.transpose(ps[:, t % 4, k * P:(k + 1) * P], ts[:, t, k * P:(k + 1) * P], ident[:, :])
                m.then_inc(s_hT, 1)
                if t >= 2:
                    logits(t - 2)
            logits(T - 2)
            logits(T - 1)
            pe.transpose(ps[:, 4, 0:EXPERTS * FC], b1_rows, ident[0:EXPERTS * FC, 0:EXPERTS * FC]).then_inc(s_b1, 1)
            pe.wait_ge(s_route, ROUTE_ONE_HOT)
            flat = one_hot.rearrange("p t e -> p (t e)")
            pe.matmul(ps[:, 5, 0:P], before[:, :], flat, start=True, stop=True).then_inc(s_prefix, 1)
            pe.matmul(ps[:, 6, 0:P], ones[:, :], flat, start=True, stop=True).then_inc(s_prefix, 1)

            def turn(p, j):
                pe.wait_ge(s_sorted_in[p], (j - p) * 8 + 16)
                pe.wait_ge(s_sT_out, j * 2 + 2)
                for k in range(KC):
                    m = pe.transpose(ps[:, 6 + p, k * P:(k + 1) * P], sorted_in[:, p, k * P:(k + 1) * P], ident[:, :])
                m.then_inc(s_sT, 1)

            registers = [pe.alloc_register(name=f"expert{n}") for n in range(4)]

            def experts_of(first, n):
                pe.load(registers[0:n], slot_expert[0:1, bass.ds(first, n)])
                return [pe.snap(r, min_val=0, max_val=EXPERTS - 1) for r in registers[0:n]]

            def hidden_and_out(p, up, down, up_expert=None, down_expert=None):
                if up is not None:
                    expert = up_expert
                    w1 = [w[:, bass.ds(expert * (KC * FF), KC * FF)] for w in (w1h, w1l)]
                    pe.wait_ge(s_sT_out, up * 2 + 6)
                    pe.wait_ge(s_gelu, up + 1)
                if down is not None:
                    expert = down_expert
                    w2 = [w[:, bass.ds(expert * (FC * D), FC * D)] for w in (w2h, w2l)]
                    pe.wait_ge(s_hid, down * 2 + 6)
                    pe.wait_ge(s_y, down + 1)
                for c in range(FC):
                    if up is not None:
                        bank = ps[:, 2 * p + c // 4, (c % 4) * P:(c % 4 + 1) * P]
                        for k in range(KC):
                            high, low = (w[:, k * FF + c * P:k * FF + (c + 1) * P] for w in w1)
                            pe.matmul(bank, high, sTh[:, p, k, :], start=k == 0, stop=False)
                            pe.matmul(bank, high, sTl[:, p, k, :], start=False, stop=False)
                            m = pe.matmul(bank, low, sTh[:, p, k, :], start=False, stop=k == KC - 1)
                        if c == FC - 1:
                            m.then_inc(s_up, 1)
                    if down is not None:
                        bank = ps[:, 4 + p, 0:D]
                        high, low = (w[:, c * D:(c + 1) * D] for w in w2)
                        pe.matmul(bank, hid_h[:, p, c, :], high, start=c == 0, stop=False)
                        pe.matmul(bank, hid_l[:, p, c, :], high, start=False, stop=False)
                        m = pe.matmul(bank, hid_h[:, p, c, :], low, start=False, stop=c == FC - 1)
                        if c == FC - 1:
                            m.then_inc(s_down, 1)

            pe.wait_ge(s_b1_out, 1)
            pe.wait_ge(s_route, ROUTE_DONE)
            pe.wait_ge(s_w_split, 2 * 4 * EXPERTS)
            turn(0, 0)
            turn(1, 1)
            e = experts_of(0, 2)
            hidden_and_out(0, 0, None, e[0])
            turn(0, 2)
            hidden_and_out(1, 1, None, e[1])
            with pe.Fori(0, TILE_PAIRS - 1) as i:
                e = experts_of(2 * i, 4)
                turn(1, 2 * i + 3)
                hidden_and_out(0, 2 * i + 2, 2 * i, e[2], e[0])
                turn(0, 2 * i + 4)
                hidden_and_out(1, 2 * i + 3, 2 * i + 1, e[3], e[1])
            e = experts_of(SLOTS - 3, 3)
            hidden_and_out(0, SLOTS - 1, SLOTS - 3, e[2], e[0])
            hidden_and_out(1, None, SLOTS - 2, None, e[1])
            hidden_and_out(0, None, SLOTS - 1, None, e[2])

        @block.vector
        def _(dve):
            dve.wait_ge(s_const, 3)
            nc.vector.tensor_scalar(identb[:, :], ident[:, :], MASKED, None, ALU.mult).then_inc(s_const2, 1)
            nc.vector.tensor_copy(identt[:, :], ident[:, :]).then_inc(s_const2, 1)
            nc.vector.memset(amax[:, :, :], 0.0).then_inc(s_const2, 1)

            def norm_factors(semaphore, root, tile_ready, out, half):
                h = slice(half * HALF, (half + 1) * HALF)

                def link(ins):
                    ins.then_inc(semaphore, 1)
                    count[0] += 1
                    dve.wait_ge(semaphore, count[0])

                count = [half * NORM_STEPS]
                for t in range(half * HALF, (half + 1) * HALF):
                    source = tile_ready(t)
                    nc.vector.bn_stats(stats[:, t, :], source).then_inc(semaphore, 1)
                count[0] += HALF
                dve.wait_ge(semaphore, count[0])
                for t in range(half * HALF, (half + 1) * HALF):
                    nc.vector.bn_aggr(out[:, t, :], stats[:, t, :]).then_inc(semaphore, 1)
                count[0] += HALF
                dve.wait_ge(semaphore, count[0])
                link(nc.vector.tensor_scalar(veps[:, h], out[:, h, 1], EPS, None, ALU.add))
                assert count[0] == half * NORM_STEPS + NORM_ROOT
                dve.wait_ge(root, half + 1)
                link(nc.vector.reciprocal(rstd[:, h], std[:, h]))
                link(nc.vector.tensor_tensor(tmp[:, h], rstd[:, h], rstd[:, h], ALU.mult))
                link(nc.vector.tensor_tensor(tmp[:, h], tmp[:, h], veps[:, h], ALU.mult))
                link(nc.vector.tensor_scalar(tmp[:, h], tmp[:, h], -0.5, 1.5, ALU.mult, ALU.add))
                link(nc.vector.tensor_tensor(rstd[:, h], rstd[:, h], tmp[:, h], ALU.mult))
                assert count[0] == (half + 1) * NORM_STEPS

            def layer_norm(A):
                def source(t):
                    if A is G and t % HALF == 0:
                        dve.wait_ge(s_x[t // HALF], 16)
                    if A is F:
                        dve.wait_ge(G.s.proj, t + 1)
                        nc.vector.tensor_tensor(xs[:, t, :], ps[:, t % 4, 0:D], xs[:, t, :], ALU.add)\
                            .then_inc(G.s.proj_used, 1)
                        dve.wait_ge(G.s.proj_used, t + 1)
                    return xs[:, t, :]

                base = 0 if A is G else A_GNN

                def normalised(t):
                    if t >= 4:
                        dve.wait_ge(s_mmA, base + (t - 4) // 2 + 1)
                    nc.vector.tensor_scalar(nx[:, t % 4, :], xs[:, t, :], mv[:, t, 0:1], rstd[:, t:t + 1],
                                            ALU.subtract, ALU.mult).then_inc(A.s.nx, 1)

                norm_factors(A.s.ln, A.s.sqrt, source, mv, 0)
                for t in range(4):
                    normalised(t)
                norm_factors(A.s.ln, A.s.sqrt, source, mv, 1)
                for t in range(4, T):
                    normalised(t)

            def low_half(A, d_base, k):
                n, b, j = k // NB, k % NB, d_base + k
                if n >= 2 and b == 0:
                    dve.wait_ge(A.s.qk_stored[n % 2], 32 * (n // 2))
                dve.wait_ge(s_mmD, j + 1)
                dve.wait_ge(A.s.hi, k + 1)
                cols = slice(b * BLOCK, (b + 1) * BLOCK)
                bank, hi, lo = ps[:, 4 + j % 4, :], hi_st[:, n % 2, cols], lo_st[:, n % 2, cols]
                if A is F:
                    col = (bq_cols, bk_cols)[n % 2][:, n // 2:n // 2 + 1]
                    nc.vector.scalar_tensor_tensor(out=lo, in0=bank, scalar=col, in1=hi, op0=ALU.add,
                                                   op1=ALU.subtract).then_inc(s_evD, 1)
                else:
                    nc.vector.tensor_tensor(lo, bank, hi, ALU.subtract).then_inc(s_evD, 1)

            def attention(A):
                def block_max(u, job, value):
                    qt, mb = u // NB, u % NB
                    dve.wait_ge(A.s.job, value)
                    bank = ps[:, 6 + job % 2, :]
                    if A.masked:
                        nc.vector.tensor_tensor_reduce(
                            out=A.junk[:, u % 2, :], in0=bank, in1=mask_rows[:, qt, mb * BLOCK:(mb + 1) * BLOCK],
                            scale=1.0, scalar=-3e38, op0=ALU.add, op1=ALU.max,
                            accum_out=amax[:, qt, mb:mb + 1]).wait_op(s_mask_scaled, T, "sem-ge")\
                            .then_inc(A.s.drained, 1)
                    else:
                        nc.vector.tensor_reduce(amax[:, qt, mb:mb + 1], bank, AX.X, ALU.max)\
                            .then_inc(A.s.drained, 1)

                def head_max(drained, tiles):
                    dve.wait_ge(A.s.drained, drained)
                    nc.vector.tensor_reduce(top[:, tiles], amax[:, tiles, :], AX.X, ALU.max).then_inc(A.s.top, 1)

                def negate(job, value, qp, row_in=None):
                    dve.wait_ge(A.s.job, value)
                    if row_in is not None:
                        dve.wait_ge(A.s.row_in[qp], row_in)
                    nc.vector.tensor_scalar(neg_top[qp][:, :], ps[0:T // QP, 6 + job % 2, 0:P], -1.0, None, ALU.mult)\
                        .then_inc(A.s.drained, 1)

                for i in range(2):
                    dve.wait_ge(A.s.qk_stored[i], 32 * A.chunks)
                for i in range(2):
                    nc.vector.memset(A.ones_row[i], 1.0).then_inc(A.s.ones_row, 1)
                for u in range(T * NB):
                    job = u + u // TURN_UNIT
                    block_max(u, job, job + 1)
                    if u == TURN_UNIT - 1:
                        head_max(TURN_UNIT, slice(0, T // 2))
                        negate(TURN_UNIT, TURN_UNIT + 1, 0)
                head_max(FIRST_JOBS, slice(T // 2, T))
                first = FIRST_JOBS

                def heads(i, last):
                    job = first
                    for p in range(2):
                        final = last and p == 1

                        def group_out(qp):
                            nonlocal job
                            g = 2 * p + qp
                            acc, o = ps[:, 4 + g % 2, :], A.o[:, qp, :]
                            if A.masked:
                                dve.wait_ge(A.s.job, i * (2 * A.jobs) + (job + 1))
                                dve.wait_ge(A.s.evac, i * 4 + (g + 2))
                                nc.vector.reciprocal(A.r, ps[:, 6 + job % 2, :]).then_inc(A.s.drained, 1)
                                job += 1
                                dve.wait_ge(A.s.drained, i * (2 * A.jobs) + job)
                                dve.wait_ge(A.s.pv, i * (2 * UNITS) + (RING + T * (g + 1)))
                                dve.wait_ge(A.s.o_stored[qp], i * 64 + 32 * (p + 1))
                                nc.vector.tensor_tensor(o, acc, A.r, ALU.mult).then_inc(A.s.evac, 1)
                            else:
                                dve.wait_ge(A.s.pv, i * (2 * UNITS) + (RING + T * (g + 1)))
                                dve.wait_ge(A.s.evac, i * 4 + (g + 2))
                                nc.vector.reciprocal(A.r[0:64, :], acc[64:128, :]).then_inc(A.s.evac_step, 1)
                                dve.wait_ge(A.s.evac_step, i * 4 + (g + 1))
                                dve.wait_ge(A.s.o_stored[qp], i * 64 + 32 * (p + 1))
                                nc.vector.tensor_tensor(o[0:64, :], acc[0:64, :], A.r[0:64, :], ALU.mult)\
                                    .then_inc(A.s.evac, 1)

                        for j in range(UNITS):
                            if not final:
                                for u in max_units(A, j):
                                    block_max(u, job, i * (2 * A.jobs) + (job + 1))
                                    job += 1
                                    if u % TURN_UNIT == TURN_UNIT - 1:
                                        half = u // TURN_UNIT
                                        head_max(i * (2 * A.jobs) + job, slice(half * T // 2, (half + 1) * T // 2))
                            if j == TURN_OWN:
                                negate(job, i * (2 * A.jobs) + (job + 1), 1, i * 32 + 16 * (p + 1))
                                job += 1
                            if j == TURN_NEXT and not final:
                                negate(job, i * (2 * A.jobs) + (job + 1), 0, i * 32 + 16 * (p + 1))
                                job += 1
                            if j == T:
                                group_out(0)
                        group_out(1)

                with dve.Fori(0, PAIRS - 1) as i:
                    heads(i, False)
                heads(PAIRS - 1, True)

            layer_norm(G)
            def scale_mask(t):
                dve.wait_ge(s_mmA, XT + 2 * t + 2)
                nc.vector.tensor_scalar(mask_rows[:, t, :], mask_rows[:, t, :], MASKED, None, ALU.mult)\
                    .then_inc(s_mask_scaled, 1)

            for t in range(T):
                dve.wait_ge(s_adj[t % 2], 16 * (t // 2 + 1))
                diag = adj_in[:, t % 2, t * P:(t + 1) * P]
                nc.vector.tensor_tensor(diag, diag, ident[:, :], ALU.max).then_inc(s_adj_diag, 1)
                dve.wait_ge(s_adj_diag, t + 1)
                nc.vector.tensor_scalar(mask_rows[:, t, :], adj_in[:, t % 2, :], -1.0, None, ALU.add)\
                    .then_inc(s_mask, 1)
                for k in (2 * t, 2 * t + 1):
                    low_half(G, 0, k)
                if t >= 1:
                    scale_mask(t - 1)
            scale_mask(T - 1)
            attention(G)
            layer_norm(F)
            dve.wait_ge(s_fw, 16 * 10)
            for k in range(FD_QK):
                low_half(F, D_GNN, k)
            attention(F)

            nc.vector.tensor_tensor(shift, mv[:, :, 0], rstd, ALU.mult).then_inc(s_shift, 1)
            dve.wait_ge(s_shift, 1)
            nc.vector.tensor_copy(rstd1, rstd).then_inc(s_shift, 1)
            dve.wait_ge(s_shift, 2)

            def residual(t):
                dve.wait_ge(F.s.proj, t + 1)
                nc.vector.scalar_tensor_tensor(out=ts[:, t, :], in0=xs[:, t, :], scalar=rstd1[:, t:t + 1],
                                               in1=ps[:, t % 4, 0:D], op0=ALU.mult, op1=ALU.add)\
                    .then_inc(F.s.proj_used, 1)
                dve.wait_ge(F.s.proj_used, t + 1)
                nc.vector.scalar_tensor_tensor(out=ts[:, t, :], in0=ts[:, t, :], scalar=shift[:, t:t + 1],
                                               in1=bias_o, op0=ALU.subtract, op1=ALU.add).then_inc(s_hsum, 1)
                dve.wait_ge(s_hsum, t + 1)
                return ts[:, t, :]

            for half in range(2):
                norm_factors(s_ln2, s_sqrt2, residual, mv2, half)
                tiles_of_half = range(half * HALF, (half + 1) * HALF)
                for t in tiles_of_half:
                    nc.vector.scalar_tensor_tensor(out=ts[:, t, :], in0=ts[:, t, :], scalar=mv2[:, t, 0:1],
                                                   in1=ln_g, op0=ALU.subtract, op1=ALU.mult).then_inc(s_centred, 1)
                for t in tiles_of_half:
                    dve.wait_ge(s_centred, t + 1)
                    nc.vector.scalar_tensor_tensor(out=ts[:, t, :], in0=ts[:, t, :], scalar=rstd[:, t:t + 1],
                                                   in1=ln_b, op0=ALU.mult, op1=ALU.add).then_inc(s_h, 1)
            dve.wait_ge(s_lg, T)
            nc.vector.tensor_tensor(logits, ps[:, 5, 0:T * EXPERTS].rearrange("p (t e) -> p t e", t=T),
                                    gate_b.unsqueeze(1).to_broadcast([P, T, EXPERTS]), ALU.add).then_inc(s_lg_out, 1)
            dve.wait_ge(s_lg_out, 1)

            r = [0]

            def link(ins):
                ins.then_inc(s_route, 1)
                r[0] += 1
                dve.wait_ge(s_route, r[0])

            def wide(a):
                return a.unsqueeze(2).to_broadcast([P, T, EXPERTS])

            def tiles(a, n):
                return a.unsqueeze(1).to_broadcast([P, n, EXPERTS])

            link(nc.vector.tensor_reduce(tmp, logits, AX.X, ALU.max))
            link(nc.vector.tensor_tensor(choice, logits, wide(tmp), ALU.subtract))
            assert r[0] == ROUTE_EXP
            link(nc.vector.tensor_tensor(one_hot, logits, wide(tmp), ALU.is_equal))
            link(nc.vector.tensor_tensor(one_hot, one_hot, tiles(e_iota[:, :], T), ALU.mult))
            link(nc.vector.tensor_reduce(tmp, one_hot, AX.X, ALU.max))
            link(nc.vector.tensor_tensor(one_hot, one_hot, wide(tmp), ALU.is_equal))
            assert r[0] == ROUTE_ONE_HOT
            dve.wait_ge(s_route_exp, 1)
            link(nc.vector.tensor_reduce(tmp, choice, AX.X, ALU.add))
            link(nc.vector.reciprocal(gate[:, :], tmp))
            link(nc.vector.tensor_copy(token_rows[:, :, D], gate[:, :]))
            dve.wait_ge(s_numbers, 1)
            link(nc.vector.tensor_copy(token_rows[:, :, D + 1].bitcast(I32), token_number[:, :]))
            dve.wait_ge(s_prefix, 2)
            link(nc.vector.tensor_copy(totals, ps[:, 6, 0:P].rearrange("p (t e) -> p t e", t=T)))
            src, dst = totals, run0
            for step in (1, 2, 4, 8):
                link(nc.vector.tensor_copy(dst[:, 0:step, :], src[:, 0:step, :]))
                link(nc.vector.tensor_tensor(dst[:, step:T, :], src[:, step:T, :], src[:, 0:T - step, :], ALU.add))
                src, dst = dst, (run1 if dst is run0 else run0)
            link(nc.vector.tensor_tensor(place, src, totals, ALU.subtract))
            link(nc.vector.tensor_tensor(rank, ps[:, 5, 0:P].rearrange("p (t e) -> p t e", t=T), place, ALU.add))
            link(nc.vector.tensor_scalar(counts[:, 0, :], src[:, T - 1, :], float(P - 1), None, ALU.add))
            link(nc.vector.tensor_copy(counts_i[:, :], counts[:, 0, :]))
            link(nc.vector.tensor_scalar(counts_i[:, :], counts_i[:, :], P.bit_length() - 1, None,
                                         ALU.logical_shift_right))
            link(nc.vector.tensor_copy(counts[:, 0, :], counts_i[:, :]))
            for step, a, b in ((1, 0, 1), (2, 1, 2), (4, 2, 1)):
                link(nc.vector.tensor_copy(counts[:, b, 0:step], counts[:, a, 0:step]))
                link(nc.vector.tensor_tensor(counts[:, b, step:EXPERTS], counts[:, a, step:EXPERTS],
                                             counts[:, a, 0:EXPERTS - step], ALU.add))
            link(nc.vector.tensor_tensor(counts[:, 2, :], counts[:, 1, :], counts[:, 0, :], ALU.subtract))
            link(nc.vector.tensor_scalar(counts[:, 2, :], counts[:, 2, :], float(P), None, ALU.mult))
            link(nc.vector.tensor_tensor(rank, rank, tiles(counts[:, 2, :], T), ALU.add))
            link(nc.vector.tensor_tensor(rank, rank, one_hot, ALU.mult))
            link(nc.vector.tensor_reduce(tmp, rank, AX.X, ALU.add))
            link(nc.vector.tensor_copy(slot_row[:, :], tmp))
            assert r[0] == ROUTE_ROWS, r[0]
            link(nc.vector.tensor_tensor(slot_of, tiles(counts[:, 1, :], SLOTS),
                                         slot_iota[:, :].unsqueeze(2).to_broadcast([P, SLOTS, EXPERTS]), ALU.is_le))
            link(nc.vector.tensor_reduce(slot_expert_f[:, :], slot_of, AX.X, ALU.add))
            link(nc.vector.tensor_scalar(slot_expert_f[:, :], slot_expert_f[:, :], float(EXPERTS - 1), None, ALU.min))
            link(nc.vector.tensor_copy(slot_expert[:, :], slot_expert_f[:, :]))
            assert r[0] == ROUTE_DONE, r[0]

            dve.wait_ge(s_b1_out, 1)
            dve.wait_ge(s_placed, 16 * T)

            def split_input(p, j):
                dve.wait_ge(s_sT, j + 1)
                dve.wait_ge(s_up, j + 1)
                bank = ps[:, 6 + p, 0:D].rearrange("p (k n) -> p k n", k=KC)
                nc.vector.tensor_copy(sTh[:, p, :, :], bank).then_inc(s_sT_out, 1)
                dve.wait_ge(s_sT_out, j * 2 + 5)
                nc.vector.tensor_tensor(sTl[:, p, :, :], bank, sTh[:, p, :, :], ALU.subtract).then_inc(s_sT_out, 1)

            registers = [dve.alloc_register(name=f"dve_expert{n}") for n in range(4)]

            def experts_of(first, n):
                dve.load(registers[0:n], slot_expert[0:1, bass.ds(first, n)])
                return [dve.snap(r, min_val=0, max_val=EXPERTS - 1) for r in registers[0:n]]

            def first_bias(p, j, expert):
                dve.wait_ge(s_gelu, j + 1)
                nc.vector.tensor_copy(b1_tile[:, p, :], b1_cols[:, bass.ds(expert * FC, FC)]).then_inc(s_b1_tile, 1)

            def split_hidden(p, j):
                dve.wait_ge(s_gelu, j + 3)
                dve.wait_ge(s_down, j + 1)
                nc.vector.tensor_copy(hid_h[:, p, :, :], hid[:, p, :, :]).then_inc(s_hid, 1)
                dve.wait_ge(s_hid, j * 2 + 5)
                nc.vector.tensor_tensor(hid_l[:, p, :, :], hid[:, p, :, :], hid_h[:, p, :, :], ALU.subtract)\
                    .then_inc(s_hid, 1)

            def expert_out(p, j, expert):
                nc.vector.tensor_copy(slot_gate[:, p:p + 1], slot_meta[:, bass.ds(2 * j, 1)]).then_inc(s_gate, 1)
                dve.wait_ge(s_down, j + 3)
                dve.wait_ge(s_res_free, j + 1)
                nc.vector.tensor_tensor(res[:, p, :], ps[:, 4 + p, 0:D], b2_all[:, bass.ds(expert * D, D)], ALU.add)\
                    .then_inc(s_sum, 1)
                dve.wait_ge(s_x_in[p], (j - p) * 8 + 16)
                dve.wait_ge(s_gate, j + 1)
                dve.wait_ge(s_sum, j + 1)
                nc.vector.scalar_tensor_tensor(out=res[:, p, :], in0=res[:, p, :], scalar=slot_gate[:, p:p + 1],
                                               in1=x_in[:, p, :], op0=ALU.mult, op1=ALU.add).then_inc(s_y, 1)

            e = experts_of(0, 2)
            first_bias(0, 0, e[0])
            split_input(0, 0)
            split_input(1, 1)
            split_input(0, 2)
            first_bias(1, 1, e[1])
            split_hidden(0, 0)
            dve.wait_ge(s_meta, 16)
            dve.wait_ge(s_b2_in, 16)
            with dve.Fori(0, TILE_PAIRS - 1) as i:
                e = experts_of(2 * i, 4)
                for n, p in ((1, 1), (2, 0)):
                    j = 2 * i + n
                    split_input(p, j + 2)
                    first_bias(1 - p, j + 1, e[n + 1])
                    split_hidden(p, j)
                    expert_out(1 - p, j - 1, e[n - 1])
            e = experts_of(SLOTS - 3, 3)
            first_bias(0, SLOTS - 1, e[2])
            split_hidden(1, SLOTS - 2)
            expert_out(0, SLOTS - 3, e[0])
            split_hidden(0, SLOTS - 1)
            expert_out(1, SLOTS - 2, e[1])
            expert_out(0, SLOTS - 1, e[2])


_INS = ['x', 'adj', 'L0_gnn_Wks', 'L0_gnn_Wqs', 'L0_gnn_Wvs', 'L0_gnn_Wo', 'L0_ffn_ln1_g', 'L0_ffn_ln1_b',
        'L0_ffn_Wq', 'L0_ffn_bq', 'L0_ffn_Wk', 'L0_ffn_bk', 'L0_ffn_Wv', 'L0_ffn_bv', 'L0_ffn_Wo', 'L0_ffn_bo',
        'L0_ffn_gate_W', 'L0_ffn_gate_b', 'L0_ffn_W1', 'L0_ffn_b1', 'L0_ffn_W2', 'L0_ffn_b2']


def kernel(**inputs):
    import numpy as np
    import concourse.bacc as bacc
    from concourse.bass_utils import run_bass_kernel_spmd

    nc = bacc.Bacc("TRN2", target_bir_lowering=False, num_devices=1)
    arrays, aps = {}, {}
    for name in _INS:
        a = np.ascontiguousarray(inputs[name])
        arrays["in_" + name] = a
        aps[name] = nc.dram_tensor("in_" + name, a.shape, mybir.dt.from_np(a.dtype), kind="ExternalInput").ap()
    out = nc.dram_tensor("out", (N, D), F32, kind="ExternalOutput").ap()
    gnn = {k[len("L0_gnn_"):]: v for k, v in aps.items() if k.startswith("L0_gnn_")}
    ffn = {k[len("L0_ffn_"):]: v for k, v in aps.items() if k.startswith("L0_ffn_")}
    fused_graph_ffn(nc, aps["x"], aps["adj"], gnn, ffn, out)
    r = run_bass_kernel_spmd(nc, [arrays], core_ids=[0])
    return r.results[0]["out"]
```
